# Optimizing a Trainium2 kernel written in Bass

```python
import numpy as np
import jax
import jax.numpy as jnp

def _softmax(x, axis=-1):
    return jax.nn.softmax(x, axis=axis)

def _gelu(x):
    return jax.nn.gelu(x, approximate=True)

def _silu(x):
    return jax.nn.silu(x)

def _sigmoid(x):
    return jax.nn.sigmoid(x)

def _layernorm(x, axis=-1, eps=1e-05):
    m = jnp.mean(x, axis=axis, keepdims=True)
    v = jnp.var(x, axis=axis, keepdims=True)
    return (x - m) / jnp.sqrt(v + eps)

def _scatter_add(tgt, idx, src, axis=0):
    return tgt.at[idx].add(src)

def _segment_sum(src, seg, n):
    return jax.ops.segment_sum(src, seg, n)
kernel_name = 'mk_hybrid_d1_jaxref_r8_9868c2'

def setup_inputs(seed: int=0):
    np.random.seed(seed)
    _w = jnp.asarray

    def _L0_attn_a_setup():
        import jax, jax.numpy as jnp
        import numpy as np
        B, T, D = (2, 256, 128)
        H = 16
        DH = D // H

        def alibi_bias(n_heads, token_cnt, dtype=jnp.float32):
            slopes = 2.0 ** (-8.0 * jnp.arange(1, n_heads + 1, dtype=dtype) / n_heads)
            pos = jnp.arange(token_cnt, dtype=dtype)
            rel = pos[None, :] - pos[:, None]
            return slopes[:, None, None] * rel[None, :, :]
        key = jax.random.key(seed)
        ks = jax.random.split(key, 5)
        s = 1.0 / np.sqrt(D)
        return {'x': jax.random.normal(ks[0], (B, T, D), dtype=jnp.float32), 'W_query': jax.random.normal(ks[1], (D, D), dtype=jnp.float32) * s, 'W_key': jax.random.normal(ks[2], (D, D), dtype=jnp.float32) * s, 'W_value': jax.random.normal(ks[3], (D, D), dtype=jnp.float32) * s, 'W_proj': jax.random.normal(ks[4], (D, D), dtype=jnp.float32) * s, 'b_proj': jnp.zeros((D,), dtype=jnp.float32)}
    _L0_attn_a_in = _L0_attn_a_setup()

    def _L0_attn_b_setup():
        import jax, jax.numpy as jnp
        import numpy as np
        WINDOW = 64
        SHIFT = 32
        HEADS = 8
        key = jax.random.key(seed)
        k1, k2, k3 = jax.random.split(key, 3)
        B, L, D = (8, 512, 128)
        scale = 0.02
        return {'x': jax.random.normal(k1, (B, L, D), dtype=jnp.float32), 'in_proj_w': jax.random.normal(k2, (3 * D, D), dtype=jnp.float32) * scale, 'in_proj_b': jnp.zeros((3 * D,), dtype=jnp.float32), 'out_w': jax.random.normal(k3, (D, D), dtype=jnp.float32) * scale, 'out_b': jnp.zeros((D,), dtype=jnp.float32)}
    _L0_attn_b_in = _L0_attn_b_setup()

    def _L0_ffn_setup():
        import jax, jax.numpy as jnp
        import numpy as np
        D, H, N, K = (128, 256, 8, 2)
        B, S = (4, 256)
        key = jax.random.key(seed)
        ks = jax.random.split(key, 4)
        x = jax.random.normal(ks[0], (B, S, D), dtype=jnp.float32)
        Wr = jax.random.normal(ks[1], (N, D), dtype=jnp.float32) / np.sqrt(D)
        br = jnp.zeros((N,), jnp.float32)
        Wl1 = jax.random.normal(ks[2], (N, D, 2 * H), dtype=jnp.float32) / np.sqrt(D)
        bl1 = jnp.zeros((N, 2 * H), jnp.float32)
        Wl2 = jax.random.normal(ks[3], (N, H, D), dtype=jnp.float32) / np.sqrt(H)
        bl2 = jnp.zeros((N, D), jnp.float32)
        biases_N = jnp.zeros((N,), jnp.float32)
        return {'x': x, 'Wr': Wr, 'br': br, 'Wl1': Wl1, 'bl1': bl1, 'Wl2': Wl2, 'bl2': bl2, 'biases_N': biases_N}
    _L0_ffn_in = _L0_ffn_setup()
    _d = {'L0_attn_a_x': _L0_attn_a_in['x'], 'L0_attn_a_W_query': _L0_attn_a_in['W_query'], 'L0_attn_a_W_key': _L0_attn_a_in['W_key'], 'L0_attn_a_W_value': _L0_attn_a_in['W_value'], 'L0_attn_a_W_proj': _L0_attn_a_in['W_proj'], 'L0_attn_a_b_proj': _L0_attn_a_in['b_proj'], 'L0_attn_b_in_proj_w': _L0_attn_b_in['in_proj_w'], 'L0_attn_b_in_proj_b': _L0_attn_b_in['in_proj_b'], 'L0_attn_b_out_w': _L0_attn_b_in['out_w'], 'L0_attn_b_out_b': _L0_attn_b_in['out_b'], 'L0_ffn_Wr': _L0_ffn_in['Wr'], 'L0_ffn_br': _L0_ffn_in['br'], 'L0_ffn_Wl1': _L0_ffn_in['Wl1'], 'L0_ffn_bl1': _L0_ffn_in['bl1'], 'L0_ffn_Wl2': _L0_ffn_in['Wl2'], 'L0_ffn_bl2': _L0_ffn_in['bl2'], 'L0_ffn_biases_N': _L0_ffn_in['biases_N']}
    _x0 = _d['L0_attn_a_x']
    _d['L0_attn_a_x'] = jax.random.normal(jax.random.fold_in(jax.random.key(seed), 1), (2, 1024, 128), dtype=_x0.dtype)
    del _x0
    return _d

def reference(L0_attn_a_x, L0_attn_a_W_query, L0_attn_a_W_key, L0_attn_a_W_value, L0_attn_a_W_proj, L0_attn_a_b_proj, L0_attn_b_in_proj_w, L0_attn_b_in_proj_b, L0_attn_b_out_w, L0_attn_b_out_b, L0_ffn_Wr, L0_ffn_br, L0_ffn_Wl1, L0_ffn_bl1, L0_ffn_Wl2, L0_ffn_bl2, L0_ffn_biases_N):

    def _L0_attn_a_ref(x, W_query, W_key, W_value, W_proj, b_proj):
        import jax, jax.numpy as jnp
        import numpy as np
        B, T, D = (2, 256, 128)
        H = 16
        DH = D // H

        def alibi_bias(n_heads, token_cnt, dtype=jnp.float32):
            slopes = 2.0 ** (-8.0 * jnp.arange(1, n_heads + 1, dtype=dtype) / n_heads)
            pos = jnp.arange(token_cnt, dtype=dtype)
            rel = pos[None, :] - pos[:, None]
            return slopes[:, None, None] * rel[None, :, :]
        b, t, _ = x.shape

        def heads(y):
            return y.reshape(b, t, H, DH).transpose(0, 2, 1, 3)
        q = heads(x @ W_query)
        k = heads(x @ W_key)
        v = heads(x @ W_value)
        scores = jnp.einsum('bhqd,bhkd->bhqk', q, k)
        causal = jnp.triu(jnp.ones((t, t), dtype=bool), k=1)
        scores = jnp.where(causal[None, None], -jnp.inf, scores)
        scores = scores + alibi_bias(H, t, scores.dtype)[None]
        scores = scores / jnp.sqrt(jnp.asarray(DH, scores.dtype))
        w = jax.nn.softmax(scores, axis=-1)
        ctx = jnp.einsum('bhqk,bhkd->bqhd', w, v).reshape(b, t, H * DH)
        return ctx @ W_proj + b_proj

    def _L0_attn_b_ref(x, in_proj_w, in_proj_b, out_w, out_b):
        import jax, jax.numpy as jnp
        import numpy as np
        WINDOW = 64
        SHIFT = 32
        HEADS = 8
        B, L, D = x.shape
        H, W, S = (HEADS, WINDOW, SHIFT)
        hd = D // H
        xs = jnp.roll(x, -S, axis=1)
        nw = L // W
        xw = xs.reshape(B * nw, W, D)
        qkv = xw @ in_proj_w.T + in_proj_b
        q, k, v = jnp.split(qkv, 3, axis=-1)

        def to_heads(t):
            return t.reshape(-1, W, H, hd).transpose(0, 2, 1, 3)
        q, k, v = (to_heads(q), to_heads(k), to_heads(v))
        scores = jnp.einsum('nhqd,nhkd->nhqk', q, k) * (1.0 / np.sqrt(hd))
        attn = jax.nn.softmax(scores, axis=-1)
        o = jnp.einsum('nhqk,nhkd->nhqd', attn, v)
        o = o.transpose(0, 2, 1, 3).reshape(-1, W, D)
        o = o @ out_w.T + out_b
        o = o.reshape(B, L, D)
        o = jnp.roll(o, S, axis=1)
        return o + o

    def _L0_ffn_ref(x, Wr, br, Wl1, bl1, Wl2, bl2, biases_N):
        import jax, jax.numpy as jnp
        import numpy as np
        D, H, N, K = (128, 256, 8, 2)
        B, S = (4, 256)
        Bb, Ss, Dd = x.shape
        scores_BSN = jnp.einsum('bsd,nd->bsn', x, Wr) + br
        w_BSN = jax.nn.softmax(scores_BSN, axis=-1)
        _, idx_BSK = jax.lax.top_k(scores_BSN + biases_N[None, None, :], K)
        val_BSK = jnp.take_along_axis(w_BSN, idx_BSK, axis=-1)
        val_BSK = val_BSK / jnp.sum(val_BSK, axis=-1, keepdims=True)
        M = Bb * Ss
        x_MD = x.reshape(M, Dd)
        idx_MK = idx_BSK.reshape(M, K)
        val_MK = val_BSK.reshape(M, K)
        h_NM2H = jnp.einsum('md,ndh->nmh', x_MD, Wl1) + bl1[:, None, :]
        a_NMH, b_NMH = (h_NM2H[..., :H], h_NM2H[..., H:])
        y_NMD = jnp.einsum('nmh,nhd->nmd', jax.nn.silu(a_NMH) * b_NMH, Wl2) + bl2[:, None, :]
        ew_MN = jnp.zeros((M, N), x.dtype)
        ew_MN = ew_MN.at[jnp.arange(M)[:, None], idx_MK].set(val_MK)
        y_MD = jnp.einsum('mn,nmd->md', ew_MN, y_NMD)
        return y_MD.reshape(Bb, Ss, Dd)
    x = L0_attn_a_x
    x = x + _L0_attn_a_ref(_layernorm(x, axis=-1), L0_attn_a_W_query, L0_attn_a_W_key, L0_attn_a_W_value, L0_attn_a_W_proj, L0_attn_a_b_proj)
    x = x + _L0_ffn_ref(_layernorm(x, axis=-1), L0_ffn_Wr, L0_ffn_br, L0_ffn_Wl1, L0_ffn_bl1, L0_ffn_Wl2, L0_ffn_bl2, L0_ffn_biases_N)
    x = x + _L0_attn_b_ref(_layernorm(x, axis=-1), L0_attn_b_in_proj_w, L0_attn_b_in_proj_b, L0_attn_b_out_w, L0_attn_b_out_b)
    x = x + _L0_ffn_ref(_layernorm(x, axis=-1), L0_ffn_Wr, L0_ffn_br, L0_ffn_Wl1, L0_ffn_bl1, L0_ffn_Wl2, L0_ffn_bl2, L0_ffn_biases_N)
    return x

_drawn_inputs = setup_inputs


def setup_inputs(seed=0):
    import zlib

    import numpy as np

    out = dict(_drawn_inputs(seed))
    spreads = {'L0_attn_a_b_proj': (0.0, 0.1),
     'L0_attn_b_in_proj_b': (0.0, 0.1),
     'L0_attn_b_out_b': (0.0, 0.1),
     'L0_ffn_br': (0.0, 0.1),
     'L0_ffn_bl1': (0.0, 0.1),
     'L0_ffn_bl2': (0.0, 0.1),
     'L0_ffn_biases_N': (0.0, 0.1)}
    factors = {}
    for name, (base, spread) in spreads.items():
        noise = np.random.default_rng([zlib.crc32(name.encode()), seed]).standard_normal(out[name].shape)
        drawn = base * np.exp(spread * noise) if base else spread * noise
        out[name] = jnp.asarray(drawn.astype(out[name].dtype))
    for name, factor in factors.items():
        out[name] = (out[name] * factor).astype(out[name].dtype)
    return out
```

```python
from contextlib import ExitStack

import concourse.bass as bass
from concourse import mybir

F32 = mybir.dt.float32
BF16 = mybir.dt.bfloat16
ALU = mybir.AluOpType
ACT = mybir.ActivationFunctionType
AX = mybir.AxisListType

P = 128
BATCH, TOKENS, DIM = 2, 1024, 128
ROLL = 32
TILES = TOKENS // P
QUADS = BATCH * 2
QT = 4
QCOLS = QT * P
EPS = 1e-5

A_HEADS, A_DIM = 16, 8
GROUP = 4
GROUPS = A_HEADS // GROUP
UNITS = BATCH * GROUPS
PARTS = 3
PAIR_ROWS = PARTS * PARTS * A_DIM
MAX_ROWS_FROM = PAIR_ROWS + PARTS
SCORE_ROWS = MAX_ROWS_FROM + PARTS
VCOLS = A_DIM + 1
A_SCALE = float(A_DIM) ** -0.5

EXPERTS, HID = 8, 256

B_HEADS, B_DIM, WIN = 8, 16, 64
B_PAIRS = B_HEADS // 2
WINS_PER_QUAD = QCOLS // WIN
B_SCALE = float(B_DIM) ** -0.5
NEG_BIG = -1e30
NEG_HUGE = -3e38

STEPS = []
for _c in range(2):
    for _j in range(4 * _c + 4):
        _q = max(P * _j, QCOLS * _c)
        STEPS.append((_c, _j, _q, QCOLS * (_c + 1) - _q))
N_STEPS = len(STEPS)
DIAG = [s for s, (c, j, q, w) in enumerate(STEPS) if q == P * j]
LAST_STEP = [3, N_STEPS - 1]
ROUNDS = []
for _i in range(TILES):
    for _hp in range(2):
        for _kc in range(1 + (_i >= 4)):
            ROUNDS.append((_i, _hp, _kc, min(QCOLS, P * (_i + 1) - QCOLS * _kc)))
N_ROUNDS = len(ROUNDS)
HALF_ROUNDS = 8


def stage_plan():
    plan = [("S1", 0), ("S1", 1), ("CTX_PREV", 1), ("MAX", 1)]
    done1 = sum(2 * ROUNDS[r][3] for r in range(2))
    done2, r = 0, 2
    maxed = False
    for s in range(N_STEPS):
        plan.append(("S2", s))
        if s >= 1:
            plan.append(("PV", s - 1))
            if s - 1 == LAST_STEP[0]:
                plan.append(("CTX_COPY", 0))
        if s - 1 == LAST_STEP[0] + 1:
            plan.append(("CTX", 0))
        done2 += 4 * STEPS[s][3]
        while r < N_ROUNDS and done1 < done2:
            plan.append(("S1", r))
            done1 += 2 * ROUNDS[r][3]
            r += 1
        if not maxed and r >= HALF_ROUNDS + 2 and s >= 7:
            plan.append(("MAX_NEXT", 0))
            maxed = True
    while r < N_ROUNDS:
        plan.append(("S1", r))
        r += 1
    plan += [("PV", N_STEPS - 1), ("CTX_COPY", 1)]
    return plan


PLAN = stage_plan()

ITEMS = [(n, f) for n in range(EXPERTS) for f in range(2)]


class Chain:

    def __init__(self, eng, sem):
        self.eng, self.sem, self.n = eng, sem, 0

    def add(self, ins):
        self.n += 1
        return ins.then_inc(self.sem, 1)

    def settle(self):
        if self.n:
            self.eng.wait_ge(self.sem, self.n)


def build(nc, x, w_q, w_k, w_v, w_proj, b_proj, b_in_wt, b_in_b, b_in_b_t, b_out_wt, b_out_b,
          wr_t, br, wl1, bl1_t, wl2, bl2, biases, ident, ident_bf, causal, key_rows,
          expert_rows, head_mask, order, out):
    with ExitStack() as ctx:
        def sb(name, shape, dt=F32):
            return ctx.enter_context(nc.sbuf_tensor(name, shape, dt))

        def sem(name):
            return ctx.enter_context(nc.semaphore(name))

        parts_dram = nc.dram_tensor("qk_parts", [2, BATCH, PARTS, P, TOKENS], BF16).ap()

        xs = sb("x_rolled", [P, BATCH * TILES, DIM])
        xn = sb("x_normed", [P, QT, DIM])
        xn_t = sb("x_normed_t", [P, BATCH, TOKENS + ROLL])
        ident_s = sb("ident_s", [P, P])
        ident_b = sb("ident_b", [P, P], BF16)
        causal_s = sb("causal_s", [P, P], BF16)
        wa = sb("attn_a_weights", [P, 4, DIM])
        bproj_s = sb("bproj_s", [P, DIM])
        stats = sb("stats", [P, QT, 6])
        mv = sb("mean_var", [P, QT, 2])
        var_eps = sb("var_eps", [P, QT])
        std = sb("std", [P, QT])
        rstd = sb("rstd", [P, QT])

        region = sb("region", [P, 2 * BATCH * A_HEADS * TOKENS // 2])
        region_b = region[:].bitcast(BF16)
        side = A_HEADS * TOKENS
        q_rows = [region_b[0:SCORE_ROWS, (2 * b) * side:(2 * b + 1) * side].rearrange("r (h t) -> r h t", h=A_HEADS)
                  for b in range(BATCH)]
        k_rows = [region_b[0:SCORE_ROWS, (2 * b + 1) * side:(2 * b + 2) * side].rearrange("r (h t) -> r h t", h=A_HEADS)
                  for b in range(BATCH)]
        part_s = sb("parts", [P, PARTS, QCOLS], BF16)
        rest_s = sb("rest", [P, QCOLS])
        v_s = sb("v_ones", [P, BATCH * TILES, A_HEADS, VCOLS])
        probs = sb("probs", [P, 2, GROUP, QCOLS])
        neg_max = sb("neg_max", [P, 2, GROUP, TILES])
        max_joined = sb("max_joined", [P, GROUP, QT])
        max_rest = sb("max_rest", [P, GROUP, QT])
        max_parts = sb("max_parts", [P, PARTS, GROUP, QT], BF16)
        max_t = sb("max_t", [PARTS * GROUP * QT, P], BF16)
        ctx_s = sb("ctx_s", [P, QCOLS])
        ctx_rec = sb("ctx_rec", [P, QT, GROUP])

        at = [0]

        def carve(shape):
            n = 1
            for d in shape:
                n *= d
            v = region[:, at[0]:at[0] + n]
            at[0] += n
            names = "abcd"[:len(shape)]
            if len(shape) == 1:
                return v
            return v.rearrange(f"p ({' '.join(names)}) -> p {' '.join(names)}", **dict(zip(names, shape)))

        w1_s = carve([EXPERTS, 2 * HID])
        w2_s = carve([EXPERTS, 2, DIM])
        bl1_s = carve([EXPERTS, 4])
        bl2_s = carve([DIM])
        wr_s = carve([EXPERTS])
        br_s = carve([EXPERTS])
        bias_s = carve([EXPERTS])
        order_s = carve([EXPERTS])
        b_win = carve([3 * DIM])
        b_wout = carve([DIM])
        b_bin = carve([3])
        b_bv = carve([DIM])
        b_bout = carve([DIM])
        b_bout2 = carve([DIM])
        mask_s = carve([B_HEADS])
        mask_bias = carve([B_HEADS])
        exp_rows = carve([EXPERTS * P // 2]).bitcast(BF16).rearrange("p (n q) -> p n q", n=EXPERTS)
        assert at[0] <= A_HEADS * TOKENS
        at[0] = A_HEADS * TOKENS
        silu_s = carve([2, QCOLS])
        gated = carve([2, QCOLS])
        ew_wide = carve([2, QCOLS])
        hidden = carve([3, QCOLS])
        y_s = carve([QCOLS])
        r_s = [carve([QT, EXPERTS]) for _ in range(14)]
        r_m = [carve([QT]) for _ in range(10)]
        ew_parts = carve([QT * PARTS * EXPERTS // 2]).bitcast(BF16).rearrange("p (t q n) -> p t q n", t=QT, q=PARTS)
        ew_rows = carve([2, QCOLS // 2]).bitcast(BF16).rearrange("p a (q) -> p a q")
        ew_t = carve([2, QCOLS])
        bq_s = carve([QCOLS])
        bk_s = carve([B_HEADS, QCOLS])
        b_vbd = carve([WINS_PER_QUAD, B_PAIRS, 2 * B_DIM])
        b_p = carve([2, B_HEADS, WIN])
        b_mx = carve([2, B_HEADS])
        b_sum = carve([2, B_HEADS])
        b_rec = carve([2, B_HEADS])
        b_pt = carve([2, B_PAIRS, P])
        b_o = carve([2, DIM])
        b_ot = carve([2, P])
        ctx_tok = carve([0 + 1]) if False else sb("ctx_tok", [P, TILES, DIM])
        ctx_t = sb("ctx_t", [P, TOKENS + ROLL])
        assert at[0] <= 2 * A_HEADS * TOKENS

        ps = ctx.enter_context(nc.psum_tensor("ps", [P, 8, QCOLS], F32))
        MISC = 7

        s_x = sem("x_loaded")
        s_const = sem("constants_loaded")
        s_wa = sem("attn_a_weights_loaded")
        s_dve = sem("dve_own")
        s_act = sem("act_own")
        s_pool = sem("pool_own")
        s_var = sem("variance_ready")
        s_std = sem("std_ready")
        s_normed = sem("quad_normed")
        s_norm_t = sem("quad_transposed")
        s_xt = sem("xn_t_written")
        s_xt_used = sem("xn_t_used")
        s_qk_psum = sem("qk_in_psum")
        s_part1 = sem("part1_ready")
        s_rest = sem("rest_ready")
        s_part2 = sem("part2_ready")
        s_part3 = sem("part3_ready")
        s_parts_out = sem("parts_stored")
        s_v_psum = sem("v_in_psum")
        s_v = sem("v_ready")
        s_ones = sem("v_ones_set")
        s_rows = [sem(f"score_rows_loaded_{u}") for u in range(UNITS)]
        s_s1 = sem("round_scored")
        s_s1_read = sem("round_maxed")
        s_joined = sem("chunk_maxima_joined")
        s_maxp = sem("max_parts_ready")
        s_maxt = sem("max_transposed")
        s_maxc = sem("max_rows_copied")
        s_maxd = sem("max_rows_placed")
        s_s2 = sem("step_scored")
        s_probs = sem("exp_done")
        s_masked = sem("diagonal_masked")
        s_pv = sem("pv_done")
        s_ctx_clear = sem("ctx_bank_cleared")
        s_ctx_copied = sem("ctx_copied")
        s_ctx_t = sem("ctx_transposed")
        s_ctx_n = sem("ctx_normalised")
        s_ctxf_t = sem("ctx_tiles_transposed")
        s_ctxf = sem("ctx_t_written")
        s_proj = sem("projection_done")
        s_proj_read = sem("projection_added")
        s_w = sem("late_weights_loaded")
        s_late = sem("late_constants_ready")
        s_router = sem("router_scores_done")
        s_rshift = sem("router_shifted")
        s_rexp = sem("router_exp_done")
        s_ew = sem("expert_weights_ready")
        s_ew_t = sem("expert_weights_transposed")
        s_ew_c = sem("expert_weights_copied")
        s_up = sem("item_up_done")
        s_silu = sem("item_silu_done")
        s_gate = sem("item_gated")
        s_wide = sem("expert_weight_spread")
        s_wide_c = sem("expert_weight_copied")
        s_hid = sem("item_hidden_ready")
        s_down = sem("item_down_done")
        s_y_c = sem("y_copied")
        s_y_t = sem("y_transposed")
        s_added = sem("y_added")
        s_bqk = sem("b_qk_done")
        s_bq_c = sem("b_q_copied")
        s_bk_c = sem("b_k_copied")
        s_bv = sem("b_v_done")
        s_bv_c = sem("b_v_copied")
        s_bs = sem("b_scores_done")
        s_bshift = sem("b_scores_shifted")
        s_bexp = sem("b_exp_done")
        s_bpt = sem("b_probs_transposed")
        s_bpt_c = sem("b_probs_t_copied")
        s_bo = sem("b_pv_done")
        s_bo_n = sem("b_o_normalised")
        s_bot = sem("b_o_transposed")
        s_bot_c = sem("b_o_t_copied")
        s_by = sem("b_y_done")
        s_out = sem("out_stored")

        def rolled(dram, b):
            full = TILES - 1
            yield (xs[:, b * TILES:b * TILES + full, :],
                   dram[b, ROLL:ROLL + full * P, :].rearrange("(t p) d -> p t d", p=P))
            yield xs[0:P - ROLL, b * TILES + full, :], dram[b, ROLL + full * P:TOKENS, :]
            yield xs[P - ROLL:P, b * TILES + full, :], dram[b, 0:ROLL, :]

        def quad_cols(c):
            return c // 2, ROLL + (c % 2) * QCOLS

        def norm_dve(dve, chain, g):
            c = g % QUADS
            if g < QUADS:
                dve.wait_ge(s_x, 96)
            for t in range(QT):
                chain.settle()
                chain.add(nc.vector.bn_stats(stats[:, t, :], xs[:, c * QT + t, :]))
            for t in range(QT):
                chain.settle()
                chain.add(nc.vector.bn_aggr(mv[:, t, :], stats[:, t, :]))
            chain.settle()
            if g:
                dve.wait_ge(s_std, g)
            nc.vector.tensor_scalar_add(var_eps[:], mv[:, :, 1], EPS).then_inc(s_var, 1)
            dve.wait_ge(s_std, g + 1)
            chain.add(nc.vector.reciprocal(rstd[:], std[:]))
            chain.settle()
            if g:
                dve.wait_ge(s_norm_t, g)
            for t in range(QT):
                nc.vector.tensor_scalar(xn[:, t, :], xs[:, c * QT + t, :], mv[:, t, 0:1], rstd[:, t:t + 1],
                                        ALU.subtract, ALU.mult).then_inc(s_normed, 1)
            dve.wait_ge(s_normed, QT * (g + 1))

        def norm_act(act, g):
            act.wait_ge(s_var, g + 1)
            if g:
                act.wait_ge(s_normed, QT * g)
            nc.scalar.activation(std[:], var_eps[:], ACT.Sqrt).then_inc(s_std, 1)

        def norm_pe(pe, g):
            pe.wait_ge(s_normed, QT * (g + 1))
            for t in range(QT):
                ins = nc.tensor.transpose(ps[:, MISC, t * P:(t + 1) * P], xn[:, t, :], ident_s[:])
            ins.then_inc(s_norm_t, 1)

        def norm_copy(act, g):
            b, col = quad_cols(g % QUADS)
            act.wait_ge(s_norm_t, g + 1)
            nc.scalar.copy(xn_t[:, b, col:col + QCOLS], ps[:, MISC, :]).then_inc(s_xt, 1)
            if g < QUADS and g % 2:
                nc.scalar.copy(xn_t[:, b, 0:ROLL], ps[:, MISC, QCOLS - ROLL:QCOLS]).then_inc(s_xt, 1)

        XT_HEAD = {1: 2 + 1, 3: 4 + 2}

        def xt_count(g):
            return g + 1 + (2 if g >= 3 else 1 if g >= 1 else 0)

        block = ctx.enter_context(nc.Block())

        def load_late(sp):
            sp.wait_ge(s_pv, N_STEPS * GROUPS)
            sp.dma_start(w1_s, wl1.rearrange("n d h -> d n h")).then_inc(s_w, 16)
            for f in range(2):
                sp.dma_start(w2_s[:, :, f, :], wl2[:, f * P:(f + 1) * P, :].rearrange("n h d -> h n d")).then_inc(s_w, 16)
            sp.dma_start(bl1_s, bl1_t).then_inc(s_w, 16)
            sp.dma_start(bl2_s[0:EXPERTS, :], bl2).then_inc(s_w, 16)
            sp.dma_start(wr_s, wr_t).then_inc(s_w, 16)
            sp.dma_start(br_s, br.partition_broadcast(P)).then_inc(s_w, 16)
            sp.dma_start(bias_s, biases.partition_broadcast(P)).then_inc(s_w, 16)
            sp.dma_start(order_s, order).then_inc(s_w, 16)
            sp.dma_start(b_win, b_in_wt).then_inc(s_w, 16)
            sp.dma_start(b_wout, b_out_wt).then_inc(s_w, 16)
            sp.dma_start(b_bin, b_in_b_t).then_inc(s_w, 16)
            sp.dma_start(b_bv, b_in_b[2 * DIM:3 * DIM].partition_broadcast(P)).then_inc(s_w, 16)
            sp.dma_start(b_bout, b_out_b.partition_broadcast(P)).then_inc(s_w, 16)
            sp.dma_start(mask_s, head_mask).then_inc(s_w, 16)
            sp.dma_start(exp_rows[0:PARTS * EXPERTS, :, :], expert_rows).then_inc(s_w, 16)
        @block.sync
        def _(sp):
            for b in range(BATCH):
                for dst, src in rolled(x, b):
                    sp.dma_start(dst, src).then_inc(s_x, 16)
            sp.dma_start(ident_s[:], ident).then_inc(s_const, 16)
            sp.dma_start(ident_b[:], ident_bf).then_inc(s_const, 16)
            sp.dma_start(causal_s[:], causal).then_inc(s_const, 16)
            for n, w in enumerate((w_q, w_k, w_v, w_proj)):
                sp.dma_start(wa[:, n, :], w).then_inc(s_wa, 16)
            sp.dma_start(bproj_s[:], b_proj.partition_broadcast(P)).then_inc(s_wa, 16)
            for b in range(BATCH):
                for half in range(2):
                    for s in range(2):
                        n = (b * 2 + half) * 2 + s
                        sp.wait_ge(s_part3, n + 1)
                        sp.dma_start(parts_dram[s, b, :, :, half * QCOLS:(half + 1) * QCOLS]
                                     .rearrange("a p t -> p a t"), part_s[:]).then_inc(s_parts_out, 16)
                sp.wait_ge(s_parts_out, 64 * (b + 1))
                for hg in range(GROUPS):
                    u = b * GROUPS + hg
                    hs = slice(hg * GROUP, (hg + 1) * GROUP)
                    for i in range(PARTS):
                        for j in range(PARTS):
                            r = (i * PARTS + j) * A_DIM
                            for s, rows, part in ((0, q_rows, i), (1, k_rows, j)):
                                sp.dma_start(rows[b][r:r + A_DIM, hs, :],
                                             parts_dram[s, b, part].rearrange("(h d) t -> d h t", d=A_DIM)[:, hs, :])\
                                    .then_inc(s_rows[u], 16)
                    sp.dma_start(k_rows[b][PAIR_ROWS:SCORE_ROWS, hs, :], key_rows[:, hs, :]).then_inc(s_rows[u], 16)
                    sp.dma_start(q_rows[b][PAIR_ROWS:MAX_ROWS_FROM, hs, :], key_rows[PARTS:2 * PARTS, hs, :])\
                        .then_inc(s_rows[u], 16)
            for n in range(2 * UNITS):
                u, half = divmod(n, 2)
                b, hg = divmod(u, GROUPS)
                if u > GROUPS and half == 0 and u == GROUPS + 1:
                    load_late(sp)
                sp.wait_ge(s_maxc, n + 1)
                for p in range(PARTS):
                    dst = q_rows[b][MAX_ROWS_FROM + p:MAX_ROWS_FROM + p + 1, hg * GROUP:(hg + 1) * GROUP,
                                    half * QCOLS:(half + 1) * QCOLS]
                    for h in range(GROUP):
                        sp.dma_start(dst[:, h, :].rearrange("o (t q) -> o t q", q=P),
                                     max_t[(p * GROUP + h) * QT:(p * GROUP + h + 1) * QT, :]).then_inc(s_maxd, 16)
            sp.wait_ge(s_added, 3 * QUADS)
            for b in range(BATCH):
                for src, dst in rolled(out, b):
                    sp.dma_start(dst, src).then_inc(s_out, 16)
            sp.wait_ge(s_out, 96)

        W_ALL = 16 * 16

        @block.gpsimd
        def _(pool):
            chain = Chain(pool, s_pool)
            nc.gpsimd.memset(v_s[:, :, :, A_DIM:VCOLS], 1.0).then_inc(s_ones, 1)
            for n in range(2 * QUADS):
                pool.wait_ge(s_part2, n + 1)
                nc.gpsimd.tensor_tensor(part_s[:, 2, :], rest_s[:], part_s[:, 1, :], ALU.subtract).then_inc(s_part3, 1)

            def max_parts_of(u, half):
                n = 2 * u + half
                if half:
                    pool.wait_ge(s_joined, u + 1)
                else:
                    pool.wait_ge(s_s1_read, N_ROUNDS * u + HALF_ROUNDS)
                if n:
                    pool.wait_ge(s_maxt, n)
                m = neg_max[:, 0, :, QT * half:QT * half + QT]
                if half:
                    m = max_joined[:]
                chain.add(nc.gpsimd.tensor_copy(max_parts[:, 0], m))
                chain.settle()
                chain.add(nc.gpsimd.tensor_tensor(max_rest[:], m, max_parts[:, 0], ALU.subtract))
                chain.settle()
                chain.add(nc.gpsimd.tensor_copy(max_parts[:, 1], max_rest[:]))
                chain.settle()
                nc.gpsimd.tensor_tensor(max_parts[:, 2], max_rest[:], max_parts[:, 1], ALU.subtract).then_inc(s_maxp, 1)
                pool.wait_ge(s_maxp, n + 1)

            def mask_of(u, s):
                d = len(DIAG) * u + DIAG.index(s)
                pool.wait_ge(s_probs, GROUP * (N_STEPS * u + s + 1))
                tile = probs[:, s % 2, :, 0:P]
                nc.gpsimd.affine_select(out=tile, in_=tile, compare_op=ALU.is_ge, fill=0.0, base=0,
                                        pattern=[[0, GROUP], [1, P]], channel_multiplier=-1).then_inc(s_masked, 1)

            max_parts_of(0, 0)
            for u in range(UNITS):
                for kind, n in PLAN:
                    if kind == "S2" and n in DIAG:
                        mask_of(u, n)
                    if kind == "MAX":
                        max_parts_of(u, 1)
                    if kind == "MAX_NEXT" and u + 1 < UNITS:
                        max_parts_of(u + 1, 0)

            def expert_items(f_index, items):
                for i in items:
                    k = len(ITEMS) * f_index + i
                    pool.wait_ge(s_gate, k + 1)
                    pool.wait_ge(s_wide_c, k // 2 + 1)
                    if k >= 3:
                        pool.wait_ge(s_down, k - 2)
                    nc.gpsimd.tensor_tensor(hidden[:, k % 3, :], gated[:, k % 2, :], ew_wide[:, (k // 2) % 2, :],
                                            ALU.mult).then_inc(s_hid, 1)

            pool.wait_ge(s_w, W_ALL)
            pool.wait_ge(s_pv, N_STEPS * UNITS)
            chain.add(nc.gpsimd.memset(b_vbd, 0.0))
            chain.add(nc.gpsimd.tensor_scalar(mask_bias, mask_s, b_bin[:, 1:2], None, ALU.mult))
            chain.add(nc.gpsimd.tensor_scalar(b_bout2, b_bout, 2.0, None, ALU.mult))
            chain.settle()
            nc.gpsimd.memset(b_mx, 0.0).then_inc(s_late, 1)
            for f_index in range(2 * QUADS):
                expert_items(f_index, range(len(ITEMS)))

        @block.scalar
        def _(act):
            def parts_act(n):
                act.wait_ge(s_qk_psum, n + 1)
                if n:
                    act.wait_ge(s_parts_out, 16 * n)
                nc.scalar.copy(part_s[:, 0, :], ps[:, n % 2, :]).then_inc(s_part1, 1)
                act.wait_ge(s_rest, n + 1)
                nc.scalar.copy(part_s[:, 1, :], rest_s[:]).then_inc(s_part2, 1)

            def v_act(c):
                act.wait_ge(s_v_psum, c + 1)
                nc.scalar.copy(v_s[:, c * QT:(c + 1) * QT, :, 0:A_DIM],
                               ps[:, 2 + c % 2, :].rearrange("p (t h d) -> p t h d", t=QT, h=A_HEADS)).then_inc(s_v, 1)

            for b in range(BATCH):
                for g in (2 * b, 2 * b + 1):
                    norm_act(act, g)
                    norm_copy(act, g)
                for k in range(2):
                    parts_act(4 * b + 2 * k)
                    parts_act(4 * b + 2 * k + 1)
                    v_act(2 * b + k)

            def max_copy(u, half):
                n = 2 * u + half
                act.wait_ge(s_maxt, n + 1)
                if n:
                    act.wait_ge(s_maxd, 16 * PARTS * GROUP * n)
                nc.scalar.copy(max_t[:], max_bank(ps)).then_inc(s_maxc, 1)

            def exps(u, s):
                c, j, q, w = STEPS[s]
                k = N_STEPS * u + s
                if k >= 2:
                    act.wait_ge(s_pv, k - 1)
                for h in range(GROUP):
                    n = GROUP * k + h
                    act.wait_ge(s_s2, n + 1)
                    nc.scalar.activation(probs[:, s % 2, h, 0:w], ps[:, 4 + n % 2, 0:w], ACT.Exp,
                                         scale=A_SCALE).then_inc(s_probs, 1)

            def ctx_copy(u, half):
                n = 2 * u + half
                act.wait_ge(s_pv, N_STEPS * u + LAST_STEP[half] + 1)
                if n:
                    act.wait_ge(s_ctx_t, n)
                nc.scalar.copy(ctx_s[:], ps[:, 6, :]).then_inc(s_ctx_copied, 1)

            def ctx_finish(b):
                for k in range(2):
                    act.wait_ge(s_ctxf_t, 2 * b + k + 1)
                    if b and k == 0:
                        act.wait_ge(s_proj, 2)
                    nc.scalar.copy(ctx_t[:, k * QCOLS:(k + 1) * QCOLS], ps[:, 2 + k, :]).then_inc(s_ctxf, 1)
                    if k == 0:
                        nc.scalar.copy(ctx_t[:, TOKENS:TOKENS + ROLL], ps[:, 2, 0:ROLL]).then_inc(s_ctxf, 1)

            max_copy(0, 0)
            for u in range(UNITS):
                for kind, n in PLAN:
                    if kind == "S2":
                        exps(u, n)
                    if kind == "MAX":
                        max_copy(u, 1)
                    if kind == "MAX_NEXT" and u + 1 < UNITS:
                        max_copy(u + 1, 0)
                    if kind == "CTX_COPY":
                        ctx_copy(u, n)
                if u % GROUPS == GROUPS - 1:
                    ctx_finish(u // GROUPS)

            def router_exp(g, r):
                act.wait_ge(s_rshift, r + 1)
                nc.scalar.activation(r_s[5], r_s[4], ACT.Exp).then_inc(s_rexp, 1)

            def ew_copy(r):
                act.wait_ge(s_ew_t, r + 1)
                nc.scalar.copy(ew_rows[0:PARTS * EXPERTS, r % 2, :], ew_bank(ps)[0]).then_inc(s_ew_c, 1)
                nc.scalar.copy(ew_t[0:EXPERTS, r % 2, :], ps[0:EXPERTS, MISC - 1, :]).then_inc(s_ew_c, 1)

            def expert_items(f, pieces):
                for i, (n, half) in enumerate(ITEMS):
                    k = len(ITEMS) * f + i
                    if half == 0:
                        e = k // 2
                        act.wait_ge(s_wide, e + 1)
                        if e >= 2:
                            act.wait_ge(s_hid, 2 * (e - 1))
                        nc.scalar.copy(ew_wide[:, e % 2, :], ps[:, 4, :]).then_inc(s_wide_c, 1)
                    act.wait_ge(s_up, 2 * k + 1)
                    if k >= 2:
                        act.wait_ge(s_gate, k - 1)
                    nc.scalar.activation(silu_s[:, k % 2, :], ps[:, 2 * (k % 2), :], ACT.Silu,
                                         bias=bl1_s[:, n, half:half + 1]).then_inc(s_silu, 1)
                    if i in pieces:
                        pieces[i]()
                act.wait_ge(s_down, len(ITEMS) * (f + 1))
                if f:
                    act.wait_ge(s_y_t, f)
                nc.scalar.copy(y_s, ps[:, 5, :]).then_inc(s_y_c, 1)

            def prep(g, r):
                norm_act(act, g)
                norm_copy(act, g)
                router_exp(g, r)
                ew_copy(r)

            def moe(g0, r0):
                prep(g0, r0)
                for c in range(QUADS):
                    pieces = {}
                    if c + 1 < QUADS:
                        pieces = {1: lambda c=c: (norm_act(act, g0 + c + 1)), 3: lambda c=c: norm_copy(act, g0 + c + 1),
                                  6: lambda c=c: router_exp(g0 + c + 1, r0 + c + 1), 10: lambda c=c: ew_copy(r0 + c + 1)}
                    expert_items(r0 + c, pieces)

            act.wait_ge(s_late, 1)
            moe(QUADS, 0)

            def b_qk(c):
                act.wait_ge(s_bqk, 2 * c + 1)
                if c:
                    act.wait_ge(s_bs, QT * c)
                nc.scalar.activation(bq_s, ps[:, 0, :], ACT.Identity, bias=b_bin[:, 0:1]).then_inc(s_bq_c, 1)
                act.wait_ge(s_bqk, 2 * c + 2)
                for h in range(B_HEADS):
                    nc.scalar.activation(bk_s[:, h, :], ps[:, 1, :], ACT.Identity, bias=mask_bias[:, h:h + 1],
                                         scale=mask_s[:, h:h + 1]).then_inc(s_bk_c, 1)

            def b_exp(p):
                act.wait_ge(s_bshift, p + 1)
                nc.scalar.activation(b_p[:, p % 2], b_p[:, p % 2], ACT.Exp, scale=B_SCALE).then_inc(s_bexp, 1)

            def b_pt_copy(p):
                act.wait_ge(s_bpt, p + 1)
                if p >= 2:
                    act.wait_ge(s_bo, p - 1)
                nc.scalar.copy(b_pt[:, p % 2], ps[:, 4, :].rearrange("p (g q) -> p g q", g=B_PAIRS)).then_inc(s_bpt_c, 1)

            def b_ot_copy(p):
                act.wait_ge(s_bot, p + 1)
                if p >= 2:
                    act.wait_ge(s_by, p - 1)
                nc.scalar.copy(b_ot[:, p % 2, :], ps[:, MISC, 0:P]).then_inc(s_bot_c, 1)

            for c in range(QUADS):
                norm_act(act, 2 * QUADS + c)
                norm_copy(act, 2 * QUADS + c)
                b_qk(c)
                for t in range(QT + 3):
                    if t < QT:
                        b_exp(QT * c + t)
                    if 1 <= t < QT + 1:
                        b_pt_copy(QT * c + t - 1)
                    if t >= 3:
                        b_ot_copy(QT * c + t - 3)
            moe(3 * QUADS, QUADS)

        @block.vector
        def _(dve):
            chain = Chain(dve, s_dve)
            nc.vector.memset(ps[:, 6, :], 0.0).then_inc(s_ctx_clear, 1)
            for b in range(BATCH):
                for g in (2 * b, 2 * b + 1):
                    norm_dve(dve, chain, g)
                for n in range(4 * b, 4 * b + 4):
                    dve.wait_ge(s_part1, n + 1)
                    if n:
                        dve.wait_ge(s_part3, n)
                    nc.vector.tensor_tensor(rest_s[:], ps[:, n % 2, :], part_s[:, 0, :], ALU.subtract).then_inc(s_rest, 1)

            def row_max(u, r):
                i, hp, kc, w = ROUNDS[r]
                n = N_ROUNDS * u + r
                dve.wait_ge(s_s1, n + 1)
                if u and r == 0:
                    dve.wait_ge(s_maxp, 2 * u)
                nc.vector.tensor_reduce(neg_max[:, kc, 2 * hp:2 * hp + 2, i],
                                        ps[:, 2 * (n % 2):2 * (n % 2) + 2, 0:w], AX.X, ALU.max,
                                        negate=True).then_inc(s_s1_read, 1)
                if r == N_ROUNDS - 1:
                    dve.wait_ge(s_s1_read, n + 1)
                    nc.vector.tensor_tensor(max_joined[:], neg_max[:, 0, :, QT:TILES], neg_max[:, 1, :, QT:TILES],
                                            ALU.min).then_inc(s_joined, 1)

            def ctx_norm(u, half):
                n = 2 * u + half
                b, hg = divmod(u, GROUPS)
                dve.wait_ge(s_ctx_t, n + 1)
                v = ps[:, MISC, :].rearrange("p (t g w) -> p t g w", t=QT, g=GROUP)
                chain.settle()
                if n:
                    dve.wait_ge(s_ctx_n, n)
                chain.add(nc.vector.reciprocal(ctx_rec[:], v[:, :, :, A_DIM]))
                chain.settle()
                if u == GROUPS and half == 0:
                    dve.wait_ge(s_ctxf_t, 2)
                dst = ctx_tok[:, half * QT:(half + 1) * QT, hg * GROUP * A_DIM:(hg + 1) * GROUP * A_DIM]
                nc.vector.tensor_tensor(dst.rearrange("p t (g d) -> p t g d", g=GROUP), v[:, :, :, 0:A_DIM],
                                        ctx_rec[:].unsqueeze(3).to_broadcast([P, QT, GROUP, A_DIM]),
                                        ALU.mult).then_inc(s_ctx_n, 1)

            def project(b):
                for k in range(2):
                    c = 2 * b + k
                    dve.wait_ge(s_proj, c + 1)
                    x4 = xs[:, c * QT:(c + 1) * QT, :]
                    chain.settle()
                    nc.vector.tensor_tensor(x4, ps[:, k, :].rearrange("p (t d) -> p t d", t=QT), x4, ALU.add)\
                        .then_inc(s_proj_read, 1)
                    dve.wait_ge(s_proj_read, c + 1)
                    chain.add(nc.vector.tensor_tensor(x4, x4, bproj_s[:].unsqueeze(1).to_broadcast([P, QT, DIM]), ALU.add))

            for r in range(N_ROUNDS):
                row_max(0, r)
            for u in range(UNITS):
                for kind, n in PLAN:
                    if kind == "S1" and u + 1 < UNITS:
                        row_max(u + 1, n)
                    if kind == "CTX":
                        ctx_norm(u, 0)
                    if kind == "CTX_PREV" and u % GROUPS:
                        ctx_norm(u - 1, 1)
                if u % GROUPS == GROUPS - 1:
                    ctx_norm(u, 1)
                    project(u // GROUPS)

            def route(g, r):
                bc = lambda v: v.unsqueeze(2).to_broadcast([P, QT, EXPERTS])
                row = lambda v: v.unsqueeze(1).to_broadcast([P, QT, EXPERTS])
                step = lambda ins: (chain.add(ins), chain.settle())
                dve.wait_ge(s_router, r + 1)
                if r:
                    dve.wait_ge(s_ew_t, r)
                score, biased, t0, sel1, shifted, e, sel2, t1, wts, rest = r_s[:10]
                m1, x1, m2, x2, smax, ssum, srec, vsum, vrec = r_m[:9]
                step(nc.vector.tensor_tensor(score, ps[:, MISC, 0:QT * EXPERTS].rearrange("p (t n) -> p t n", t=QT),
                                             row(br_s), ALU.add))
                step(nc.vector.tensor_reduce(smax, score, AX.X, ALU.max))
                nc.vector.tensor_tensor(shifted, score, bc(smax), ALU.subtract).then_inc(s_rshift, 1)
                step(nc.vector.tensor_tensor(biased, score, row(bias_s), ALU.add))
                step(nc.vector.tensor_reduce(m1, biased, AX.X, ALU.max))
                step(nc.vector.tensor_tensor(t0, biased, bc(m1), ALU.is_equal))
                step(nc.vector.tensor_tensor(t0, t0, row(order_s), ALU.mult))
                step(nc.vector.tensor_reduce(x1, t0, AX.X, ALU.max))
                step(nc.vector.tensor_tensor(sel1, t0, bc(x1), ALU.is_equal))
                step(nc.vector.scalar_tensor_tensor(out=biased, in0=sel1, scalar=NEG_HUGE, in1=biased,
                                                    op0=ALU.mult, op1=ALU.add))
                step(nc.vector.tensor_reduce(m2, biased, AX.X, ALU.max))
                step(nc.vector.tensor_tensor(t1, biased, bc(m2), ALU.is_equal))
                step(nc.vector.tensor_tensor(t1, t1, row(order_s), ALU.mult))
                step(nc.vector.tensor_reduce(x2, t1, AX.X, ALU.max))
                step(nc.vector.tensor_tensor(sel2, t1, bc(x2), ALU.is_equal))
                step(nc.vector.tensor_tensor(sel1, sel1, sel2, ALU.add))
                dve.wait_ge(s_rexp, r + 1)
                step(nc.vector.tensor_reduce(ssum, e, AX.X, ALU.add))
                step(nc.vector.reciprocal(srec, ssum))
                step(nc.vector.tensor_tensor(wts, e, bc(srec), ALU.mult))
                step(nc.vector.tensor_tensor(wts, wts, sel1, ALU.mult))
                step(nc.vector.tensor_reduce(vsum, wts, AX.X, ALU.add))
                step(nc.vector.reciprocal(vrec, vsum))
                step(nc.vector.tensor_tensor(wts, wts, bc(vrec), ALU.mult))
                step(nc.vector.tensor_copy(ew_parts[:, :, 0, :], wts))
                step(nc.vector.tensor_tensor(rest, wts, ew_parts[:, :, 0, :], ALU.subtract))
                step(nc.vector.tensor_copy(ew_parts[:, :, 1, :], rest))
                nc.vector.tensor_tensor(ew_parts[:, :, 2, :], rest, ew_parts[:, :, 1, :], ALU.subtract).then_inc(s_ew, 1)
                dve.wait_ge(s_ew, r + 1)

            def expert_items(f, pieces):
                for i, (n, half) in enumerate(ITEMS):
                    k = len(ITEMS) * f + i
                    dve.wait_ge(s_silu, k + 1)
                    dve.wait_ge(s_up, 2 * k + 2)
                    if k >= 2:
                        dve.wait_ge(s_hid, k - 1)
                    nc.vector.scalar_tensor_tensor(out=gated[:, k % 2, :], in0=ps[:, 2 * (k % 2) + 1, :],
                                                   scalar=bl1_s[:, n, 2 + half:3 + half], in1=silu_s[:, k % 2, :],
                                                   op0=ALU.add, op1=ALU.mult).then_inc(s_gate, 1)
                    if i in pieces:
                        pieces[i]()
                dve.wait_ge(s_y_t, f + 1)
                x4 = xs[:, (f % QUADS) * QT:(f % QUADS + 1) * QT, :]
                chain.settle()
                nc.vector.tensor_tensor(x4, ps[:, 6, :].rearrange("p (t d) -> p t d", t=QT), x4, ALU.add)\
                    .then_inc(s_added, 1)
                dve.wait_ge(s_added, f + 1 + (QUADS if f >= QUADS else 0))

            def moe(g0, r0):
                norm_dve(dve, chain, g0)
                route(g0, r0)
                for c in range(QUADS):
                    pieces = {}
                    if c + 1 < QUADS:
                        pieces = {1: lambda c=c: norm_dve(dve, chain, g0 + c + 1), 6: lambda c=c: route(g0 + c + 1, r0 + c + 1)}
                    expert_items(r0 + c, pieces)

            dve.wait_ge(s_late, 1)
            moe(QUADS, 0)

            def b_v(c):
                for k in range(2):
                    dve.wait_ge(s_bv, 2 * c + k + 1)
                    if c and k == 0:
                        dve.wait_ge(s_bo, QT * c)
                    for e in range(2):
                        lanes = slice(WIN * e, WIN * (e + 1))
                        src = ps[lanes, k, :].rearrange("p (w g e d) -> p w g e d", w=4, g=B_PAIRS, e=2)[:, :, :, e, :]
                        bias = b_bv[lanes, :].rearrange("p (g e d) -> p g e d", g=B_PAIRS, e=2)[:, :, e, :]
                        for w in range(4):
                            nc.vector.tensor_tensor(b_vbd[lanes, 4 * k + w, :, e * B_DIM:(e + 1) * B_DIM],
                                                    src[:, w], bias, ALU.add).then_inc(s_bv_c, 1)

            def b_shift(p):
                dve.wait_ge(s_bs, p + 1)
                s = ps[:, 2 + p % 2, :].rearrange("p (h k) -> p h k", h=B_HEADS)
                if p >= 2:
                    dve.wait_ge(s_bpt, p - 1)
                chain.add(nc.vector.tensor_reduce(b_mx[:, p % 2], s, AX.X, ALU.max))
                chain.settle()
                nc.vector.tensor_tensor(b_p[:, p % 2], s, b_mx[:, p % 2].unsqueeze(2).to_broadcast([P, B_HEADS, WIN]),
                                        ALU.subtract).then_inc(s_bshift, 1)

            def b_sums(p):
                dve.wait_ge(s_bexp, p + 1)
                if p >= 2:
                    dve.wait_ge(s_bo_n, p - 1)
                chain.settle()
                chain.add(nc.vector.tensor_reduce(b_sum[:, p % 2], b_p[:, p % 2], AX.X, ALU.add))
                chain.settle()
                chain.add(nc.vector.reciprocal(b_rec[:, p % 2], b_sum[:, p % 2]))
                chain.settle()

            def b_norm(p):
                dve.wait_ge(s_bo, p + 1)
                if p >= 2:
                    dve.wait_ge(s_bot, p - 1)
                nc.vector.tensor_tensor(b_o[:, p % 2, :].rearrange("p (h d) -> p h d", h=B_HEADS),
                                        ps[:, 6, 0:DIM].rearrange("p (h d) -> p h d", h=B_HEADS),
                                        b_rec[:, p % 2].unsqueeze(2).to_broadcast([P, B_HEADS, B_DIM]),
                                        ALU.mult).then_inc(s_bo_n, 1)

            for c in range(QUADS):
                norm_dve(dve, chain, 2 * QUADS + c)
                b_v(c)
                for t in range(QT + 3):
                    if t < QT:
                        b_shift(QT * c + t)
                    if 2 <= t < QT + 2:
                        b_norm(QT * c + t - 2)
                    if t < QT:
                        b_sums(QT * c + t)
                dve.wait_ge(s_by, QT * (c + 1))
                x4 = xs[:, c * QT:(c + 1) * QT, :]
                chain.settle()
                chain.add(nc.vector.scalar_tensor_tensor(out=x4, in0=ps[:, 5, :].rearrange("p (t d) -> p t d", t=QT),
                                                         scalar=2.0, in1=x4, op0=ALU.mult, op1=ALU.add))
                chain.settle()
                nc.vector.tensor_tensor(x4, x4, b_bout2.unsqueeze(1).to_broadcast([P, QT, DIM]), ALU.add)\
                    .then_inc(s_added, 1)
                dve.wait_ge(s_added, QUADS + c + 1)
            moe(3 * QUADS, QUADS)

        @block.tensor
        def _(pe):
            pe.wait_ge(s_const, 48)
            pe.wait_ge(s_wa, 80)
            pe.wait_ge(s_ctx_clear, 1)
            for b in range(BATCH):
                for g in (2 * b, 2 * b + 1):
                    if g:
                        pe.wait_ge(s_xt, xt_count(g - 1))
                    norm_pe(pe, g)
                pe.wait_ge(s_xt, xt_count(2 * b + 1))
                for k in range(2):
                    cols = xn_t[:, b, k * QCOLS:(k + 1) * QCOLS]
                    for s in range(2):
                        n = 4 * b + 2 * k + s
                        if n >= 2:
                            pe.wait_ge(s_rest, n - 1)
                        nc.tensor.matmul(ps[:, n % 2, :], wa[:, s, :], cols, start=True, stop=True).then_inc(s_qk_psum, 1)
                    c = 2 * b + k
                    if c >= 2:
                        pe.wait_ge(s_v, c - 1)
                    for t in range(QT):
                        ins = nc.tensor.matmul(ps[:, 2 + c % 2, t * P:(t + 1) * P], cols[:, t * P:(t + 1) * P],
                                               wa[:, 2, :], start=True, stop=True)
                    ins.then_inc(s_v_psum, 1)
            pe.wait_ge(s_v, QUADS)
            pe.wait_ge(s_ones, 1)

            def score_queries(u, r):
                i, hp, kc, w = ROUNDS[r]
                b, hg = divmod(u, GROUPS)
                n = N_ROUNDS * u + r
                if r == 0:
                    pe.wait_ge(s_rows[u], 16 * 20)
                if n >= 2:
                    pe.wait_ge(s_s1_read, n - 1)
                diagonal = kc == i // 4
                for h2 in range(2):
                    h = hg * GROUP + 2 * hp + h2
                    bank = 2 * (n % 2) + h2
                    ins = nc.tensor.matmul(ps[:, bank, 0:w], q_rows[b][0:MAX_ROWS_FROM, h, i * P:(i + 1) * P],
                                           k_rows[b][0:MAX_ROWS_FROM, h, kc * QCOLS:kc * QCOLS + w],
                                           start=True, stop=not diagonal)
                    if diagonal:
                        ins = nc.tensor.matmul(ps[:, bank, w - P:w], ident_b[:], causal_s[:], start=False, stop=True)
                ins.then_inc(s_s1, 1)

            def turn_max(u, half):
                n = 2 * u + half
                pe.wait_ge(s_maxp, n + 1)
                if half == 0 and u:
                    pe.wait_ge(s_ctx_n, 2 * (u - 1) + 1)
                if half and u:
                    pe.wait_ge(s_ctx_n, 2 * u)
                if n:
                    pe.wait_ge(s_maxc, n)
                nc.tensor.transpose(max_bank(ps), max_parts[:].rearrange("p a h t -> p (a h t)"), ident_b[:])\
                    .then_inc(s_maxt, 1)

            def score_keys(u, s):
                c, j, q, w = STEPS[s]
                b, hg = divmod(u, GROUPS)
                if s == 0:
                    pe.wait_ge(s_maxd, 16 * PARTS * GROUP * (2 * u + 1))
                if j == 0 and c == 1:
                    pe.wait_ge(s_maxd, 16 * PARTS * GROUP * (2 * u + 2))
                for h in range(GROUP):
                    n = GROUP * (N_STEPS * u + s) + h
                    if n >= 2:
                        pe.wait_ge(s_probs, n - 1)
                    nc.tensor.matmul(ps[:, 4 + n % 2, 0:w], k_rows[b][:, hg * GROUP + h, j * P:(j + 1) * P],
                                     q_rows[b][:, hg * GROUP + h, q:q + w], start=True, stop=True).then_inc(s_s2, 1)

            def weigh_values(u, s):
                c, j, q, w = STEPS[s]
                b, hg = divmod(u, GROUPS)
                pe.wait_ge(s_probs, GROUP * (N_STEPS * u + s + 1))
                if s in DIAG:
                    pe.wait_ge(s_masked, len(DIAG) * u + DIAG.index(s) + 1)
                if j == 0 and (u or c):
                    pe.wait_ge(s_ctx_copied, 2 * u + c)
                for h in range(GROUP):
                    ins = nc.tensor.matmul(ps[32 * h:32 * h + VCOLS, 6, q - c * QCOLS:q - c * QCOLS + w],
                                           v_s[:, b * TILES + j, hg * GROUP + h, :], probs[:, s % 2, h, 0:w],
                                           start=(j == 0), stop=(j == 4 * c + 3))
                ins.then_inc(s_pv, 1)

            def turn_ctx(u, half):
                n = 2 * u + half
                pe.wait_ge(s_ctx_copied, n + 1)
                if n:
                    pe.wait_ge(s_ctx_n, n)
                if half == 0:
                    pe.wait_ge(s_maxc, 2 * u + 2)
                else:
                    pe.wait_ge(s_maxc, min(2 * u + 3, 2 * UNITS))
                for t in range(QT):
                    ins = nc.tensor.transpose(ps[:, MISC, t * P:(t + 1) * P], ctx_s[:, t * P:(t + 1) * P], ident_s[:])
                ins.then_inc(s_ctx_t, 1)

            def finish_batch(b):
                pe.wait_ge(s_ctx_n, 2 * GROUPS * (b + 1))
                pe.wait_ge(s_s1_read, min(N_ROUNDS * (GROUPS * (b + 1) + 1), N_ROUNDS * UNITS))
                for k in range(2):
                    for t in range(QT):
                        ins = nc.tensor.transpose(ps[:, 2 + k, t * P:(t + 1) * P], ctx_tok[:, k * QT + t, :], ident_s[:])
                    ins.then_inc(s_ctxf_t, 1)
                pe.wait_ge(s_ctxf, 3 * (b + 1))
                for k in range(2):
                    for t in range(QT):
                        col = ROLL + (k * QT + t) * P
                        ins = nc.tensor.matmul(ps[:, k, t * P:(t + 1) * P], ctx_t[:, col:col + P], wa[:, 3, :],
                                               start=True, stop=True)
                    ins.then_inc(s_proj, 1)
                pe.wait_ge(s_proj_read, 2 * (b + 1))

            for r in range(N_ROUNDS):
                score_queries(0, r)
                if r == HALF_ROUNDS + 1:
                    turn_max(0, 0)
            for u in range(UNITS):
                for kind, n in PLAN:
                    if kind == "S1" and u + 1 < UNITS:
                        score_queries(u + 1, n)
                    if kind == "S2":
                        score_keys(u, n)
                    if kind == "PV":
                        weigh_values(u, n)
                    if kind == "MAX":
                        turn_max(u, 1)
                    if kind == "MAX_NEXT" and u + 1 < UNITS:
                        turn_max(u + 1, 0)
                    if kind == "CTX":
                        turn_ctx(u, 0)
                    if kind == "CTX_PREV" and u % GROUPS:
                        turn_ctx(u - 1, 1)
                if u % GROUPS == GROUPS - 1:
                    turn_ctx(u, 1)
                    finish_batch(u // GROUPS)

            def router(g, r):
                b, col = quad_cols(g % QUADS)
                pe.wait_ge(s_xt, xt_count(g))
                for t in range(QT):
                    ins = nc.tensor.matmul(ps[:, MISC, t * EXPERTS:(t + 1) * EXPERTS],
                                           xn_t[:, b, col + t * P:col + (t + 1) * P], wr_s, start=True, stop=True)
                ins.then_inc(s_router, 1)

            def turn_weights(g, r):
                pe.wait_ge(s_ew, r + 1)
                rows = ew_bank(ps)[0]
                for t in range(QT):
                    nc.tensor.transpose(rows[:, t * P:(t + 1) * P], ew_parts[:, t].rearrange("p q n -> p (q n)"), ident_b[:])
                if r >= QUADS or r % QUADS >= 2:
                    pe.wait_ge(s_added, max(r - 1, QUADS) + QUADS if r >= QUADS else r - 1)
                for t in range(QT):
                    ins = nc.tensor.transpose(ps[0:EXPERTS, MISC - 1, t * P:(t + 1) * P], r_s[8][:, t, :], ident_s[:])
                ins.then_inc(s_ew_t, 1)

            def expert_items(f, pieces):
                b, col = quad_cols(f % QUADS)
                cols = xn_t[:, b, col:col + QCOLS]
                pe.wait_ge(s_ew_c, 2 * (f + 1))

                def down(i):
                    k = len(ITEMS) * f + i
                    n, half = ITEMS[i]
                    pe.wait_ge(s_hid, k + 1)
                    nc.tensor.matmul(ps[:, 5, :], w2_s[:, n, half, :], hidden[:, k % 3, :],
                                     start=False, stop=(i == len(ITEMS) - 1)).then_inc(s_down, 1)

                if f:
                    pe.wait_ge(s_y_c, f)
                nc.tensor.matmul(ps[:, 5, :], bl2_s[0:EXPERTS, :], ew_t[0:EXPERTS, f % 2, :], start=True, stop=False)
                for i, (n, half) in enumerate(ITEMS):
                    k = len(ITEMS) * f + i
                    if half == 0:
                        if k:
                            pe.wait_ge(s_wide_c, k // 2)
                        nc.tensor.matmul(ps[:, 4, :], exp_rows[0:PARTS * EXPERTS, n, :], ew_rows[0:PARTS * EXPERTS, f % 2, :],
                                         start=True, stop=True).then_inc(s_wide, 1)
                    if k >= 2:
                        pe.wait_ge(s_gate, k - 1)
                    for s in range(2):
                        h = s * HID + half * P
                        nc.tensor.matmul(ps[:, 2 * (k % 2) + s, :], w1_s[:, n, h:h + P], cols,
                                         start=True, stop=True).then_inc(s_up, 1)
                    if i >= 2:
                        down(i - 2)
                    if i in pieces:
                        pieces[i]()
                down(len(ITEMS) - 2)
                down(len(ITEMS) - 1)
                pe.wait_ge(s_down, len(ITEMS) * (f + 1))

            def finish_y(f):
                pe.wait_ge(s_y_c, f + 1)
                if f + 1 < 2 * QUADS and f % QUADS < QUADS - 1:
                    pe.wait_ge(s_ew_c, 2 * (f + 2))
                for t in range(QT):
                    ins = nc.tensor.transpose(ps[:, 6, t * P:(t + 1) * P], y_s[:, t * P:(t + 1) * P], ident_s[:])
                ins.then_inc(s_y_t, 1)

            def moe(g0, r0):
                norm_pe(pe, g0)
                router(g0, r0)
                turn_weights(g0, r0)
                for c in range(QUADS):
                    pieces = {}
                    if c + 1 < QUADS:
                        pieces = {3: lambda c=c: norm_pe_after(pe, g0 + c + 1, r0 + c),
                                  5: lambda c=c: router(g0 + c + 1, r0 + c + 1),
                                  10: lambda c=c: turn_weights(g0 + c + 1, r0 + c + 1)}
                    expert_items(r0 + c, pieces)
                    finish_y(r0 + c)

            def norm_pe_after(pe, g, r):
                pe.wait_ge(s_ew_c, 2 * (r + 1))
                norm_pe(pe, g)

            pe.wait_ge(s_late, 1)
            moe(QUADS, 0)

            for c in range(QUADS):
                g = 2 * QUADS + c
                b, col = quad_cols(c)
                cols = xn_t[:, b, col:col + QCOLS]
                if c:
                    pe.wait_ge(s_bot_c, QT * c)
                norm_pe(pe, g)
                pe.wait_ge(s_xt, xt_count(g))
                if c:
                    pe.wait_ge(s_bv_c, 16 * c)
                for s in range(2):
                    nc.tensor.matmul(ps[:, s, :], b_win[:, s * DIM:(s + 1) * DIM], cols, start=True, stop=True)\
                        .then_inc(s_bqk, 1)
                for k in range(2):
                    pe.wait_ge(s_bq_c if k == 0 else s_bk_c, c + 1 if k == 0 else B_HEADS * (c + 1))
                    for w in range(4):
                        at_col = col + (4 * k + w) * WIN
                        for e in range(2):
                            ins = nc.tensor.matmul(ps[WIN * e:WIN * (e + 1), k, w * P:(w + 1) * P],
                                                   xn_t[:, b, at_col:at_col + WIN], b_win[:, 2 * DIM:3 * DIM],
                                                   start=True, stop=True)
                    ins.then_inc(s_bv, 1)

                def scores(t):
                    p = QT * c + t
                    if p >= 2:
                        pe.wait_ge(s_bshift, p - 1)
                    for e in range(2):
                        w = 2 * t + e
                        ins = nc.tensor.matmul(ps[WIN * e:WIN * (e + 1), 2 + p % 2, :], bq_s[:, w * WIN:(w + 1) * WIN],
                                               bk_s[:, :, w * WIN:(w + 1) * WIN], start=True, stop=True)
                    ins.then_inc(s_bs, 1)

                def turn_probs(t):
                    p = QT * c + t
                    pe.wait_ge(s_bexp, p + 1)
                    if p:
                        pe.wait_ge(s_bpt_c, p)
                    for g2 in range(B_PAIRS):
                        ins = nc.tensor.transpose(ps[:, 4, g2 * P:(g2 + 1) * P],
                                                  b_p[:, p % 2, 2 * g2:2 * g2 + 2, :].rearrange("p h k -> p (h k)"), ident_s[:])
                    ins.then_inc(s_bpt, 1)

                def weigh(t):
                    p = QT * c + t
                    pe.wait_ge(s_bpt_c, p + 1)
                    pe.wait_ge(s_bv_c, 16 * c + 16)
                    if p:
                        pe.wait_ge(s_bo_n, p)
                    for e in range(2):
                        for g2 in range(B_PAIRS):
                            ins = nc.tensor.matmul(ps[WIN * e:WIN * (e + 1), 6, g2 * 32:(g2 + 1) * 32],
                                                   b_pt[:, p % 2, g2, WIN * e:WIN * (e + 1)], b_vbd[:, 2 * t + e, g2, :],
                                                   start=True, stop=True)
                    ins.then_inc(s_bo, 1)

                def turn_o(t):
                    p = QT * c + t
                    pe.wait_ge(s_bo_n, p + 1)
                    if p:
                        pe.wait_ge(s_bot_c, p)
                    nc.tensor.transpose(ps[:, MISC, 0:P], b_o[:, p % 2, :], ident_s[:]).then_inc(s_bot, 1)

                def out_proj(t):
                    p = QT * c + t
                    pe.wait_ge(s_bot_c, p + 1)
                    if t == 0:
                        pe.wait_ge(s_added, QUADS + c)
                    nc.tensor.matmul(ps[:, 5, t * DIM:(t + 1) * DIM], b_ot[:, p % 2, :], b_wout,
                                     start=True, stop=True).then_inc(s_by, 1)

                pe.wait_ge(s_bk_c, B_HEADS * (c + 1))
                for t in range(QT + 3):
                    if t < QT:
                        scores(t)
                    if 1 <= t < QT + 1:
                        turn_probs(t - 1)
                    if 2 <= t < QT + 2:
                        weigh(t - 2)
                    if t >= 3:
                        turn_o(t - 3)
                        out_proj(t - 3)
            moe(3 * QUADS, QUADS)


def max_bank(ps):
    return ps[0:PARTS * GROUP * QT, 7, 0:P // 2].bitcast(BF16)


def ew_bank(ps):
    return ps[0:PARTS * EXPERTS, 7, 0:QCOLS // 2].bitcast(BF16), None


def constants():
    import numpy as np

    def bf(a):
        bits = np.ascontiguousarray(a, np.float32).view(np.uint32)
        return ((bits + 0x7FFF + ((bits >> 16) & 1)) >> 16).astype(np.uint16)

    def split(a):
        parts = []
        for _ in range(PARTS):
            parts.append(bf(a))
            a = a - (parts[-1].astype(np.uint32) << 16).view(np.float32)
        return np.stack(parts)

    slopes = (np.float32(2.0) ** (np.float32(-8.0) * np.arange(1, A_HEADS + 1, dtype=np.float32) / A_HEADS)).astype(np.float32)
    slope_pos = slopes[:, None] * np.arange(TOKENS, dtype=np.float32)[None, :]
    key_rows = np.concatenate([split(slope_pos), bf(np.ones((PARTS, A_HEADS, TOKENS)))])
    causal = bf(np.where(np.arange(P)[None, :] > np.arange(P)[:, None], NEG_BIG, 0.0))
    rows = np.zeros((PARTS, EXPERTS, EXPERTS, P))
    for n in range(EXPERTS):
        rows[:, n, n, :] = 1
    mask = np.zeros((P, B_HEADS), np.float32)
    for h in range(B_HEADS):
        mask[h * B_DIM:(h + 1) * B_DIM, h] = 1
    return {
        "ident": np.eye(P, dtype=np.float32), "ident_bf": bf(np.eye(P)), "causal": causal,
        "key_rows": key_rows, "expert_rows": bf(rows.reshape(PARTS * EXPERTS, EXPERTS, P)), "head_mask": mask,
        "order": np.tile(np.arange(EXPERTS, 0, -1, dtype=np.float32), (P, 1)),
    }


def kernel(**inputs):
    import numpy as np
    import concourse.bacc as bacc
    from concourse.bass_utils import run_bass_kernel_spmd

    a = {k: np.asarray(v) for k, v in inputs.items()}
    bl1 = a["L0_ffn_bl1"]
    arrays = {
        "x": a["L0_attn_a_x"], "w_q": a["L0_attn_a_W_query"], "w_k": a["L0_attn_a_W_key"],
        "w_v": a["L0_attn_a_W_value"], "w_proj": a["L0_attn_a_W_proj"], "b_proj": a["L0_attn_a_b_proj"],
        "b_in_wt": a["L0_attn_b_in_proj_w"].T, "b_in_b": a["L0_attn_b_in_proj_b"],
        "b_in_b_t": a["L0_attn_b_in_proj_b"].reshape(3, P).T,
        "b_out_wt": a["L0_attn_b_out_w"].T, "b_out_b": a["L0_attn_b_out_b"],
        "wr_t": a["L0_ffn_Wr"].T, "br": a["L0_ffn_br"], "wl1": a["L0_ffn_Wl1"],
        "bl1_t": bl1.reshape(EXPERTS, 4, P).transpose(2, 0, 1), "wl2": a["L0_ffn_Wl2"], "bl2": a["L0_ffn_bl2"],
        "biases": a["L0_ffn_biases_N"], **constants(),
    }
    nc = bacc.Bacc("TRN2", target_bir_lowering=False, num_devices=1)
    feed, args = {}, {}
    for name, v in arrays.items():
        v = np.ascontiguousarray(v)
        feed[f"in_{name}"] = v
        ap = nc.dram_tensor(f"in_{name}", v.shape, mybir.dt.from_np(v.dtype), kind="ExternalInput").ap()
        args[name] = ap.bitcast(BF16) if v.dtype == np.uint16 else ap
    out = nc.dram_tensor("out_x", (BATCH, TOKENS, DIM), F32, kind="ExternalOutput").ap()
    build(nc, **args, out=out)
    r = run_bass_kernel_spmd(nc, [feed], core_ids=[0])
    return r.results[0]["out_x"]
```

```python
from contextlib import ExitStack

import concourse.bass as bass
from concourse import mybir

F32 = mybir.dt.float32
BF16 = mybir.dt.bfloat16
ALU = mybir.AluOpType
ACT = mybir.ActivationFunctionType
AX = mybir.AxisListType

P = 128
BATCH, TOKENS, DIM = 2, 1024, 128
ROLL = 32
TILES = TOKENS // P
QUADS = BATCH * 2
QT = 4
QCOLS = QT * P
EPS = 1e-5

A_HEADS, A_DIM = 16, 8
GROUP = 4
GROUPS = A_HEADS // GROUP
UNITS = BATCH * GROUPS
PARTS = 3
PAIR_ROWS = PARTS * PARTS * A_DIM
MAX_ROWS_FROM = PAIR_ROWS + PARTS
SCORE_ROWS = MAX_ROWS_FROM + PARTS
VCOLS = A_DIM + 1
A_SCALE = float(A_DIM) ** -0.5

EXPERTS, HID = 8, 256

B_HEADS, B_DIM, WIN = 8, 16, 64
B_PAIRS = B_HEADS // 2
WINS_PER_QUAD = QCOLS // WIN
B_SCALE = float(B_DIM) ** -0.5
NEG_BIG = -1e30
NEG_HUGE = -3e38

STEPS = []
for _c in range(2):
    for _j in range(4 * _c + 4):
        _q = max(P * _j, QCOLS * _c)
        STEPS.append((_c, _j, _q, QCOLS * (_c + 1) - _q))
N_STEPS = len(STEPS)
DIAG = [s for s, (c, j, q, w) in enumerate(STEPS) if q == P * j]
LAST_STEP = [3, N_STEPS - 1]
ROUNDS = []
for _i in range(TILES):
    for _h in range(GROUP):
        for _kc in range(1 + (_i >= QT)):
            ROUNDS.append((_i, _h, _kc, min(QCOLS, P * (_i + 1) - QCOLS * _kc)))
N_ROUNDS = len(ROUNDS)
HALF_ROUNDS = QT * GROUP
RING = 3


AHEAD = 3


def stage_plan():
    plan = [("S1", r) for r in range(AHEAD)] + [("CTX_PREV", 1), ("MAX", 1)]
    work = sum(w for _, _, _, w in ROUNDS) / sum(GROUP * w for _, _, _, w in STEPS)
    r, done1, done2 = AHEAD, sum(ROUNDS[r][3] for r in range(AHEAD)), 0
    maxed = False

    def rounds_until(goal):
        nonlocal r, done1
        while r < N_ROUNDS and done1 < goal:
            plan.append(("S1", r))
            done1 += ROUNDS[r][3]
            r += 1

    for s in range(N_STEPS):
        for half in range(2):
            plan.append(("S2", 2 * s + half))
            done2 += 2 * STEPS[s][3]
            if half and s >= 1:
                plan.append(("PV", s - 1))
                if s - 1 == LAST_STEP[0]:
                    plan.append(("CTX_COPY", 0))
                if s - 1 == LAST_STEP[0] + 1:
                    plan.append(("CTX", 0))
            rounds_until(done2 * work)
        if not maxed and r >= HALF_ROUNDS + RING and s >= 7:
            plan.append(("MAX_NEXT", 0))
            maxed = True
    rounds_until(1 << 30)
    plan += [("PV", N_STEPS - 1), ("CTX_COPY", 1)]
    return plan


PLAN = stage_plan()

ITEMS = [(n, f) for n in range(EXPERTS) for f in range(2)]


K_ON_ACT = 4


def b_plan():
    plan = [("QK", 0), ("K_MASK", 0), ("V", 0)]
    pairs = QUADS * QT
    for t in range(pairs + 5):
        if t < pairs:
            plan.append(("S", t))
        for kind, lag in (("T", 2), ("W", 3), ("O", 4)):
            if 0 <= t - lag < pairs:
                plan.append((kind, t - lag))
        if t >= 4 and (t - 4) % QT == QT - 1 and t - 4 < pairs:
            plan.append(("Y", (t - 4) // QT))
        c = t // QT + 1
        if c < QUADS:
            plan += {0: [("NORM", 2 * QUADS + c)], 1: [("QK", c)], 2: [("K_MASK", c)], 3: [("V", c)]}[t % QT]
        if t == 13:
            plan.append(("NORM", 3 * QUADS))
    return plan


B_PLAN = b_plan()


class Chain:

    def __init__(self, eng, sem):
        self.eng, self.sem, self.n = eng, sem, 0

    def add(self, ins):
        self.n += 1
        return ins.then_inc(self.sem, 1)

    def settle(self):
        if self.n:
            self.eng.wait_ge(self.sem, self.n)


def build(nc, x, w_q, w_k, w_v, w_proj, b_proj, b_in_wt, b_in_b, b_in_b_t, b_out_wt, b_out_b,
          wr_t, br, wl1, bl1_t, wl2, bl2, biases, ident, ident_bf, causal, key_rows,
          expert_rows, head_mask, order, out):
    with ExitStack() as ctx:
        def sb(name, shape, dt=F32):
            return ctx.enter_context(nc.sbuf_tensor(name, shape, dt))

        def sem(name):
            return ctx.enter_context(nc.semaphore(name))

        q_dram = nc.dram_tensor("q_parts", [BATCH, 2, A_HEADS, 2 * PARTS - 1, A_DIM, QCOLS], BF16).ap()
        k_dram = nc.dram_tensor("k_parts", [BATCH, A_HEADS, PARTS, A_DIM, TOKENS], BF16).ap()

        xs = sb("x_rolled", [P, BATCH * TILES, DIM])
        xn = sb("x_normed", [P, QT, DIM])
        xn_t = sb("x_normed_t", [P, BATCH, TOKENS + ROLL])
        ident_s = sb("ident_s", [P, P])
        ident_b = sb("ident_b", [P, P], BF16)
        causal_s = sb("causal_s", [P, P], BF16)
        wa = sb("attn_a_weights", [P, 4, DIM])
        bproj_s = sb("bproj_s", [P, DIM])
        stats = sb("stats", [P, QT, 6])
        mv = sb("mean_var", [P, QT, 2])
        var_eps = sb("var_eps", [P, QT])
        minus_half = sb("minus_half", [P, QT])
        rstd = sb("rstd", [P, QT])

        region = sb("region", [P, 2 * BATCH * A_HEADS * TOKENS // 2])
        region_b = region[:].bitcast(BF16)
        side = A_HEADS * TOKENS
        q_rows = [region_b[0:SCORE_ROWS, (2 * b) * side:(2 * b + 1) * side]
                  .rearrange("r (c h t) -> r c h t", c=2, h=A_HEADS) for b in range(BATCH)]
        k_rows = [region_b[0:SCORE_ROWS, (2 * b + 1) * side:(2 * b + 2) * side].rearrange("r (h t) -> r h t", h=A_HEADS)
                  for b in range(BATCH)]
        part_s = sb("parts", [P, 2, 2, PARTS, QCOLS], BF16)
        rest_s = sb("rest", [P, 2, QCOLS])
        v_s = sb("v_ones", [P, BATCH * TILES, A_HEADS, VCOLS])
        probs = sb("probs", [P, 2, GROUP, QCOLS])
        neg_max = sb("neg_max", [P, 2, GROUP, TILES])
        max_joined = sb("max_joined", [P, GROUP, QT])
        max_rest = sb("max_rest", [P, GROUP, QT])
        max_parts = sb("max_parts", [P, PARTS, GROUP, QT], BF16)
        max_t = sb("max_t", [PARTS * GROUP * QT, P], BF16)
        ctx_s = sb("ctx_s", [P, QCOLS])
        ctx_rec = sb("ctx_rec", [P, QT, GROUP])

        at = [0]

        def carve(shape):
            n = 1
            for d in shape:
                n *= d
            v = region[:, at[0]:at[0] + n]
            at[0] += n
            names = "abcd"[:len(shape)]
            if len(shape) == 1:
                return v
            return v.rearrange(f"p ({' '.join(names)}) -> p {' '.join(names)}", **dict(zip(names, shape)))

        w1_s = carve([EXPERTS, 2 * HID])
        w2_s = carve([EXPERTS, 2, DIM])
        bl1_s = carve([EXPERTS, 4])
        bl2_s = carve([DIM])
        wr_s = carve([EXPERTS])
        br_s = carve([EXPERTS])
        bias_s = carve([EXPERTS])
        order_s = carve([EXPERTS])
        b_win = carve([3 * DIM])
        b_wout = carve([DIM])
        b_bin = carve([3])
        b_bv = carve([DIM])
        b_bout = carve([DIM])
        b_bout2 = carve([DIM])
        mask_s = carve([B_HEADS])
        mask_bias = carve([B_HEADS])
        exp_rows = carve([EXPERTS * P // 2]).bitcast(BF16).rearrange("p (n q) -> p n q", n=EXPERTS)
        silu_s = carve([2, QCOLS])
        gated = carve([2, QCOLS])
        ew_wide = carve([2, QCOLS])
        hidden = carve([3, QCOLS])
        y_s = carve([QCOLS])
        r_s = [carve([QT, EXPERTS]) for _ in range(14)]
        r_m = [carve([QT]) for _ in range(10)]
        ew_parts = carve([QT * PARTS * EXPERTS // 2]).bitcast(BF16).rearrange("p (t q n) -> p t q n", t=QT, q=PARTS)
        ew_rows = carve([2, QCOLS // 2]).bitcast(BF16).rearrange("p a (q) -> p a q")
        ew_t = carve([2, QCOLS])
        assert at[0] <= A_HEADS * TOKENS
        at[0] = A_HEADS * TOKENS
        bq_s = carve([2, QCOLS])
        bk1_s = carve([QCOLS])
        bk_s = carve([2, B_HEADS, QCOLS])
        b_vbd = carve([2, WINS_PER_QUAD, B_PAIRS, 2 * B_DIM])
        b_p = carve([3, B_HEADS, WIN])
        b_mx = carve([2, B_HEADS])
        b_sum = carve([4, B_HEADS])
        b_rec = carve([4, B_HEADS])
        b_pt = carve([2, B_PAIRS, P])
        b_o = carve([2, DIM])
        b_ot = carve([2, P])
        ctx_tok = carve([0 + 1]) if False else sb("ctx_tok", [P, TILES, DIM])
        ctx_t = sb("ctx_t", [P, TOKENS + ROLL])
        assert at[0] <= 2 * A_HEADS * TOKENS

        ps = ctx.enter_context(nc.psum_tensor("ps", [P, 8, QCOLS], F32))
        MISC = 7

        s_x = sem("x_loaded")
        s_const = sem("constants_loaded")
        s_wa = sem("attn_a_weights_loaded")
        s_dve = sem("dve_own")
        s_act = sem("act_own")
        s_pool = sem("pool_own")
        s_var = sem("variance_ready")
        s_std = sem("rstd_ready")
        s_normed = sem("quad_normed")
        s_norm_t = sem("quad_transposed")
        s_xt = sem("xn_t_written")
        s_xt_used = sem("xn_t_used")
        s_qk_psum = sem("qk_in_psum")
        s_part1 = sem("part1_ready")
        s_rest = sem("rest_ready")
        s_part2 = sem("part2_ready")
        s_part3 = sem("part3_ready")
        s_parts_out = sem("parts_stored")
        s_v_psum = sem("v_in_psum")
        s_v = sem("v_ready")
        s_ones = sem("v_ones_set")
        s_rows = [sem(f"score_rows_loaded_{u}") for u in range(UNITS)]
        s_fixed = sem("fixed_rows_loaded")
        s_s1 = sem("round_scored")
        s_s1_read = sem("round_maxed")
        s_joined = sem("chunk_maxima_joined")
        s_maxp = sem("max_parts_ready")
        s_maxt = sem("max_transposed")
        s_maxc = sem("max_rows_copied")
        s_maxd = sem("max_rows_placed")
        s_s2 = sem("step_scored")
        s_probs = sem("exp_done")
        s_masked = sem("diagonal_masked")
        s_pv = sem("pv_done")
        s_ctx_clear = sem("ctx_bank_cleared")
        s_ctx_copied = sem("ctx_copied")
        s_ctx_t = sem("ctx_transposed")
        s_ctx_n = sem("ctx_normalised")
        s_ctxf_t = sem("ctx_tiles_transposed")
        s_ctxf = sem("ctx_t_written")
        s_proj = sem("projection_done")
        s_proj_read = sem("projection_added")
        s_w = sem("late_weights_loaded")
        s_late = sem("late_constants_ready")
        s_router = sem("router_scores_done")
        s_rshift = sem("router_shifted")
        s_rexp = sem("router_exp_done")
        s_ew = sem("expert_weights_ready")
        s_ew_t = sem("expert_weights_transposed")
        s_ew_c = sem("expert_weights_copied")
        s_up = sem("item_up_done")
        s_silu = sem("item_silu_done")
        s_gate = sem("item_gated")
        s_wide = sem("expert_weight_spread")
        s_wide_c = sem("expert_weight_copied")
        s_hid = sem("item_hidden_ready")
        s_down = sem("item_down_done")
        s_y_c = sem("y_copied")
        s_y_t = sem("y_transposed")
        s_added = sem("y_added")
        s_bqk = sem("b_qk_done")
        s_bq_c = sem("b_q_copied")
        s_bk_c = sem("b_k_copied")
        s_bk1 = sem("b_k_biased")
        s_bkp = sem("b_k_masked_by_pool")
        s_bv = sem("b_v_done")
        s_bv_c = sem("b_v_copied")
        s_bs = sem("b_scores_done")
        s_bshift = sem("b_scores_shifted")
        s_bexp = sem("b_exp_done")
        s_bpt = sem("b_probs_transposed")
        s_bpt_c = sem("b_probs_t_copied")
        s_bo = sem("b_pv_done")
        s_bo_n = sem("b_o_normalised")
        s_bot = sem("b_o_transposed")
        s_bot_c = sem("b_o_t_copied")
        s_by = sem("b_y_done")
        s_out = sem("out_stored")

        def rolled(dram, b):
            full = TILES - 1
            yield (xs[:, b * TILES:b * TILES + full, :],
                   dram[b, ROLL:ROLL + full * P, :].rearrange("(t p) d -> p t d", p=P))
            yield xs[0:P - ROLL, b * TILES + full, :], dram[b, ROLL + full * P:TOKENS, :]
            yield xs[P - ROLL:P, b * TILES + full, :], dram[b, 0:ROLL, :]

        def quad_cols(c):
            return c // 2, ROLL + (c % 2) * QCOLS

        def norm_dve(dve, chain, g):
            c = g % QUADS
            if g < QUADS:
                dve.wait_ge(s_x, 96)
            chain.settle()
            for t in range(QT):
                chain.add(nc.vector.bn_stats(stats[:, t, :], xs[:, c * QT + t, :]))
            chain.settle()
            for t in range(QT):
                chain.add(nc.vector.bn_aggr(mv[:, t, :], stats[:, t, :]))
            chain.settle()
            if g:
                dve.wait_ge(s_std, g)
            nc.vector.tensor_scalar_add(var_eps[:], mv[:, :, 1], EPS).then_inc(s_var, 1)
            dve.wait_ge(s_std, g + 1)
            if g:
                dve.wait_ge(s_norm_t, g)
            for t in range(QT):
                nc.vector.tensor_scalar(xn[:, t, :], xs[:, c * QT + t, :], mv[:, t, 0:1], rstd[:, t:t + 1],
                                        ALU.subtract, ALU.mult).then_inc(s_normed, 1)
            dve.wait_ge(s_normed, QT * (g + 1))

        def norm_pool(pool, g):
            pool.wait_ge(s_var, g + 1)
            if g:
                pool.wait_ge(s_normed, QT * g)
            nc.gpsimd.tensor_tensor(rstd[:], var_eps[:], minus_half[:], ALU.pow).then_inc(s_std, 1)

        def norm_pe(pe, g):
            pe.wait_ge(s_normed, QT * (g + 1))
            for t in range(QT):
                ins = nc.tensor.transpose(ps[:, MISC, t * P:(t + 1) * P], xn[:, t, :], ident_s[:])
            ins.then_inc(s_norm_t, 1)

        def norm_copy(act, g):
            b, col = quad_cols(g % QUADS)
            act.wait_ge(s_norm_t, g + 1)
            nc.scalar.copy(xn_t[:, b, col:col + QCOLS], ps[:, MISC, :]).then_inc(s_xt, 1)
            if g < QUADS and g % 2:
                nc.scalar.copy(xn_t[:, b, 0:ROLL], ps[:, MISC, QCOLS - ROLL:QCOLS]).then_inc(s_xt, 1)

        PARTS_OUT = 2 * 16 * (3 * PARTS - 1)

        def xt_count(g):
            return g + 1 + (2 if g >= 3 else 1 if g >= 1 else 0)

        block = ctx.enter_context(nc.Block())

        def load_late(sp):
            sp.wait_ge(s_pv, N_STEPS * GROUPS)
            sp.dma_start(w1_s, wl1.rearrange("n d h -> d n h")).then_inc(s_w, 16)
            for f in range(2):
                sp.dma_start(w2_s[:, :, f, :], wl2[:, f * P:(f + 1) * P, :].rearrange("n h d -> h n d")).then_inc(s_w, 16)
            sp.dma_start(bl1_s, bl1_t).then_inc(s_w, 16)
            sp.dma_start(bl2_s[0:EXPERTS, :], bl2).then_inc(s_w, 16)
            sp.dma_start(wr_s, wr_t).then_inc(s_w, 16)
            sp.dma_start(br_s, br.partition_broadcast(P)).then_inc(s_w, 16)
            sp.dma_start(bias_s, biases.partition_broadcast(P)).then_inc(s_w, 16)
            sp.dma_start(order_s, order).then_inc(s_w, 16)
            sp.dma_start(b_win, b_in_wt).then_inc(s_w, 16)
            sp.dma_start(b_wout, b_out_wt).then_inc(s_w, 16)
            sp.dma_start(b_bin, b_in_b_t).then_inc(s_w, 16)
            sp.dma_start(b_bv, b_in_b[2 * DIM:3 * DIM].partition_broadcast(P)).then_inc(s_w, 16)
            sp.dma_start(b_bout, b_out_b.partition_broadcast(P)).then_inc(s_w, 16)
            sp.dma_start(mask_s, head_mask).then_inc(s_w, 16)
            sp.dma_start(exp_rows[0:PARTS * EXPERTS, :, :], expert_rows).then_inc(s_w, 16)
        @block.sync
        def _(sp):
            for b in range(BATCH):
                for dst, src in rolled(x, b):
                    sp.dma_start(dst, src).then_inc(s_x, 16)
            sp.dma_start(ident_s[:], ident).then_inc(s_const, 16)
            sp.dma_start(ident_b[:], ident_bf).then_inc(s_const, 16)
            sp.dma_start(causal_s[:], causal).then_inc(s_const, 16)
            for n, w in enumerate((w_q, w_k, w_v, w_proj)):
                sp.dma_start(wa[:, n, :], w).then_inc(s_wa, 16)
            sp.dma_start(bproj_s[:], b_proj.partition_broadcast(P)).then_inc(s_wa, 16)
            for b in range(BATCH):
                sp.dma_start(k_rows[b][PAIR_ROWS:SCORE_ROWS], key_rows).then_inc(s_fixed, 16)
                sp.dma_start(q_rows[b][PAIR_ROWS:MAX_ROWS_FROM].rearrange("r c h t -> r (c h t)"),
                             key_rows[PARTS:2 * PARTS].rearrange("r h t -> r (h t)")).then_inc(s_fixed, 16)
            for b in range(BATCH):
                for half in range(2):
                    cols = slice(half * QCOLS, (half + 1) * QCOLS)
                    sp.wait_ge(s_part3, 4 * b + 2 * half + 1)
                    for n in range(2 * PARTS - 1):
                        sp.dma_start(q_dram[b, half, :, n], part_s[:, 0, half, n % PARTS, :]).then_inc(s_parts_out, 16)
                    sp.wait_ge(s_part3, 4 * b + 2 * half + 2)
                    for n in range(PARTS):
                        sp.dma_start(k_dram[b, :, n, :, cols], part_s[:, 1, half, n, :]).then_inc(s_parts_out, 16)
                sp.wait_ge(s_parts_out, PARTS_OUT * (b + 1))
                for hg in range(GROUPS):
                    u = b * GROUPS + hg
                    hs = slice(hg * GROUP, (hg + 1) * GROUP)
                    for i in range(PARTS):
                        rows = slice(i * PARTS * A_DIM, (i + 1) * PARTS * A_DIM)
                        sp.dma_start(k_rows[b][rows, hs, :], k_dram[b].rearrange("h n d t -> (n d) h t")[:, hs, :])\
                            .then_inc(s_rows[u], 16)
                        for half in range(2):
                            sp.dma_start(q_rows[b][rows, half, hs, :],
                                         q_dram[b, half].rearrange("h n d t -> (n d) h t")
                                         [i * A_DIM:(i + PARTS) * A_DIM, hs, :]).then_inc(s_rows[u], 16)
            for n in range(2 * UNITS):
                u, half = divmod(n, 2)
                b, hg = divmod(u, GROUPS)
                if u > GROUPS and half == 0 and u == GROUPS + 1:
                    load_late(sp)
                sp.wait_ge(s_maxc, n + 1)
                sp.dma_start(q_rows[b][MAX_ROWS_FROM:SCORE_ROWS, half, hg * GROUP:(hg + 1) * GROUP, :]
                             .rearrange("r h (t q) -> r (h t) q", q=P), max_t[:]).then_inc(s_maxd, 16)
            sp.wait_ge(s_added, 3 * QUADS)
            for b in range(BATCH):
                for src, dst in rolled(out, b):
                    sp.dma_start(dst, src).then_inc(s_out, 16)
            sp.wait_ge(s_out, 96)

        W_ALL = 16 * 16

        @block.gpsimd
        def _(pool):
            chain = Chain(pool, s_pool)
            chain.add(nc.gpsimd.memset(minus_half[:], -0.5))
            chain.settle()
            norm_pool(pool, 0)
            norm_pool(pool, 1)
            nc.gpsimd.memset(v_s[:, :, :, A_DIM:VCOLS], 1.0).then_inc(s_ones, 1)
            for n in range(2 * QUADS):
                if n == QUADS:
                    norm_pool(pool, 2)
                    norm_pool(pool, 3)
                pool.wait_ge(s_part2, n + 1)
                p = part_s[:, n % 2, n // 2 % 2]
                nc.gpsimd.tensor_tensor(p[:, 2, :], rest_s[:, n % 2, :], p[:, 1, :], ALU.subtract).then_inc(s_part3, 1)

            def max_parts_of(u, half):
                n = 2 * u + half
                if half:
                    pool.wait_ge(s_joined, u + 1)
                else:
                    pool.wait_ge(s_s1_read, N_ROUNDS * u + HALF_ROUNDS)
                if n:
                    pool.wait_ge(s_maxt, n)
                m = neg_max[:, 0, :, QT * half:QT * half + QT]
                if half:
                    m = max_joined[:]
                chain.add(nc.gpsimd.tensor_copy(max_parts[:, 0], m))
                chain.settle()
                chain.add(nc.gpsimd.tensor_tensor(max_rest[:], m, max_parts[:, 0], ALU.subtract))
                chain.settle()
                chain.add(nc.gpsimd.tensor_copy(max_parts[:, 1], max_rest[:]))
                chain.settle()
                nc.gpsimd.tensor_tensor(max_parts[:, 2], max_rest[:], max_parts[:, 1], ALU.subtract).then_inc(s_maxp, 1)
                pool.wait_ge(s_maxp, n + 1)

            def mask_of(u, s):
                d = len(DIAG) * u + DIAG.index(s)
                pool.wait_ge(s_probs, GROUP * (N_STEPS * u + s + 1))
                tile = probs[:, s % 2, :, 0:P]
                nc.gpsimd.affine_select(out=tile, in_=tile, compare_op=ALU.is_ge, fill=0.0, base=0,
                                        pattern=[[0, GROUP], [1, P]], channel_multiplier=-1).then_inc(s_masked, 1)

            max_parts_of(0, 0)
            for u in range(UNITS):
                for kind, n in PLAN:
                    if kind == "S2" and n % 2 and n // 2 in DIAG:
                        mask_of(u, n // 2)
                    if kind == "MAX":
                        max_parts_of(u, 1)
                    if kind == "MAX_NEXT" and u + 1 < UNITS:
                        max_parts_of(u + 1, 0)

            def expert_items(f_index, items):
                for i in items:
                    k = len(ITEMS) * f_index + i
                    pool.wait_ge(s_gate, k + 1)
                    pool.wait_ge(s_wide_c, k // 2 + 1)
                    if k >= 3:
                        pool.wait_ge(s_down, k - 2)
                    nc.gpsimd.tensor_tensor(hidden[:, k % 3, :], gated[:, k % 2, :], ew_wide[:, (k // 2) % 2, :],
                                            ALU.mult).then_inc(s_hid, 1)

            pool.wait_ge(s_w, W_ALL)
            pool.wait_ge(s_pv, N_STEPS * UNITS)
            chain.add(nc.gpsimd.memset(b_vbd, 0.0))
            chain.add(nc.gpsimd.tensor_scalar(mask_bias, mask_s, b_bin[:, 1:2], None, ALU.mult))
            chain.add(nc.gpsimd.tensor_scalar(b_bout2, b_bout, 2.0, None, ALU.mult))
            chain.settle()
            nc.gpsimd.memset(b_mx, 0.0).then_inc(s_late, 1)

            def moe(g0, r0):
                if g0 == QUADS:
                    norm_pool(pool, g0)
                for c in range(QUADS):
                    expert_items(r0 + c, (0, 1))
                    if c + 1 < QUADS or g0 == QUADS:
                        norm_pool(pool, g0 + c + 1)
                    expert_items(r0 + c, range(2, len(ITEMS)))

            moe(QUADS, 0)
            for kind, n in B_PLAN:
                if kind == "NORM":
                    norm_pool(pool, n)
                if kind == "K_MASK":
                    pool.wait_ge(s_bk1, n + 1)
                    if n >= 2:
                        pool.wait_ge(s_bs, QT * (n - 1))
                    for h in range(K_ON_ACT, B_HEADS):
                        nc.gpsimd.tensor_scalar(bk_s[:, n % 2, h, :], bk1_s, mask_s[:, h:h + 1], None, ALU.mult)\
                            .then_inc(s_bkp, 1)
            moe(3 * QUADS, QUADS)

        @block.scalar
        def _(act):
            def parts_act(n):
                act.wait_ge(s_qk_psum, n + 1)
                if n >= 4:
                    act.wait_ge(s_parts_out, PARTS_OUT)
                p = part_s[:, n % 2, n // 2 % 2]
                nc.scalar.copy(p[:, 0, :], ps[:, n % 2, :]).then_inc(s_part1, 1)

            def parts_act2(n):
                act.wait_ge(s_rest, n + 1)
                nc.scalar.copy(part_s[:, n % 2, n // 2 % 2, 1, :], rest_s[:, n % 2, :]).then_inc(s_part2, 1)

            def v_act(c):
                act.wait_ge(s_v_psum, c + 1)
                nc.scalar.copy(v_s[:, c * QT:(c + 1) * QT, :, 0:A_DIM],
                               ps[:, 2 + c % 2, :].rearrange("p (t h d) -> p t h d", t=QT, h=A_HEADS)).then_inc(s_v, 1)

            for b in range(BATCH):
                for g in (2 * b, 2 * b + 1):
                    norm_copy(act, g)
                for k in range(2):
                    parts_act(4 * b + 2 * k)
                    parts_act(4 * b + 2 * k + 1)
                    parts_act2(4 * b + 2 * k)
                    parts_act2(4 * b + 2 * k + 1)
                    v_act(2 * b + k)

            def max_copy(u, half):
                n = 2 * u + half
                act.wait_ge(s_maxt, n + 1)
                if n:
                    act.wait_ge(s_maxd, 16 * n)
                nc.scalar.copy(max_t[:], max_bank(ps)).then_inc(s_maxc, 1)

            def exps(u, sh):
                s, half = divmod(sh, 2)
                c, j, q, w = STEPS[s]
                k = N_STEPS * u + s
                if k >= 2 and half == 0:
                    act.wait_ge(s_pv, k - 1)
                for h in (2 * half, 2 * half + 1):
                    n = GROUP * k + h
                    act.wait_ge(s_s2, n + 1)
                    nc.scalar.activation(probs[:, s % 2, h, 0:w], ps[:, RING + n % RING, 0:w], ACT.Exp,
                                         scale=A_SCALE).then_inc(s_probs, 1)

            def ctx_copy(u, half):
                n = 2 * u + half
                act.wait_ge(s_pv, N_STEPS * u + LAST_STEP[half] + 1)
                if n:
                    act.wait_ge(s_ctx_t, n)
                nc.scalar.copy(ctx_s[:], ps[:, 6, :]).then_inc(s_ctx_copied, 1)

            def ctx_finish(b):
                for k in range(2):
                    act.wait_ge(s_ctxf_t, 2 * b + k + 1)
                    if b and k == 0:
                        act.wait_ge(s_proj, 2)
                    nc.scalar.copy(ctx_t[:, k * QCOLS:(k + 1) * QCOLS], ps[:, k, :]).then_inc(s_ctxf, 1)
                    if k == 0:
                        nc.scalar.copy(ctx_t[:, TOKENS:TOKENS + ROLL], ps[:, 0, 0:ROLL]).then_inc(s_ctxf, 1)

            max_copy(0, 0)
            for u in range(UNITS):
                for kind, n in PLAN:
                    if kind == "S2":
                        exps(u, n)
                    if kind == "MAX":
                        max_copy(u, 1)
                    if kind == "MAX_NEXT" and u + 1 < UNITS:
                        max_copy(u + 1, 0)
                    if kind == "CTX_COPY":
                        ctx_copy(u, n)
                if u % GROUPS == GROUPS - 1:
                    ctx_finish(u // GROUPS)

            def router_exp(g, r):
                act.wait_ge(s_rshift, r + 1)
                nc.scalar.activation(r_s[5], r_s[4], ACT.Exp).then_inc(s_rexp, 1)

            def ew_copy(r):
                act.wait_ge(s_ew_t, r + 1)
                nc.scalar.copy(ew_rows[0:PARTS * EXPERTS, r % 2, :], ew_bank(ps)[0]).then_inc(s_ew_c, 1)
                nc.scalar.copy(ew_t[0:EXPERTS, r % 2, :], ps[0:EXPERTS, MISC - 1, :]).then_inc(s_ew_c, 1)

            def expert_items(f, pieces):
                for i, (n, half) in enumerate(ITEMS):
                    k = len(ITEMS) * f + i
                    if half == 0:
                        e = k // 2
                        act.wait_ge(s_wide, e + 1)
                        if e >= 2:
                            act.wait_ge(s_hid, 2 * (e - 1))
                        nc.scalar.copy(ew_wide[:, e % 2, :], ps[:, 4, :]).then_inc(s_wide_c, 1)
                    act.wait_ge(s_up, 2 * k + 1)
                    if k >= 2:
                        act.wait_ge(s_gate, k - 1)
                    nc.scalar.activation(silu_s[:, k % 2, :], ps[:, 2 * (k % 2), :], ACT.Silu,
                                         bias=bl1_s[:, n, half:half + 1]).then_inc(s_silu, 1)
                    if i in pieces:
                        pieces[i]()
                act.wait_ge(s_down, len(ITEMS) * (f + 1))
                if f:
                    act.wait_ge(s_y_t, f)
                nc.scalar.copy(y_s, ps[:, 5, :]).then_inc(s_y_c, 1)

            def moe(g0, r0):
                if g0 == QUADS:
                    norm_copy(act, g0)
                router_exp(g0, r0)
                ew_copy(r0)
                for c in range(QUADS):
                    pieces = {}
                    if c + 1 < QUADS:
                        pieces = {3: lambda c=c: norm_copy(act, g0 + c + 1),
                                  6: lambda c=c: router_exp(g0 + c + 1, r0 + c + 1), 10: lambda c=c: ew_copy(r0 + c + 1)}
                    elif g0 == QUADS:
                        pieces = {3: lambda: norm_copy(act, 2 * QUADS)}
                    expert_items(r0 + c, pieces)

            act.wait_ge(s_late, 1)
            moe(QUADS, 0)

            def b_qk(c):
                act.wait_ge(s_bqk, 2 * c + 1)
                if c >= 2:
                    act.wait_ge(s_bs, QT * (c - 1))
                nc.scalar.activation(bq_s[:, c % 2, :], ps[:, 0, :], ACT.Identity, bias=b_bin[:, 0:1]).then_inc(s_bq_c, 1)
                act.wait_ge(s_bqk, 2 * c + 2)
                if c:
                    act.wait_ge(s_bkp, (B_HEADS - K_ON_ACT) * c)
                nc.scalar.activation(bk1_s, ps[:, 1, :], ACT.Identity, bias=b_bin[:, 1:2]).then_inc(s_bk1, 1)

            def b_k_mask(c):
                for h in range(K_ON_ACT):
                    nc.scalar.activation(bk_s[:, c % 2, h, :], ps[:, 1, :], ACT.Identity, bias=mask_bias[:, h:h + 1],
                                         scale=mask_s[:, h:h + 1]).then_inc(s_bk_c, 1)

            def b_exp(p):
                act.wait_ge(s_bshift, p + 1)
                nc.scalar.activation(b_p[:, p % 3], b_p[:, p % 3], ACT.Exp, scale=B_SCALE).then_inc(s_bexp, 1)

            def b_pt_copy(p):
                act.wait_ge(s_bpt, p + 1)
                if p >= 2:
                    act.wait_ge(s_bo, p - 1)
                nc.scalar.copy(b_pt[:, p % 2], ps[:, 4, :].rearrange("p (g q) -> p g q", g=B_PAIRS)).then_inc(s_bpt_c, 1)

            def b_ot_copy(p):
                act.wait_ge(s_bot, p + 1)
                if p >= 2:
                    act.wait_ge(s_by, p - 1)
                nc.scalar.copy(b_ot[:, p % 2, :], ps[:, MISC, 0:P]).then_inc(s_bot_c, 1)

            for kind, n in B_PLAN:
                if kind == "NORM":
                    norm_copy(act, n)
                if kind == "QK":
                    b_qk(n)
                if kind == "K_MASK":
                    b_k_mask(n)
                if kind == "S":
                    b_exp(n)
                if kind == "T":
                    b_pt_copy(n)
                if kind == "O":
                    b_ot_copy(n)
            moe(3 * QUADS, QUADS)

        @block.vector
        def _(dve):
            chain = Chain(dve, s_dve)
            nc.vector.memset(ps[:, 6, :], 0.0).then_inc(s_ctx_clear, 1)
            for b in range(BATCH):
                for g in (2 * b, 2 * b + 1):
                    norm_dve(dve, chain, g)
                for n in range(4 * b, 4 * b + 4):
                    dve.wait_ge(s_part1, n + 1)
                    if n >= 2:
                        dve.wait_ge(s_part3, n - 1)
                    nc.vector.tensor_tensor(rest_s[:, n % 2, :], ps[:, n % 2, :], part_s[:, n % 2, n // 2 % 2, 0, :],
                                            ALU.subtract).then_inc(s_rest, 1)

            def row_max(u, r):
                i, h, kc, w = ROUNDS[r]
                n = N_ROUNDS * u + r
                dve.wait_ge(s_s1, n + 1)
                if u and r == 0:
                    dve.wait_ge(s_maxp, 2 * u)
                nc.vector.tensor_reduce(neg_max[:, kc, h, i:i + 1], ps[:, n % RING, 0:w], AX.X, ALU.max,
                                        negate=True).then_inc(s_s1_read, 1)
                if r == N_ROUNDS - 1:
                    dve.wait_ge(s_s1_read, n + 1)
                    nc.vector.tensor_tensor(max_joined[:], neg_max[:, 0, :, QT:TILES], neg_max[:, 1, :, QT:TILES],
                                            ALU.min).then_inc(s_joined, 1)

            def ctx_norm(u, half):
                n = 2 * u + half
                b, hg = divmod(u, GROUPS)
                dve.wait_ge(s_ctx_t, n + 1)
                v = ps[:, MISC, :].rearrange("p (t g w) -> p t g w", t=QT, g=GROUP)
                chain.settle()
                if n:
                    dve.wait_ge(s_ctx_n, n)
                chain.add(nc.vector.reciprocal(ctx_rec[:], v[:, :, :, A_DIM]))
                chain.settle()
                if u == GROUPS and half == 0:
                    dve.wait_ge(s_ctxf_t, 2)
                dst = ctx_tok[:, half * QT:(half + 1) * QT, hg * GROUP * A_DIM:(hg + 1) * GROUP * A_DIM]
                nc.vector.tensor_tensor(dst.rearrange("p t (g d) -> p t g d", g=GROUP), v[:, :, :, 0:A_DIM],
                                        ctx_rec[:].unsqueeze(3).to_broadcast([P, QT, GROUP, A_DIM]),
                                        ALU.mult).then_inc(s_ctx_n, 1)

            def project(b):
                for k in range(2):
                    c = 2 * b + k
                    dve.wait_ge(s_proj, c + 1)
                    x4 = xs[:, c * QT:(c + 1) * QT, :]
                    chain.settle()
                    nc.vector.tensor_tensor(x4, ps[:, k + 1, :].rearrange("p (t d) -> p t d", t=QT), x4, ALU.add)\
                        .then_inc(s_proj_read, 1)
                    dve.wait_ge(s_proj_read, c + 1)
                    chain.add(nc.vector.tensor_tensor(x4, x4, bproj_s[:].unsqueeze(1).to_broadcast([P, QT, DIM]), ALU.add))

            for r in range(N_ROUNDS):
                row_max(0, r)
            for u in range(UNITS):
                for kind, n in PLAN:
                    if kind == "S1" and u + 1 < UNITS:
                        row_max(u + 1, n)
                    if kind == "CTX":
                        ctx_norm(u, 0)
                    if kind == "CTX_PREV" and u % GROUPS:
                        ctx_norm(u - 1, 1)
                if u % GROUPS == GROUPS - 1:
                    ctx_norm(u, 1)
                    project(u // GROUPS)

            def route(g, r):
                bc = lambda v: v.unsqueeze(2).to_broadcast([P, QT, EXPERTS])
                row = lambda v: v.unsqueeze(1).to_broadcast([P, QT, EXPERTS])
                step = lambda ins: (chain.add(ins), chain.settle())
                dve.wait_ge(s_router, r + 1)
                if r:
                    dve.wait_ge(s_ew_t, r)
                score, biased, t0, sel1, shifted, e, sel2, t1, wts, rest = r_s[:10]
                m1, x1, m2, x2, smax, ssum, srec, vsum, vrec = r_m[:9]
                step(nc.vector.tensor_tensor(score, ps[:, MISC, 0:QT * EXPERTS].rearrange("p (t n) -> p t n", t=QT),
                                             row(br_s), ALU.add))
                step(nc.vector.tensor_reduce(smax, score, AX.X, ALU.max))
                nc.vector.tensor_tensor(shifted, score, bc(smax), ALU.subtract).then_inc(s_rshift, 1)
                step(nc.vector.tensor_tensor(biased, score, row(bias_s), ALU.add))
                step(nc.vector.tensor_reduce(m1, biased, AX.X, ALU.max))
                step(nc.vector.tensor_tensor(t0, biased, bc(m1), ALU.is_equal))
                step(nc.vector.tensor_tensor(t0, t0, row(order_s), ALU.mult))
                step(nc.vector.tensor_reduce(x1, t0, AX.X, ALU.max))
                step(nc.vector.tensor_tensor(sel1, t0, bc(x1), ALU.is_equal))
                step(nc.vector.scalar_tensor_tensor(out=biased, in0=sel1, scalar=NEG_HUGE, in1=biased,
                                                    op0=ALU.mult, op1=ALU.add))
                step(nc.vector.tensor_reduce(m2, biased, AX.X, ALU.max))
                step(nc.vector.tensor_tensor(t1, biased, bc(m2), ALU.is_equal))
                step(nc.vector.tensor_tensor(t1, t1, row(order_s), ALU.mult))
                step(nc.vector.tensor_reduce(x2, t1, AX.X, ALU.max))
                step(nc.vector.tensor_tensor(sel2, t1, bc(x2), ALU.is_equal))
                step(nc.vector.tensor_tensor(sel1, sel1, sel2, ALU.add))
                dve.wait_ge(s_rexp, r + 1)
                step(nc.vector.tensor_reduce(ssum, e, AX.X, ALU.add))
                step(nc.vector.reciprocal(srec, ssum))
                step(nc.vector.tensor_tensor(wts, e, bc(srec), ALU.mult))
                step(nc.vector.tensor_tensor(wts, wts, sel1, ALU.mult))
                step(nc.vector.tensor_reduce(vsum, wts, AX.X, ALU.add))
                step(nc.vector.reciprocal(vrec, vsum))
                step(nc.vector.tensor_tensor(wts, wts, bc(vrec), ALU.mult))
                step(nc.vector.tensor_copy(ew_parts[:, :, 0, :], wts))
                step(nc.vector.tensor_tensor(rest, wts, ew_parts[:, :, 0, :], ALU.subtract))
                step(nc.vector.tensor_copy(ew_parts[:, :, 1, :], rest))
                nc.vector.tensor_tensor(ew_parts[:, :, 2, :], rest, ew_parts[:, :, 1, :], ALU.subtract).then_inc(s_ew, 1)
                dve.wait_ge(s_ew, r + 1)

            def expert_items(f, pieces):
                for i, (n, half) in enumerate(ITEMS):
                    k = len(ITEMS) * f + i
                    dve.wait_ge(s_silu, k + 1)
                    dve.wait_ge(s_up, 2 * k + 2)
                    if k >= 2:
                        dve.wait_ge(s_hid, k - 1)
                    nc.vector.scalar_tensor_tensor(out=gated[:, k % 2, :], in0=ps[:, 2 * (k % 2) + 1, :],
                                                   scalar=bl1_s[:, n, 2 + half:3 + half], in1=silu_s[:, k % 2, :],
                                                   op0=ALU.add, op1=ALU.mult).then_inc(s_gate, 1)
                    if i in pieces:
                        pieces[i]()
                dve.wait_ge(s_y_t, f + 1)
                x4 = xs[:, (f % QUADS) * QT:(f % QUADS + 1) * QT, :]
                chain.settle()
                nc.vector.tensor_tensor(x4, ps[:, 6, :].rearrange("p (t d) -> p t d", t=QT), x4, ALU.add)\
                    .then_inc(s_added, 1)
                dve.wait_ge(s_added, f + 1 + (QUADS if f >= QUADS else 0))

            def moe(g0, r0):
                if g0 == QUADS:
                    norm_dve(dve, chain, g0)
                route(g0, r0)
                for c in range(QUADS):
                    pieces = {}
                    if c + 1 < QUADS:
                        pieces = {1: lambda c=c: norm_dve(dve, chain, g0 + c + 1), 6: lambda c=c: route(g0 + c + 1, r0 + c + 1)}
                    elif g0 == QUADS:
                        pieces = {1: lambda: norm_dve(dve, chain, 2 * QUADS)}
                    expert_items(r0 + c, pieces)

            dve.wait_ge(s_late, 1)
            moe(QUADS, 0)

            def b_v(c):
                for k in range(2):
                    dve.wait_ge(s_bv, 2 * c + k + 1)
                    if c >= 2:
                        dve.wait_ge(s_bo, QT * (c - 1))
                    for e in range(2):
                        lanes = slice(WIN * e, WIN * (e + 1))
                        src = ps[lanes, k, :].rearrange("p (w g e d) -> p w g e d", w=4, g=B_PAIRS, e=2)[:, :, :, e, :]
                        bias = b_bv[lanes, :].rearrange("p (g e d) -> p g e d", g=B_PAIRS, e=2)[:, :, e, :]
                        for w in range(4):
                            nc.vector.tensor_tensor(b_vbd[lanes, c % 2, 4 * k + w, :, e * B_DIM:(e + 1) * B_DIM],
                                                    src[:, w], bias, ALU.add).then_inc(s_bv_c, 1)

            def b_shift(p):
                dve.wait_ge(s_bs, p + 1)
                s = ps[:, 2 + p % 2, :].rearrange("p (h k) -> p h k", h=B_HEADS)
                if p >= 3:
                    dve.wait_ge(s_bpt, p - 2)
                chain.add(nc.vector.tensor_reduce(b_mx[:, p % 2], s, AX.X, ALU.max))
                chain.settle()
                nc.vector.tensor_tensor(b_p[:, p % 3], s, b_mx[:, p % 2].unsqueeze(2).to_broadcast([P, B_HEADS, WIN]),
                                        ALU.subtract).then_inc(s_bshift, 1)

            def b_sums(p):
                dve.wait_ge(s_bexp, p + 1)
                if p >= 4:
                    dve.wait_ge(s_bo_n, p - 3)
                chain.settle()
                chain.add(nc.vector.tensor_reduce(b_sum[:, p % 4], b_p[:, p % 3], AX.X, ALU.add))
                chain.settle()
                chain.add(nc.vector.reciprocal(b_rec[:, p % 4], b_sum[:, p % 4]))
                chain.settle()

            def b_norm(p):
                dve.wait_ge(s_bo, p + 1)
                if p >= 2:
                    dve.wait_ge(s_bot, p - 1)
                nc.vector.tensor_tensor(b_o[:, p % 2, :].rearrange("p (h d) -> p h d", h=B_HEADS),
                                        ps[:, 6, 0:DIM].rearrange("p (h d) -> p h d", h=B_HEADS),
                                        b_rec[:, p % 4].unsqueeze(2).to_broadcast([P, B_HEADS, B_DIM]),
                                        ALU.mult).then_inc(s_bo_n, 1)

            def b_add(c):
                dve.wait_ge(s_by, QT * (c + 1))
                x4 = xs[:, c * QT:(c + 1) * QT, :]
                chain.settle()
                chain.add(nc.vector.scalar_tensor_tensor(out=x4, in0=ps[:, 5, :].rearrange("p (t d) -> p t d", t=QT),
                                                         scalar=2.0, in1=x4, op0=ALU.mult, op1=ALU.add))
                chain.settle()
                nc.vector.tensor_tensor(x4, x4, b_bout2.unsqueeze(1).to_broadcast([P, QT, DIM]), ALU.add)\
                    .then_inc(s_added, 1)
                dve.wait_ge(s_added, QUADS + c + 1)

            for kind, n in B_PLAN:
                if kind == "NORM":
                    norm_dve(dve, chain, n)
                if kind == "V":
                    b_v(n)
                if kind == "S":
                    b_shift(n)
                    if n:
                        b_sums(n - 1)
                if kind == "T" and n == QUADS * QT - 2:
                    b_sums(n + 1)
                if kind == "W":
                    b_norm(n)
                if kind == "Y":
                    b_add(n)
            moe(3 * QUADS, QUADS)

        @block.tensor
        def _(pe):
            pe.wait_ge(s_const, 48)
            pe.wait_ge(s_wa, 80)
            pe.wait_ge(s_ctx_clear, 1)
            for b in range(BATCH):
                for g in (2 * b, 2 * b + 1):
                    if g:
                        pe.wait_ge(s_xt, xt_count(g - 1))
                    norm_pe(pe, g)
                pe.wait_ge(s_xt, xt_count(2 * b + 1))
                for k in range(2):
                    cols = xn_t[:, b, k * QCOLS:(k + 1) * QCOLS]
                    for s in range(2):
                        n = 4 * b + 2 * k + s
                        if n >= 2:
                            pe.wait_ge(s_rest, n - 1)
                        nc.tensor.matmul(ps[:, n % 2, :], wa[:, s, :], cols, start=True, stop=True).then_inc(s_qk_psum, 1)
                    c = 2 * b + k
                    if c >= 2:
                        pe.wait_ge(s_v, c - 1)
                    for t in range(QT):
                        ins = nc.tensor.matmul(ps[:, 2 + c % 2, t * P:(t + 1) * P], cols[:, t * P:(t + 1) * P],
                                               wa[:, 2, :], start=True, stop=True)
                    ins.then_inc(s_v_psum, 1)
            pe.wait_ge(s_v, QUADS)
            pe.wait_ge(s_ones, 1)

            def score_queries(u, r):
                i, h, kc, w = ROUNDS[r]
                b, hg = divmod(u, GROUPS)
                n = N_ROUNDS * u + r
                if r == 0:
                    pe.wait_ge(s_rows[u], 16 * 9)
                    pe.wait_ge(s_fixed, 16 * 2 * BATCH)
                if n >= RING:
                    pe.wait_ge(s_s1_read, n - RING + 1)
                diagonal = kc == i // QT
                ins = nc.tensor.matmul(ps[:, n % RING, 0:w],
                                       q_rows[b][0:MAX_ROWS_FROM, i // QT, hg * GROUP + h, i % QT * P:(i % QT + 1) * P],
                                       k_rows[b][0:MAX_ROWS_FROM, hg * GROUP + h, kc * QCOLS:kc * QCOLS + w],
                                       start=True, stop=not diagonal)
                if diagonal:
                    ins = nc.tensor.matmul(ps[:, n % RING, w - P:w], ident_b[:], causal_s[:], start=False, stop=True)
                ins.then_inc(s_s1, 1)

            def turn_max(u, half):
                n = 2 * u + half
                pe.wait_ge(s_maxp, n + 1)
                if half == 0 and u:
                    pe.wait_ge(s_ctx_n, 2 * (u - 1) + 1)
                if half and u:
                    pe.wait_ge(s_ctx_n, 2 * u)
                if n:
                    pe.wait_ge(s_maxc, n)
                nc.tensor.transpose(max_bank(ps), max_parts[:].rearrange("p a h t -> p (a h t)"), ident_b[:])\
                    .then_inc(s_maxt, 1)

            def score_keys(u, sh):
                s, pair = divmod(sh, 2)
                c, j, q, w = STEPS[s]
                b, hg = divmod(u, GROUPS)
                if sh == 0:
                    pe.wait_ge(s_maxd, 16 * (2 * u + 1))
                if j == 0 and c == 1 and pair == 0:
                    pe.wait_ge(s_maxd, 16 * (2 * u + 2))
                for h in (2 * pair, 2 * pair + 1):
                    n = GROUP * (N_STEPS * u + s) + h
                    if n >= RING:
                        pe.wait_ge(s_probs, n - RING + 1)
                    nc.tensor.matmul(ps[:, RING + n % RING, 0:w], k_rows[b][:, hg * GROUP + h, j * P:(j + 1) * P],
                                     q_rows[b][:, c, hg * GROUP + h, q - c * QCOLS:q - c * QCOLS + w], start=True, stop=True).then_inc(s_s2, 1)

            def weigh_values(u, s):
                c, j, q, w = STEPS[s]
                b, hg = divmod(u, GROUPS)
                pe.wait_ge(s_probs, GROUP * (N_STEPS * u + s + 1))
                if s in DIAG:
                    pe.wait_ge(s_masked, len(DIAG) * u + DIAG.index(s) + 1)
                if j == 0 and (u or c):
                    pe.wait_ge(s_ctx_copied, 2 * u + c)
                for h in range(GROUP):
                    ins = nc.tensor.matmul(ps[32 * h:32 * h + VCOLS, 6, q - c * QCOLS:q - c * QCOLS + w],
                                           v_s[:, b * TILES + j, hg * GROUP + h, :], probs[:, s % 2, h, 0:w],
                                           start=(j == 0), stop=(j == 4 * c + 3))
                ins.then_inc(s_pv, 1)

            def turn_ctx(u, half):
                n = 2 * u + half
                pe.wait_ge(s_ctx_copied, n + 1)
                if n:
                    pe.wait_ge(s_ctx_n, n)
                if half == 0:
                    pe.wait_ge(s_maxc, 2 * u + 2)
                else:
                    pe.wait_ge(s_maxc, min(2 * u + 3, 2 * UNITS))
                for t in range(QT):
                    ins = nc.tensor.transpose(ps[:, MISC, t * P:(t + 1) * P], ctx_s[:, t * P:(t + 1) * P], ident_s[:])
                ins.then_inc(s_ctx_t, 1)

            def finish_batch(b):
                pe.wait_ge(s_ctx_n, 2 * GROUPS * (b + 1))
                pe.wait_ge(s_s1_read, min(N_ROUNDS * (GROUPS * (b + 1) + 1), N_ROUNDS * UNITS))
                for k in range(2):
                    for t in range(QT):
                        ins = nc.tensor.transpose(ps[:, k, t * P:(t + 1) * P], ctx_tok[:, k * QT + t, :], ident_s[:])
                    ins.then_inc(s_ctxf_t, 1)
                pe.wait_ge(s_ctxf, 3 * (b + 1))
                for k in range(2):
                    for t in range(QT):
                        col = ROLL + (k * QT + t) * P
                        ins = nc.tensor.matmul(ps[:, k + 1, t * P:(t + 1) * P], ctx_t[:, col:col + P], wa[:, 3, :],
                                               start=True, stop=True)
                    ins.then_inc(s_proj, 1)
                pe.wait_ge(s_proj_read, 2 * (b + 1))

            for r in range(N_ROUNDS):
                score_queries(0, r)
                if r == HALF_ROUNDS + RING:
                    turn_max(0, 0)
            for u in range(UNITS):
                for kind, n in PLAN:
                    if kind == "S1" and u + 1 < UNITS:
                        score_queries(u + 1, n)
                    if kind == "S2":
                        score_keys(u, n)
                    if kind == "PV":
                        weigh_values(u, n)
                    if kind == "MAX":
                        turn_max(u, 1)
                    if kind == "MAX_NEXT" and u + 1 < UNITS:
                        turn_max(u + 1, 0)
                    if kind == "CTX":
                        turn_ctx(u, 0)
                    if kind == "CTX_PREV" and u % GROUPS:
                        turn_ctx(u - 1, 1)
                if u % GROUPS == GROUPS - 1:
                    turn_ctx(u, 1)
                    finish_batch(u // GROUPS)

            def router(g, r):
                b, col = quad_cols(g % QUADS)
                pe.wait_ge(s_xt, xt_count(g))
                for t in range(QT):
                    ins = nc.tensor.matmul(ps[:, MISC, t * EXPERTS:(t + 1) * EXPERTS],
                                           xn_t[:, b, col + t * P:col + (t + 1) * P], wr_s, start=True, stop=True)
                ins.then_inc(s_router, 1)

            def turn_weights(g, r):
                pe.wait_ge(s_ew, r + 1)
                rows = ew_bank(ps)[0]
                for t in range(QT):
                    nc.tensor.transpose(rows[:, t * P:(t + 1) * P], ew_parts[:, t].rearrange("p q n -> p (q n)"), ident_b[:])
                if r >= QUADS or r % QUADS >= 2:
                    pe.wait_ge(s_added, max(r - 1, QUADS) + QUADS if r >= QUADS else r - 1)
                for t in range(QT):
                    ins = nc.tensor.transpose(ps[0:EXPERTS, MISC - 1, t * P:(t + 1) * P], r_s[8][:, t, :], ident_s[:])
                ins.then_inc(s_ew_t, 1)

            def expert_items(f, pieces):
                b, col = quad_cols(f % QUADS)
                cols = xn_t[:, b, col:col + QCOLS]
                pe.wait_ge(s_ew_c, 2 * (f + 1))

                def down(i):
                    k = len(ITEMS) * f + i
                    n, half = ITEMS[i]
                    pe.wait_ge(s_hid, k + 1)
                    nc.tensor.matmul(ps[:, 5, :], w2_s[:, n, half, :], hidden[:, k % 3, :],
                                     start=False, stop=(i == len(ITEMS) - 1)).then_inc(s_down, 1)

                if f:
                    pe.wait_ge(s_y_c, f)
                nc.tensor.matmul(ps[:, 5, :], bl2_s[0:EXPERTS, :], ew_t[0:EXPERTS, f % 2, :], start=True, stop=False)
                for i, (n, half) in enumerate(ITEMS):
                    k = len(ITEMS) * f + i
                    if half == 0:
                        if k:
                            pe.wait_ge(s_wide_c, k // 2)
                        nc.tensor.matmul(ps[:, 4, :], exp_rows[0:PARTS * EXPERTS, n, :], ew_rows[0:PARTS * EXPERTS, f % 2, :],
                                         start=True, stop=True).then_inc(s_wide, 1)
                    if k >= 2:
                        pe.wait_ge(s_gate, k - 1)
                    for s in range(2):
                        h = s * HID + half * P
                        nc.tensor.matmul(ps[:, 2 * (k % 2) + s, :], w1_s[:, n, h:h + P], cols,
                                         start=True, stop=True).then_inc(s_up, 1)
                    if i >= 2:
                        down(i - 2)
                    if i in pieces:
                        pieces[i]()
                down(len(ITEMS) - 2)
                down(len(ITEMS) - 1)
                pe.wait_ge(s_down, len(ITEMS) * (f + 1))

            def finish_y(f):
                pe.wait_ge(s_y_c, f + 1)
                if f + 1 < 2 * QUADS and f % QUADS < QUADS - 1:
                    pe.wait_ge(s_ew_c, 2 * (f + 2))
                for t in range(QT):
                    ins = nc.tensor.transpose(ps[:, 6, t * P:(t + 1) * P], y_s[:, t * P:(t + 1) * P], ident_s[:])
                ins.then_inc(s_y_t, 1)

            def moe(g0, r0):
                if g0 == QUADS:
                    norm_pe(pe, g0)
                router(g0, r0)
                turn_weights(g0, r0)
                for c in range(QUADS):
                    pieces = {}
                    if c + 1 < QUADS:
                        pieces = {3: lambda c=c: norm_pe_after(pe, g0 + c + 1, r0 + c),
                                  5: lambda c=c: router(g0 + c + 1, r0 + c + 1),
                                  10: lambda c=c: turn_weights(g0 + c + 1, r0 + c + 1)}
                    elif g0 == QUADS:
                        pieces = {3: lambda c=c: norm_pe_after(pe, g0 + c + 1, r0 + c)}
                    expert_items(r0 + c, pieces)
                    finish_y(r0 + c)

            def norm_pe_after(pe, g, r):
                pe.wait_ge(s_ew_c, 2 * (r + 1))
                norm_pe(pe, g)

            pe.wait_ge(s_late, 1)
            moe(QUADS, 0)

            def b_norm_turn(g):
                if turned_o[0]:
                    pe.wait_ge(s_bot_c, turned_o[0])
                norm_pe(pe, g)

            def b_qk(c):
                b, col = quad_cols(c)
                pe.wait_ge(s_xt, xt_count(2 * QUADS + c))
                if c:
                    pe.wait_ge(s_bv_c, 16 * c)
                for s in range(2):
                    nc.tensor.matmul(ps[:, s, :], b_win[:, s * DIM:(s + 1) * DIM], xn_t[:, b, col:col + QCOLS],
                                     start=True, stop=True).then_inc(s_bqk, 1)

            def b_v(c):
                b, col = quad_cols(c)
                for k in range(2):
                    if k == 0:
                        pe.wait_ge(s_bq_c, c + 1)
                    else:
                        pe.wait_ge(s_bk1, c + 1)
                        pe.wait_ge(s_bk_c, K_ON_ACT * (c + 1))
                    for w in range(4):
                        at_col = col + (4 * k + w) * WIN
                        for e in range(2):
                            ins = nc.tensor.matmul(ps[WIN * e:WIN * (e + 1), k, w * P:(w + 1) * P],
                                                   xn_t[:, b, at_col:at_col + WIN], b_win[:, 2 * DIM:3 * DIM],
                                                   start=True, stop=True)
                    ins.then_inc(s_bv, 1)

            def scores(p):
                c, t = divmod(p, QT)
                if t == 0:
                    pe.wait_ge(s_bq_c, c + 1)
                    pe.wait_ge(s_bk_c, K_ON_ACT * (c + 1))
                    pe.wait_ge(s_bkp, (B_HEADS - K_ON_ACT) * (c + 1))
                if p >= 2:
                    pe.wait_ge(s_bshift, p - 1)
                for e in range(2):
                    w = 2 * t + e
                    ins = nc.tensor.matmul(ps[WIN * e:WIN * (e + 1), 2 + p % 2, :],
                                           bq_s[:, c % 2, w * WIN:(w + 1) * WIN],
                                           bk_s[:, c % 2, :, w * WIN:(w + 1) * WIN], start=True, stop=True)
                ins.then_inc(s_bs, 1)

            def turn_probs(p):
                pe.wait_ge(s_bexp, p + 1)
                if p:
                    pe.wait_ge(s_bpt_c, p)
                for g2 in range(B_PAIRS):
                    ins = nc.tensor.transpose(ps[:, 4, g2 * P:(g2 + 1) * P],
                                              b_p[:, p % 3, 2 * g2:2 * g2 + 2, :].rearrange("p h k -> p (h k)"), ident_s[:])
                ins.then_inc(s_bpt, 1)

            def weigh(p):
                c, t = divmod(p, QT)
                pe.wait_ge(s_bpt_c, p + 1)
                pe.wait_ge(s_bv_c, 16 * c + 16)
                if p:
                    pe.wait_ge(s_bo_n, p)
                for g2 in range(B_PAIRS):
                    for e in range(2):
                        ins = nc.tensor.matmul(ps[WIN * e:WIN * (e + 1), 6, g2 * 32:(g2 + 1) * 32],
                                               b_pt[:, p % 2, g2, WIN * e:WIN * (e + 1)], b_vbd[:, c % 2, 2 * t + e, g2, :],
                                               start=True, stop=True)
                ins.then_inc(s_bo, 1)

            def out_proj(p):
                c, t = divmod(p, QT)
                pe.wait_ge(s_bo_n, p + 1)
                if p:
                    pe.wait_ge(s_bot_c, p)
                pe.wait_ge(s_xt, turned_xt[0])
                nc.tensor.transpose(ps[:, MISC, 0:P], b_o[:, p % 2, :], ident_s[:]).then_inc(s_bot, 1)
                turned_o[0] = p + 1
                pe.wait_ge(s_bot_c, p + 1)
                if t == 0:
                    pe.wait_ge(s_added, QUADS + c)
                nc.tensor.matmul(ps[:, 5, t * DIM:(t + 1) * DIM], b_ot[:, p % 2, :], b_wout,
                                 start=True, stop=True).then_inc(s_by, 1)

            turned_o, turned_xt = [0], [xt_count(2 * QUADS)]
            for kind, n in B_PLAN:
                if kind == "NORM":
                    b_norm_turn(n)
                    turned_xt[0] = xt_count(n)
                if kind == "QK":
                    b_qk(n)
                if kind == "V":
                    b_v(n)
                if kind == "S":
                    scores(n)
                if kind == "T":
                    turn_probs(n)
                if kind == "W":
                    weigh(n)
                if kind == "O":
                    out_proj(n)
            moe(3 * QUADS, QUADS)


def max_bank(ps):
    return ps[0:PARTS * GROUP * QT, 7, 0:P // 2].bitcast(BF16)


def ew_bank(ps):
    return ps[0:PARTS * EXPERTS, 7, 0:QCOLS // 2].bitcast(BF16), None


def constants():
    import numpy as np

    def bf(a):
        bits = np.ascontiguousarray(a, np.float32).view(np.uint32)
        return ((bits + 0x7FFF + ((bits >> 16) & 1)) >> 16).astype(np.uint16)

    def split(a):
        parts = []
        for _ in range(PARTS):
            parts.append(bf(a))
            a = a - (parts[-1].astype(np.uint32) << 16).view(np.float32)
        return np.stack(parts)

    slopes = (np.float32(2.0) ** (np.float32(-8.0) * np.arange(1, A_HEADS + 1, dtype=np.float32) / A_HEADS)).astype(np.float32)
    slope_pos = slopes[:, None] * np.arange(TOKENS, dtype=np.float32)[None, :]
    key_rows = np.concatenate([split(slope_pos), bf(np.ones((PARTS, A_HEADS, TOKENS)))])
    causal = bf(np.where(np.arange(P)[None, :] > np.arange(P)[:, None], NEG_BIG, 0.0))
    rows = np.zeros((PARTS, EXPERTS, EXPERTS, P))
    for n in range(EXPERTS):
        rows[:, n, n, :] = 1
    mask = np.zeros((P, B_HEADS), np.float32)
    for h in range(B_HEADS):
        mask[h * B_DIM:(h + 1) * B_DIM, h] = 1
    return {
        "ident": np.eye(P, dtype=np.float32), "ident_bf": bf(np.eye(P)), "causal": causal,
        "key_rows": key_rows, "expert_rows": bf(rows.reshape(PARTS * EXPERTS, EXPERTS, P)), "head_mask": mask,
        "order": np.tile(np.arange(EXPERTS, 0, -1, dtype=np.float32), (P, 1)),
    }


def kernel(**inputs):
    import numpy as np
    import concourse.bacc as bacc
    from concourse.bass_utils import run_bass_kernel_spmd

    a = {k: np.asarray(v) for k, v in inputs.items()}
    bl1 = a["L0_ffn_bl1"]
    arrays = {
        "x": a["L0_attn_a_x"], "w_q": a["L0_attn_a_W_query"], "w_k": a["L0_attn_a_W_key"],
        "w_v": a["L0_attn_a_W_value"], "w_proj": a["L0_attn_a_W_proj"], "b_proj": a["L0_attn_a_b_proj"],
        "b_in_wt": a["L0_attn_b_in_proj_w"].T, "b_in_b": a["L0_attn_b_in_proj_b"],
        "b_in_b_t": a["L0_attn_b_in_proj_b"].reshape(3, P).T,
        "b_out_wt": a["L0_attn_b_out_w"].T, "b_out_b": a["L0_attn_b_out_b"],
        "wr_t": a["L0_ffn_Wr"].T, "br": a["L0_ffn_br"], "wl1": a["L0_ffn_Wl1"],
        "bl1_t": bl1.reshape(EXPERTS, 4, P).transpose(2, 0, 1), "wl2": a["L0_ffn_Wl2"], "bl2": a["L0_ffn_bl2"],
        "biases": a["L0_ffn_biases_N"], **constants(),
    }
    nc = bacc.Bacc("TRN2", target_bir_lowering=False, num_devices=1)
    feed, args = {}, {}
    for name, v in arrays.items():
        v = np.ascontiguousarray(v)
        feed[f"in_{name}"] = v
        ap = nc.dram_tensor(f"in_{name}", v.shape, mybir.dt.from_np(v.dtype), kind="ExternalInput").ap()
        args[name] = ap.bitcast(BF16) if v.dtype == np.uint16 else ap
    out = nc.dram_tensor("out_x", (BATCH, TOKENS, DIM), F32, kind="ExternalOutput").ap()
    build(nc, **args, out=out)
    r = run_bass_kernel_spmd(nc, [feed], core_ids=[0])
    return r.results[0]["out_x"]
```

```python
from contextlib import ExitStack

import concourse.bass as bass
from concourse import mybir

F32 = mybir.dt.float32
BF16 = mybir.dt.bfloat16
F32R = mybir.dt.float32r
ALU = mybir.AluOpType
ACT = mybir.ActivationFunctionType
AX = mybir.AxisListType

P = 128
BATCH, TOKENS, DIM = 2, 1024, 128
ROLL = 32
TILES = TOKENS // P
QUADS = BATCH * 2
QT = 4
QCOLS = QT * P
EPS = 1e-5

A_HEADS, A_DIM = 16, 8
GROUP = 4
GROUPS = A_HEADS // GROUP
UNITS = BATCH * GROUPS
PARTS = 3
PAIR_ROWS = PARTS * PARTS * A_DIM
MAX_ROWS_FROM = PAIR_ROWS + PARTS
SCORE_ROWS = MAX_ROWS_FROM + PARTS
VCOLS = A_DIM + 1
A_SCALE = float(A_DIM) ** -0.5

EXPERTS, HID = 8, 256

B_HEADS, B_DIM, WIN = 8, 16, 64
B_PAIRS = B_HEADS // 2
B_VCOLS = B_DIM + 1
WINS_PER_QUAD = QCOLS // WIN
B_SCALE = float(B_DIM) ** -0.5
NEG_BIG = -1e30
NEG_HUGE = -3e38

STEPS = []
for _c in range(2):
    for _j in range(4 * _c + 4):
        _q = max(P * _j, QCOLS * _c)
        STEPS.append((_c, _j, _q, QCOLS * (_c + 1) - _q))
N_STEPS = len(STEPS)
DIAG = [s for s, (c, j, q, w) in enumerate(STEPS) if q == P * j]
LAST_STEP = [3, N_STEPS - 1]
ROUNDS = []
for _i in range(TILES):
    for _h in range(GROUP):
        for _kc in range(1 + (_i >= QT)):
            ROUNDS.append((_i, _h, _kc, min(QCOLS, P * (_i + 1) - QCOLS * _kc)))
N_ROUNDS = len(ROUNDS)
HALF_ROUNDS = QT * GROUP
RING = 3


PV_AFTER = 3
AHEAD = 3


def stage_plan():
    plan = [("S1", r) for r in range(AHEAD)]
    work = sum(w for _, _, _, w in ROUNDS) / sum(GROUP * w for _, _, _, w in STEPS)
    r, done1, done2 = AHEAD, sum(ROUNDS[r][3] for r in range(AHEAD)), 0
    maxed = turn_in = 0

    def rounds_until(goal):
        nonlocal r, done1
        while r < N_ROUNDS and done1 < goal:
            plan.append(("S1", r))
            done1 += ROUNDS[r][3]
            r += 1

    for s in range(N_STEPS):
        for h in range(GROUP):
            plan.append(("S2", GROUP * s + h))
            done2 += STEPS[s][3]
            if turn_in:
                turn_in -= 1
                if turn_in == 0:
                    plan.append(("MAX_TURN", 0))
            if (s, h) == (0, 3):
                plan.append(("CTX_PREV", 1))
            if (s, h) == (1, 2):
                plan.append(("MAX", 1))
            if h == PV_AFTER and s >= 1:
                plan.append(("PV", s - 1))
                if s - 1 == LAST_STEP[0]:
                    plan.append(("CTX_COPY", 0))
                if s - 1 == LAST_STEP[0] + 1:
                    plan.append(("CTX", 0))
            rounds_until(done2 * work)
        if not maxed and r >= HALF_ROUNDS + RING and s >= 7:
            plan.append(("MAX_NEXT", 0))
            maxed, turn_in = True, 2
    rounds_until(1 << 30)
    plan += [("PV", N_STEPS - 1), ("CTX_COPY", 1)]
    return plan


PLAN = stage_plan()

EARLY = {4: "NORM", 12: "TURN", 16: "ROUTER", 24: "ROUTER_EXP", 38: "WEIGHTS"}

ITEMS = [(n, f) for n in range(EXPERTS) for f in range(2)]


TURN_AT = 6
X_LOW_AT = 7
ROUTE_AT = 8
ROUTE_EXP_AT = 9
WEIGHTS_AT = 14

DOWN_LAG = 3
FINISH_AT = (1, 3, 5, 7)
Y_COPY_AT = DOWN_LAG + 1
Y_TURN_AT = DOWN_LAG + 2
Y_ADD_AT = Y_TURN_AT + 1


K_ACT, K_DVE = range(0, 4), range(4, 8)
FIRST_QK_AT, FIRST_K_AT, FIRST_V_AT = 8, 9, 14
SECOND_NORM_AT = 8


def b_plan():
    plan = []
    pairs = QUADS * QT
    for t in range(pairs + 5):
        c, j = t // QT + 1, t % QT
        if t < pairs:
            plan.append(("S", t))
        for kind, lag in (("T", 2), ("O", 4), ("W", 3), ("Y", 5)):
            if 0 <= t - lag < pairs:
                plan.append((kind, t - lag))
        if t < pairs:
            plan.append(("E", t))
        if t >= 5 and (t - 5) % QT == QT - 1:
            plan.append(("ADD", (t - 5) // QT))
        if c < QUADS:
            plan += [[("NORM", 2 * QUADS + c), ("STEPS", (2 if c + 1 < QUADS else 3) * QUADS + (c + 1) % QUADS)],
                     [("QK", c), ("K_MASK", 2 * c)], [("K_MASK", 2 * c + 1)], [("V", c)]][j]
        plan += {12: [("NORM", 3 * QUADS), ("ROUTER", 0)],
                 14: [("ROUTER_EXP", 0)], 18: [("WEIGHTS", 0)]}.get(t, [])
    return plan


B_PLAN = b_plan()


class Chain:

    def __init__(self, eng, sem):
        self.eng, self.sem, self.n = eng, sem, 0

    def add(self, ins):
        self.n += 1
        return ins.then_inc(self.sem, 1)

    def settle(self):
        if self.n:
            self.eng.wait_ge(self.sem, self.n)


def build(nc, x, w_q, w_k, w_v, w_proj, b_proj, b_in_wt, b_in_b, b_in_b_t, b_out_wt, b_out_b,
          wr_t, br, wl1, bl1_t, wl2, bl2, biases, ident, ident_bf, causal, key_rows,
          head_mask, order, out):
    with ExitStack() as ctx:
        def sb(name, shape, dt=F32):
            return ctx.enter_context(nc.sbuf_tensor(name, shape, dt))

        def sem(name):
            return ctx.enter_context(nc.semaphore(name))

        q_dram = nc.dram_tensor("q_parts", [BATCH, 2, A_HEADS, 2 * PARTS - 1, A_DIM, QCOLS], BF16).ap()
        ew_dram = nc.dram_tensor("expert_weights", [2, EXPERTS, QCOLS], F32).ap()
        k_dram = nc.dram_tensor("k_parts", [BATCH, A_HEADS, PARTS, A_DIM, TOKENS], BF16).ap()

        xs = sb("x_rolled", [P, BATCH * TILES, DIM])
        xn = sb("x_normed", [P, QT, DIM])
        xn_t = sb("x_normed_t", [P, BATCH, TOKENS + ROLL])
        ident_s = sb("ident_s", [P, P])
        ident_b = sb("ident_b", [P, P], BF16)
        causal_s = sb("causal_s", [P, P], BF16)
        wa = sb("attn_a_weights", [P, 4, DIM])
        bproj_s = sb("bproj_s", [P, DIM])
        stats = sb("stats", [P, QT, 6])
        mv = sb("mean_var", [P, QT, 2])
        var_eps = sb("var_eps", [P, QT])
        minus_half = sb("minus_half", [P, QT])
        rstd = sb("rstd", [P, QT])

        v_s = sb("v_ones", [P, BATCH * TILES, A_HEADS, VCOLS])
        neg_max = sb("neg_max", [P, 2, GROUP, TILES])
        max_joined = sb("max_joined", [P, GROUP, QT])
        max_rest = sb("max_rest", [P, GROUP, QT])
        max_parts = sb("max_parts", [P, PARTS, GROUP, QT], BF16)
        max_t = sb("max_t", [PARTS * GROUP * QT, P], BF16)
        ctx_s = sb("ctx_s", [P, QCOLS])
        ctx_rec = sb("ctx_rec", [P, QT, GROUP])
        ctx_tok = sb("ctx_tok", [P, TILES, DIM])
        ctx_t = sb("ctx_t", [P, TOKENS + ROLL])
        b_wout = sb("b_wout", [P, DIM])[:]
        b_bv = sb("b_bv", [P, DIM])[:]
        b_bout = sb("b_bout", [P, DIM])[:]
        bl2_s = sb("bl2_s", [P, DIM])[:]
        mask_s = sb("mask_s", [P, B_HEADS])[:]
        mask_bias = sb("mask_bias", [P, B_HEADS])[:]
        b_win = sb("b_win", [P, 3 * DIM])

        with ExitStack() as early:
            region = early.enter_context(nc.sbuf_tensor("stacked_q_k", [P, BATCH, A_HEADS * TOKENS], F32))
            probs = early.enter_context(nc.sbuf_tensor("probs", [P, 2, GROUP, QCOLS], F32))
            scratch_from = nc.sbuf_bytes_remaining
            scratch = early.enter_context(nc.sbuf_tensor("scratch", [P, 8, QCOLS], F32))
        region_b = region[:].rearrange("p b w -> p (b w)").bitcast(BF16)
        side = A_HEADS * TOKENS
        q_rows = [region_b[0:SCORE_ROWS, (2 * b) * side:(2 * b + 1) * side]
                  .rearrange("r (c h t) -> r c h t", c=2, h=A_HEADS) for b in range(BATCH)]
        k_rows = [region_b[0:SCORE_ROWS, (2 * b + 1) * side:(2 * b + 2) * side].rearrange("r (h t) -> r h t", h=A_HEADS)
                  for b in range(BATCH)]
        part_s = scratch[:, 0:6, :].rearrange("p a q -> p (a q)").bitcast(BF16)\
            .rearrange("p (s c n q) -> p s c n q", s=2, c=2, n=PARTS)
        rest_s = scratch[:, 6:8, :]

        before = nc.sbuf_bytes_remaining
        w1_hi = sb("w1_hi", [P, EXPERTS, 2 * HID], F32R)
        w1_lo = sb("w1_lo", [P, EXPERTS, 2 * HID], F32R)
        w2_hi = sb("w2_hi", [P, EXPERTS, 2, DIM], F32R)
        w2_lo = sb("w2_lo", [P, EXPERTS, 2, DIM], F32R)
        bl1_s = sb("bl1_s", [P, EXPERTS, 4])[:]
        wr_s = sb("wr_s", [P, EXPERTS])[:]
        br_s = sb("br_s", [P, EXPERTS])[:]
        bias_s = sb("bias_s", [P, EXPERTS])[:]
        order_s = sb("order_s", [P, EXPERTS])[:]
        b_bin = sb("b_bin", [P, 3])[:]
        r_s = [sb(f"route_{n}", [P, QT, EXPERTS])[:] for n in range(9)]
        route_sums = sb("route_sums", [P, 9, QT])
        r_m = [route_sums[:, n] for n in range(9)]
        ew_t = sb("ew_t", [EXPERTS, 2, QCOLS])
        xh = sb("xn_t_hi", [P, 2, QCOLS], F32R)
        xl = sb("xn_t_lo", [P, 2, QCOLS], F32R)
        assert before - nc.sbuf_bytes_remaining <= 4 * A_HEADS * TOKENS
        silu_s = sb("silu", [P, 2, QCOLS])[:]
        gated = sb("gated", [P, 2, QCOLS])[:]
        hidden = sb("hidden", [P, 2, QCOLS])[:]
        hid_hi = sb("hidden_hi", [P, 3, QCOLS], F32R)
        hid_lo = sb("hidden_lo", [P, 3, QCOLS], F32R)
        y_s = sb("y_s", [P, QCOLS])[:]
        bq_s = sb("bq_s", [P, 2, QCOLS])[:]
        bk1_s = sb("bk1_s", [P, QCOLS])[:]
        b_vbd = sb("b_vbd", [P, 2, WINS_PER_QUAD, B_PAIRS, 2 * B_VCOLS])[:]
        b_p = sb("b_p", [P, 3, B_HEADS, WIN])[:]
        b_mx = sb("b_mx", [P, 2, B_HEADS])[:]
        b_rec = sb("b_rec", [P, B_HEADS])[:]
        b_pt = sb("b_pt", [P, 2, B_PAIRS, P])[:]
        b_o = sb("b_o", [P, 2, DIM])[:]
        b_ot = sb("b_ot", [P, 2, P])[:]
        wide_1 = sb("wide_or_masked_1", [P, EXPERTS, QCOLS])
        sb("unused", [P, (nc.sbuf_bytes_remaining - scratch_from) // 4])
        wide_0 = sb("wide_or_masked_0", [P, EXPERTS, QCOLS])
        ew_wide = (wide_0, wide_1)
        bk_s = (wide_0, wide_1)

        ps = ctx.enter_context(nc.psum_tensor("ps", [P, 8, QCOLS], F32))
        MISC = 7

        s_x = [sem(f"x_loaded_{c}") for c in range(QUADS)]
        s_const = sem("constants_loaded")
        s_wa = sem("attn_a_weights_loaded")
        s_dve = sem("dve_own")
        s_act = sem("act_own")
        s_pool = sem("pool_own")
        s_var = sem("variance_ready")
        s_std = sem("rstd_ready")
        s_normed = sem("quad_normed")
        s_norm_t = sem("quad_transposed")
        s_xt = sem("xn_t_written")
        s_xt_used = sem("xn_t_used")
        s_qk_psum = sem("qk_in_psum")
        s_part1 = sem("part1_ready")
        s_rest = sem("rest_ready")
        s_part2 = sem("part2_ready")
        s_part3 = sem("part3_ready")
        s_parts_out = [sem(f"parts_stored_{n}") for n in range(2 * BATCH)]
        s_v_psum = sem("v_in_psum")
        s_v = sem("v_ready")
        s_ones = sem("v_ones_set")
        s_rows = [[sem(f"score_rows_loaded_{b}_{n}") for n in ("first_0", "first_1", "rest")] for b in range(BATCH)]
        s_fixed = sem("fixed_rows_loaded")
        s_s1 = sem("round_scored")
        s_s1_read = sem("round_maxed")
        s_joined = sem("chunk_maxima_joined")
        s_maxp = sem("max_parts_ready")
        s_maxt = sem("max_transposed")
        s_maxc = sem("max_rows_copied")
        s_maxd = sem("max_rows_placed")
        s_s2 = sem("step_scored")
        s_probs = sem("exp_done")
        s_masked = sem("diagonal_masked")
        s_pv = sem("pv_done")
        s_ctx_clear = sem("ctx_bank_cleared")
        s_ctx_copied = sem("ctx_copied")
        s_ctx_t = sem("ctx_transposed")
        s_ctx_n = sem("ctx_normalised")
        s_ctxf_t = sem("ctx_tiles_transposed")
        s_ctxf = sem("ctx_t_written")
        s_proj = sem("projection_done")
        s_proj_read = sem("projection_added")
        s_w = sem("late_weights_loaded")
        s_bconst = sem("b_constants_ready")
        s_late = sem("late_constants_ready")
        s_router = sem("router_scores_done")
        s_rshift = sem("router_shifted")
        s_rexp = sem("router_exp_done")
        s_ew = sem("expert_weights_ready")
        s_ew_t = sem("expert_weights_transposed")
        s_ew_c = sem("expert_weights_copied")
        s_up = sem("item_up_done")
        s_silu = sem("item_silu_done")
        s_gate = sem("item_gated")
        s_ew_dram = sem("expert_weights_in_dram")
        s_wide = [[sem(f"expert_weights_spread_{a}_{n}") for n in range(EXPERTS // 2)] for a in range(2)]
        s_hid = sem("item_hidden_ready")
        s_hi = sem("item_hidden_high_part")
        s_lo = sem("item_hidden_low_part")
        s_xh = sem("xn_t_high_part")
        s_xl = sem("xn_t_low_part")
        s_w1 = sem("raw_w1_loaded")
        s_w2 = sem("raw_w2_loaded")
        s_whi = sem("weights_high_part")
        s_wlo = sem("weights_low_part")
        s_down = sem("item_down_done")
        s_y_c = sem("y_copied")
        s_y_t = sem("y_transposed")
        s_added = sem("y_added")
        s_bqk = sem("b_qk_done")
        s_bq_c = sem("b_q_copied")
        s_bk_c = sem("b_k_copied")
        s_bk1 = sem("b_k_biased")
        s_bkd = sem("b_k_masked_by_dve")
        s_bv = sem("b_v_done")
        s_bv_c = sem("b_v_copied")
        s_bs = sem("b_scores_done")
        s_bshift = sem("b_scores_shifted")
        s_bexp = sem("b_exp_done")
        s_bpt = sem("b_probs_transposed")
        s_bpt_c = sem("b_probs_t_copied")
        s_bo = sem("b_pv_done")
        s_bo_n = sem("b_o_normalised")
        s_bot = sem("b_o_transposed")
        s_bot_c = sem("b_o_t_copied")
        s_by = sem("b_y_done")
        s_out = sem("out_stored")

        def rolled(dram, c):
            b, second = divmod(c, 2)
            full = QT - second
            t0, row = c * QT, ROLL + second * QCOLS
            yield xs[:, t0:t0 + full, :], dram[b, row:row + full * P, :].rearrange("(t p) d -> p t d", p=P)
            if second:
                row += full * P
                yield xs[0:P - ROLL, t0 + full, :], dram[b, row:TOKENS, :]
                yield xs[P - ROLL:P, t0 + full, :], dram[b, 0:ROLL, :]

        def quad_cols(c):
            return c // 2, ROLL + (c % 2) * QCOLS

        def y_bank(f):
            return 5 - f % 2

        def b_banks(c):
            return (MISC, 6) if c == 0 else (0, 1)

        def norm_bank(g):
            return 0 if g in (QUADS, 3 * QUADS) else MISC

        def norm_steps(dve, chain, g):
            c = g % QUADS
            if g < QUADS:
                dve.wait_ge(s_x[c], 16 * (1 + 2 * (c % 2)))
            chain.settle()
            for t in range(QT):
                chain.add(nc.vector.bn_stats(stats[:, t, :], xs[:, c * QT + t, :]))
                yield
            chain.settle()
            for t in range(QT):
                chain.add(nc.vector.bn_aggr(mv[:, t, :], stats[:, t, :]))
                yield
            chain.settle()
            if g:
                dve.wait_ge(s_std, g)
            nc.vector.tensor_scalar_add(var_eps[:], mv[:, :, 1], EPS).then_inc(s_var, 1)
            for _ in range(5):
                yield
            dve.wait_ge(s_std, g + 1)
            if g:
                dve.wait_ge(s_norm_t, g)
            for t in range(QT):
                nc.vector.tensor_scalar(xn[:, t, :], xs[:, c * QT + t, :], mv[:, t, 0:1], rstd[:, t:t + 1],
                                        ALU.subtract, ALU.mult).then_inc(s_normed, 1)
                yield

        def norm_dve(dve, chain, g):
            for _ in norm_steps(dve, chain, g):
                pass

        def norm_pool(pool, g):
            pool.wait_ge(s_var, g + 1)
            if g:
                pool.wait_ge(s_normed, QT * g)
            nc.gpsimd.tensor_tensor(rstd[:], var_eps[:], minus_half[:], ALU.pow).then_inc(s_std, 1)

        def norm_pe(pe, g, bank=MISC):
            pe.wait_ge(s_normed, QT * (g + 1))
            for t in range(QT):
                ins = nc.tensor.transpose(ps[:, bank, t * P:(t + 1) * P], xn[:, t, :], ident_s[:])
            ins.then_inc(s_norm_t, 1)

        def norm_copy(act, g, r=None, bank=MISC):
            b, col = quad_cols(g % QUADS)
            act.wait_ge(s_norm_t, g + 1)
            if r is not None:
                if r >= 2:
                    act.wait_ge(s_up, 2 * len(ITEMS) * (r - 1))
                nc.scalar.copy(xh[:, r % 2, :], ps[:, bank, :]).then_inc(s_xh, 1)
            nc.scalar.copy(xn_t[:, b, col:col + QCOLS], ps[:, bank, :]).then_inc(s_xt, 1)
            if g < QUADS and g % 2:
                nc.scalar.copy(xn_t[:, b, 0:ROLL], ps[:, MISC, QCOLS - ROLL:QCOLS]).then_inc(s_xt, 1)

        PARTS_OUT = 16 * (3 * PARTS - 1)

        def xt_count(g):
            return g + 1 + (2 if g >= 3 else 1 if g >= 1 else 0)

        block = ctx.enter_context(nc.Block())

        def load_late(sp):
            sp.wait_ge(s_pv, N_STEPS * GROUPS)
            sp.dma_start(scratch[:], wl1.rearrange("n d h -> d n h")).then_inc(s_w1, 16)
            sp.dma_start(bl1_s, bl1_t).then_inc(s_w, 16)
            sp.dma_start(bl2_s[0:EXPERTS, :], bl2).then_inc(s_w, 16)
            sp.dma_start(wr_s, wr_t).then_inc(s_w, 16)
            sp.dma_start(br_s, br.partition_broadcast(P)).then_inc(s_w, 16)
            sp.dma_start(bias_s, biases.partition_broadcast(P)).then_inc(s_w, 16)
            sp.dma_start(order_s, order).then_inc(s_w, 16)
            sp.dma_start(b_win[:], b_in_wt).then_inc(s_w, 16)
            sp.dma_start(b_wout, b_out_wt).then_inc(s_w, 16)
            sp.dma_start(b_bin, b_in_b_t).then_inc(s_w, 16)
            sp.dma_start(b_bv, b_in_b[2 * DIM:3 * DIM].partition_broadcast(P)).then_inc(s_w, 16)
            sp.dma_start(b_bout, b_out_b.partition_broadcast(P)).then_inc(s_w, 16)
            sp.dma_start(mask_s, head_mask).then_inc(s_w, 16)

        def load_w2(sp):
            sp.wait_ge(s_wlo, 4)
            for f in range(2):
                sp.dma_start(scratch[:, 0:4, :].rearrange("p a (n f d) -> p (a n) f d", n=2, f=2)[:, :, f, :],
                             wl2[:, f * P:(f + 1) * P, :].rearrange("n h d -> h n d")).then_inc(s_w2, 16)

        W_PIECES = EXPERTS + EXPERTS // 2

        def w_piece(m):
            if m < EXPERTS:
                return scratch[:, m, :], w1_hi[:, m, :], w1_lo[:, m, :]
            e = slice(2 * (m - EXPERTS), 2 * (m - EXPERTS) + 2)
            raw = scratch[:, m - EXPERTS, :].rearrange("p (n f d) -> p n f d", n=2, f=2)
            return raw, w2_hi[:, e], w2_lo[:, e]

        def w_piece_at(u, sh):
            s, h = divmod(sh, GROUP)
            plain = [t for t in range(N_STEPS) if t not in DIAG]
            if u > GROUPS and h == 1 and s in plain:
                m = (u - GROUPS - 1) * len(plain) + plain.index(s)
                return m if m < W_PIECES else None
            return None

        @block.sync
        def _(sp):
            def load_x(c):
                for dst, src in rolled(x, c):
                    sp.dma_start(dst, src).then_inc(s_x[c], 16)

            load_x(0)
            sp.dma_start(ident_s[:], ident).then_inc(s_const, 16)
            load_x(1)
            for n, w in enumerate((w_q, w_k, w_v, w_proj)):
                sp.dma_start(wa[:, n, :], w).then_inc(s_wa, 16)
            sp.dma_start(ident_b[:], ident_bf).then_inc(s_const, 16)
            sp.dma_start(causal_s[:], causal).then_inc(s_const, 16)
            sp.dma_start(bproj_s[:], b_proj.partition_broadcast(P)).then_inc(s_wa, 16)
            load_x(2)
            load_x(3)
            for b in range(BATCH):
                sp.dma_start(k_rows[b][PAIR_ROWS:SCORE_ROWS], key_rows).then_inc(s_fixed, 16)
                sp.dma_start(q_rows[b][PAIR_ROWS:MAX_ROWS_FROM].rearrange("r c h t -> r (c h t)"),
                             key_rows[PARTS:2 * PARTS].rearrange("r h t -> r (h t)")).then_inc(s_fixed, 16)
            def store_q(b, half):
                sp.wait_ge(s_part3, 4 * b + 2 * half + 1)
                for n in range(2 * PARTS - 1):
                    sp.dma_start(q_dram[b, half, :, n], part_s[:, 0, half, n % PARTS, :])\
                        .then_inc(s_parts_out[2 * b + half], 16)

            def store_k(b, half):
                sp.wait_ge(s_part3, 4 * b + 2 * half + 2)
                for n in range(PARTS):
                    sp.dma_start(k_dram[b, :, n, :, half * QCOLS:(half + 1) * QCOLS], part_s[:, 1, half, n, :])\
                        .then_inc(s_parts_out[2 * b + half], 16)

            def load_rows(b, hs, halves, loaded):
                for half in halves:
                    sp.wait_ge(s_parts_out[2 * b + half], PARTS_OUT)
                cols = slice(halves[0] * QCOLS, (halves[-1] + 1) * QCOLS)
                for i in range(PARTS):
                    rows = slice(i * PARTS * A_DIM, (i + 1) * PARTS * A_DIM)
                    sp.dma_start(k_rows[b][rows, hs, cols], k_dram[b].rearrange("h n d t -> (n d) h t")[:, hs, cols])\
                        .then_inc(loaded, 16)
                    for half in halves:
                        sp.dma_start(q_rows[b][rows, half, hs, :],
                                     q_dram[b, half].rearrange("h n d t -> (n d) h t")
                                     [i * A_DIM:(i + PARTS) * A_DIM, hs, :]).then_inc(loaded, 16)

            first, rest = slice(0, GROUP), slice(GROUP, A_HEADS)
            store_q(0, 0)
            store_k(0, 0)
            store_q(0, 1)
            load_rows(0, first, [0], s_rows[0][0])
            store_k(0, 1)
            load_rows(0, first, [1], s_rows[0][1])
            load_rows(0, rest, [0, 1], s_rows[0][2])
            for half in range(2):
                store_q(1, half)
                store_k(1, half)
            for n in range(2 * UNITS):
                u, half = divmod(n, 2)
                b, hg = divmod(u, GROUPS)
                if n == 2:
                    load_rows(1, first, [0], s_rows[1][0])
                    load_rows(1, first, [1], s_rows[1][1])
                    load_rows(1, rest, [0, 1], s_rows[1][2])
                if n == 2 * (GROUPS + 1):
                    load_late(sp)
                if n == 2 * (GROUPS + 3):
                    load_w2(sp)
                sp.wait_ge(s_maxc, n + 1)
                sp.dma_start(q_rows[b][MAX_ROWS_FROM:SCORE_ROWS, half, hg * GROUP:(hg + 1) * GROUP, :]
                             .rearrange("r h (t q) -> r (h t) q", q=P), max_t[:]).then_inc(s_maxd, 16)
            for r in range(2 * QUADS):
                sp.wait_ge(s_ew_c, r + 1)
                sp.dma_start(ew_dram[r % 2], ew_t[:, r % 2, :]).then_inc(s_ew_dram, 16)
                if r == 0:
                    sp.wait_ge(s_wlo, W_PIECES)
                if r == 1:
                    sp.wait_ge(s_pv, N_STEPS * UNITS)
                if r >= 2:
                    sp.wait_ge(s_hid, len(ITEMS) * (r - 1))
                if r >= QUADS:
                    sp.wait_ge(s_bs, QT * min(r - 1, QUADS))
                sp.wait_ge(s_ew_dram, 16 * (r + 1))
                for n in range(EXPERTS // 2):
                    e = slice(2 * n, 2 * n + 2)
                    sp.dma_start(ew_wide[r % 2][:, e, :], ew_dram[r % 2, e].partition_broadcast(P))\
                        .then_inc(s_wide[r % 2][n], 16)
            for c in range(QUADS):
                sp.wait_ge(s_added, 2 * QUADS + c + 1)
                for src, dst in rolled(out, c):
                    sp.dma_start(dst, src).then_inc(s_out, 16)
            sp.wait_ge(s_out, 16 * 8)

        W_ALL = 16 * 12

        @block.gpsimd
        def _(pool):
            chain = Chain(pool, s_pool)
            chain.add(nc.gpsimd.memset(minus_half[:], -0.5))
            chain.settle()
            norm_pool(pool, 0)
            norm_pool(pool, 1)
            nc.gpsimd.memset(v_s[:, :, :, A_DIM:VCOLS], 1.0).then_inc(s_ones, 1)
            for n in range(2 * QUADS):
                if n == QUADS:
                    norm_pool(pool, 2)
                    norm_pool(pool, 3)
                pool.wait_ge(s_part2, n + 1)
                p = part_s[:, n % 2, n // 2 % 2]
                nc.gpsimd.tensor_tensor(p[:, 2, :], rest_s[:, n % 2, :], p[:, 1, :], ALU.subtract).then_inc(s_part3, 1)

            def max_parts_of(u, half):
                n = 2 * u + half
                if half:
                    pool.wait_ge(s_joined, u + 1)
                else:
                    pool.wait_ge(s_s1_read, N_ROUNDS * u + HALF_ROUNDS)
                if n:
                    pool.wait_ge(s_maxt, n)
                m = neg_max[:, 0, :, QT * half:QT * half + QT]
                if half:
                    m = max_joined[:]
                chain.add(nc.gpsimd.tensor_copy(max_parts[:, 0], m))
                chain.settle()
                chain.add(nc.gpsimd.tensor_tensor(max_rest[:], m, max_parts[:, 0], ALU.subtract))
                chain.settle()
                chain.add(nc.gpsimd.tensor_copy(max_parts[:, 1], max_rest[:]))
                chain.settle()
                nc.gpsimd.tensor_tensor(max_parts[:, 2], max_rest[:], max_parts[:, 1], ALU.subtract).then_inc(s_maxp, 1)
                pool.wait_ge(s_maxp, n + 1)

            def mask_of(u, s):
                d = len(DIAG) * u + DIAG.index(s)
                pool.wait_ge(s_probs, GROUP * (N_STEPS * u + s + 1))
                tile = probs[:, s % 2, :, 0:P]
                nc.gpsimd.affine_select(out=tile, in_=tile, compare_op=ALU.is_ge, fill=0.0, base=0,
                                        pattern=[[0, GROUP], [1, P]], channel_multiplier=-1).then_inc(s_masked, 1)

            max_parts_of(0, 0)
            for u in range(UNITS):
                max_parts_of(u, 1)
                for kind, n in PLAN:
                    if kind == "S2" and n % GROUP == GROUP - 1 and n // GROUP in DIAG:
                        mask_of(u, n // GROUP)
                    if kind == "S2" and u == UNITS - 1 and EARLY.get(n) == "NORM":
                        norm_pool(pool, QUADS)
                    if kind == "S2" and w_piece_at(u, n) is not None:
                        m = w_piece_at(u, n)
                        raw, hi, lo = w_piece(m)
                        pool.wait_ge(s_whi, m + 1)
                        nc.gpsimd.tensor_tensor(lo, raw, hi.bitcast(F32), ALU.subtract).then_inc(s_wlo, 1)
                    if kind == "MAX_NEXT" and u + 1 < UNITS:
                        max_parts_of(u + 1, 0)

            def expert_items(f_index, items):
                for i in items:
                    k = len(ITEMS) * f_index + i
                    pool.wait_ge(s_gate, k + 1)
                    pool.wait_ge(s_wide[f_index % 2][i // 4], 16 * (f_index // 2 + 1))
                    if k >= 2:
                        pool.wait_ge(s_lo, k - 1)
                    nc.gpsimd.tensor_tensor(hidden[:, k % 2, :], gated[:, k % 2, :], ew_wide[f_index % 2][:, i // 2, :],
                                            ALU.mult).then_inc(s_hid, 1)

            pool.wait_ge(s_w, W_ALL)
            pool.wait_ge(s_wlo, W_PIECES)
            pool.wait_ge(s_pv, N_STEPS * UNITS)
            nc.gpsimd.memset(b_mx, 0.0).then_inc(s_late, 1)

            def b_constants():
                chain.add(nc.gpsimd.memset(b_vbd, 0.0))
                for e in range(2):
                    chain.settle()
                    chain.add(nc.gpsimd.memset(b_vbd[WIN * e:WIN * (e + 1), :, :, :, e * B_VCOLS + B_DIM], 1.0))
                chain.settle()
                chain.add(nc.gpsimd.tensor_scalar(mask_bias, mask_s, b_bin[:, 1:2], None, ALU.mult))
                chain.settle()
                nc.gpsimd.tensor_scalar(b_bout, b_bout, 2.0, None, ALU.mult).then_inc(s_bconst, 1)
                pool.wait_ge(s_bconst, 1)

            def moe(g0, r0):
                for c in range(QUADS):
                    if r0 + c == 1:
                        b_constants()
                    expert_items(r0 + c, (0, 1))
                    if c + 1 < QUADS or g0 == QUADS:
                        norm_pool(pool, g0 + c + 1)
                    last = c + 1 == QUADS and g0 == QUADS
                    some = SECOND_NORM_AT + 2 if last else len(ITEMS)
                    expert_items(r0 + c, range(2, some))
                    if last:
                        norm_pool(pool, g0 + c + 2)
                    expert_items(r0 + c, range(some, len(ITEMS)))

            moe(QUADS, 0)
            for kind, n in B_PLAN:
                if kind == "STEPS":
                    norm_pool(pool, n)
            moe(3 * QUADS, QUADS)

        @block.scalar
        def _(act):
            def parts_act(n):
                act.wait_ge(s_qk_psum, n + 1)
                if n >= 4:
                    act.wait_ge(s_parts_out[n // 2 % 2], PARTS_OUT)
                p = part_s[:, n % 2, n // 2 % 2]
                nc.scalar.copy(p[:, 0, :], ps[:, n % 2, :]).then_inc(s_part1, 1)

            def parts_act2(n):
                act.wait_ge(s_rest, n + 1)
                nc.scalar.copy(part_s[:, n % 2, n // 2 % 2, 1, :], rest_s[:, n % 2, :]).then_inc(s_part2, 1)

            def v_act(c):
                act.wait_ge(s_v_psum, c + 1)
                nc.scalar.copy(v_s[:, c * QT:(c + 1) * QT, :, 0:A_DIM],
                               ps[:, 2 + c % 2, :].rearrange("p (t h d) -> p t h d", t=QT, h=A_HEADS)).then_inc(s_v, 1)

            for b in range(BATCH):
                for g in (2 * b, 2 * b + 1):
                    norm_copy(act, g)
                for k in range(2):
                    parts_act(4 * b + 2 * k)
                    parts_act(4 * b + 2 * k + 1)
                    parts_act2(4 * b + 2 * k)
                    parts_act2(4 * b + 2 * k + 1)
                    v_act(2 * b + k)

            def max_copy(u, half):
                n = 2 * u + half
                act.wait_ge(s_maxt, n + 1)
                if n:
                    act.wait_ge(s_maxd, 16 * n)
                nc.scalar.copy(max_t[:], max_bank(ps)).then_inc(s_maxc, 1)

            def exps(u, sh):
                s, h = divmod(sh, GROUP)
                c, j, q, w = STEPS[s]
                k = N_STEPS * u + s
                if k >= 2 and h == 0:
                    act.wait_ge(s_pv, k - 1)
                n = GROUP * k + h
                act.wait_ge(s_s2, n + 1)
                nc.scalar.activation(probs[:, s % 2, h, 0:w], ps[:, RING + n % RING, 0:w], ACT.Exp,
                                     scale=A_SCALE).then_inc(s_probs, 1)

            def ctx_copy(u, half):
                n = 2 * u + half
                act.wait_ge(s_pv, N_STEPS * u + LAST_STEP[half] + 1)
                if n:
                    act.wait_ge(s_ctx_t, n)
                nc.scalar.copy(ctx_s[:], ps[:, 6, :]).then_inc(s_ctx_copied, 1)

            def ctx_finish(b, halves=(0, 1)):
                for k in halves:
                    act.wait_ge(s_ctxf_t, 2 * b + k + 1)
                    if b and k == 0:
                        act.wait_ge(s_proj, 2)
                    bank = k if b == 0 else 6
                    nc.scalar.copy(ctx_t[:, k * QCOLS:(k + 1) * QCOLS], ps[:, bank, :]).then_inc(s_ctxf, 1)
                    if k == 0:
                        nc.scalar.copy(ctx_t[:, TOKENS:TOKENS + ROLL], ps[:, bank, 0:ROLL]).then_inc(s_ctxf, 1)

            def router_exp(g, r):
                act.wait_ge(s_rshift, r + 1)
                nc.scalar.activation(r_s[5], r_s[4], ACT.Exp).then_inc(s_rexp, 1)

            def ew_copy(r, bank=6):
                act.wait_ge(s_ew_t, r + 1)
                if r >= 2:
                    act.wait_ge(s_ew_dram, 16 * (r - 1))
                    act.wait_ge(s_down, len(ITEMS) * (r - 2) + 1)
                nc.scalar.copy(ew_t[0:EXPERTS, r % 2, :], ps[0:EXPERTS, bank, :]).then_inc(s_ew_c, 1)

            max_copy(0, 0)
            for u in range(UNITS):
                for kind, n in PLAN:
                    if kind == "S2":
                        exps(u, n)
                        m = w_piece_at(u, n)
                        if m is not None:
                            if m < EXPERTS:
                                act.wait_ge(s_w1, 16)
                            else:
                                act.wait_ge(s_w2, 32)
                            raw, hi, _ = w_piece(m)
                            nc.scalar.copy(hi, raw).then_inc(s_whi, 1)
                        early = EARLY.get(n) if u == UNITS - 1 else None
                        if early == "TURN":
                            norm_copy(act, QUADS, 0, 0)
                        if early == "ROUTER_EXP":
                            router_exp(QUADS, 0)
                        if early == "WEIGHTS":
                            ew_copy(0, 1)
                    if kind == "MAX":
                        max_copy(u, 1)
                    if kind == "MAX_TURN" and u + 1 < UNITS:
                        max_copy(u + 1, 0)
                    if kind == "CTX_COPY":
                        ctx_copy(u, n)
                if u == GROUPS - 1:
                    ctx_finish(0)

            def b_q_copy(c):
                act.wait_ge(s_bqk, 2 * c + 1)
                if c >= 2:
                    act.wait_ge(s_bs, QT * (c - 1))
                nc.scalar.activation(bq_s[:, c % 2, :], ps[:, b_banks(c)[0], :], ACT.Identity, bias=b_bin[:, 0:1])\
                    .then_inc(s_bq_c, 1)

            def b_k_copy(c):
                act.wait_ge(s_bqk, 2 * c + 2)
                if c:
                    act.wait_ge(s_bkd, len(K_DVE) * c)
                nc.scalar.activation(bk1_s, ps[:, b_banks(c)[1], :], ACT.Identity, bias=b_bin[:, 1:2]).then_inc(s_bk1, 1)

            def b_k_mask(c, heads):
                act.wait_ge(s_bconst, 1)
                if c < 2:
                    act.wait_ge(s_hid, len(ITEMS) * (QUADS - 1 + c))
                for h in heads:
                    nc.scalar.activation(bk_s[c % 2][:, h, :], ps[:, b_banks(c)[1], :], ACT.Identity,
                                         bias=mask_bias[:, h:h + 1], scale=mask_s[:, h:h + 1]).then_inc(s_bk_c, 1)

            def high(k):
                act.wait_ge(s_hid, k + 1)
                if k >= 3:
                    act.wait_ge(s_down, k - 2)
                nc.scalar.copy(hid_hi[:, k % 3, :], hidden[:, k % 2, :]).then_inc(s_hi, 1)

            def expert_items(f, pieces):
                for i, (n, half) in enumerate(ITEMS):
                    k = len(ITEMS) * f + i
                    if i == Y_COPY_AT and f % QUADS:
                        y_copy(f - 1)
                    act.wait_ge(s_up, 2 * k + 1)
                    if k >= 2:
                        act.wait_ge(s_gate, k - 1)
                    nc.scalar.activation(silu_s[:, k % 2, :], ps[:, 2 * (k % 2), :], ACT.Silu,
                                         bias=bl1_s[:, n, half:half + 1]).then_inc(s_silu, 1)
                    if i or f % QUADS:
                        high(k - 1)
                    if i in pieces:
                        pieces[i]()

            def y_copy(f):
                act.wait_ge(s_down, len(ITEMS) * (f + 1))
                if f:
                    act.wait_ge(s_y_t, f)
                nc.scalar.copy(y_s, ps[:, y_bank(f), :]).then_inc(s_y_c, 1)

            def moe(g0, r0):
                for c in range(QUADS):
                    pieces = {}
                    if c + 1 < QUADS:
                        pieces = {TURN_AT: lambda c=c: norm_copy(act, g0 + c + 1, r0 + c + 1),
                                  ROUTE_EXP_AT: lambda c=c: router_exp(g0 + c + 1, r0 + c + 1),
                                  WEIGHTS_AT: lambda c=c: ew_copy(r0 + c + 1)}
                    elif g0 == QUADS:
                        pieces = {TURN_AT: lambda: norm_copy(act, 2 * QUADS), FIRST_QK_AT: lambda: b_q_copy(0),
                                  FIRST_K_AT: lambda: b_k_copy(0)}
                        for h in K_ACT:
                            pieces[FIRST_K_AT + 1 + h] = lambda h=h: b_k_mask(0, [h])
                    if r0 + c == 0:
                        pieces[FINISH_AT[0]] = lambda: ctx_finish(1, (0,))
                        pieces[FINISH_AT[1]] = lambda: ctx_finish(1, (1,))
                    expert_items(r0 + c, pieces)
                high(len(ITEMS) * (r0 + QUADS) - 1)
                y_copy(r0 + QUADS - 1)

            act.wait_ge(s_late, 1)
            moe(QUADS, 0)

            def b_exp(p):
                act.wait_ge(s_bshift, p + 1)
                nc.scalar.activation(b_p[:, p % 3], b_p[:, p % 3], ACT.Exp, scale=B_SCALE).then_inc(s_bexp, 1)

            def b_pt_copy(p):
                act.wait_ge(s_bpt, p + 1)
                if p >= 2:
                    act.wait_ge(s_bo, p - 1)
                nc.scalar.copy(b_pt[:, p % 2], ps[:, 4, :].rearrange("p (g q) -> p g q", g=B_PAIRS)).then_inc(s_bpt_c, 1)

            def b_ot_copy(p):
                act.wait_ge(s_bot, p + 1)
                if p >= 2:
                    act.wait_ge(s_by, p - 1)
                nc.scalar.copy(b_ot[:, p % 2, :], ps[:, MISC, 0:P]).then_inc(s_bot_c, 1)

            for kind, n in B_PLAN:
                if kind == "NORM":
                    norm_copy(act, n, QUADS if n == 3 * QUADS else None, norm_bank(n))
                if kind == "QK":
                    b_q_copy(n)
                    b_k_copy(n)
                if kind == "K_MASK":
                    b_k_mask(n // 2, K_ACT[2 * (n % 2):2 * (n % 2) + 2])
                if kind == "E":
                    b_exp(n)
                if kind == "T":
                    b_pt_copy(n)
                if kind == "O":
                    b_ot_copy(n)
                if kind == "ROUTER_EXP":
                    router_exp(3 * QUADS, QUADS)
                if kind == "WEIGHTS":
                    ew_copy(QUADS, 1)
            moe(3 * QUADS, QUADS)

        @block.vector
        def _(dve):
            chain = Chain(dve, s_dve)
            nc.vector.memset(ps[:, 6, :], 0.0).then_inc(s_ctx_clear, 1)
            for b in range(BATCH):
                for g in (2 * b, 2 * b + 1):
                    norm_dve(dve, chain, g)
                for n in range(4 * b, 4 * b + 4):
                    dve.wait_ge(s_part1, n + 1)
                    if n >= 2:
                        dve.wait_ge(s_part3, n - 1)
                    nc.vector.tensor_tensor(rest_s[:, n % 2, :], ps[:, n % 2, :], part_s[:, n % 2, n // 2 % 2, 0, :],
                                            ALU.subtract).then_inc(s_rest, 1)

            def row_max(u, r):
                i, h, kc, w = ROUNDS[r]
                n = N_ROUNDS * u + r
                dve.wait_ge(s_s1, n + 1)
                if u and r == 0:
                    dve.wait_ge(s_maxp, 2 * u)
                nc.vector.tensor_reduce(neg_max[:, kc, h, i:i + 1], ps[:, n % RING, 0:w], AX.X, ALU.max,
                                        negate=True).then_inc(s_s1_read, 1)
                if r == N_ROUNDS - 1:
                    dve.wait_ge(s_s1_read, n + 1)
                    nc.vector.tensor_tensor(max_joined[:], neg_max[:, 0, :, QT:TILES], neg_max[:, 1, :, QT:TILES],
                                            ALU.min).then_inc(s_joined, 1)

            def ctx_norm(u, half):
                n = 2 * u + half
                b, hg = divmod(u, GROUPS)
                dve.wait_ge(s_ctx_t, n + 1)
                v = ps[:, MISC, :].rearrange("p (t g w) -> p t g w", t=QT, g=GROUP)
                chain.settle()
                if n:
                    dve.wait_ge(s_ctx_n, n)
                chain.add(nc.vector.reciprocal(ctx_rec[:], v[:, :, :, A_DIM]))
                chain.settle()
                if u == GROUPS and half == 0:
                    dve.wait_ge(s_ctxf_t, 2)
                dst = ctx_tok[:, half * QT:(half + 1) * QT, hg * GROUP * A_DIM:(hg + 1) * GROUP * A_DIM]
                nc.vector.tensor_tensor(dst.rearrange("p t (g d) -> p t g d", g=GROUP), v[:, :, :, 0:A_DIM],
                                        ctx_rec[:].unsqueeze(3).to_broadcast([P, QT, GROUP, A_DIM]),
                                        ALU.mult).then_inc(s_ctx_n, 1)

            def project(b, halves=(0, 1)):
                for k in halves:
                    c = 2 * b + k
                    dve.wait_ge(s_proj, c + 1)
                    x4 = xs[:, c * QT:(c + 1) * QT, :]
                    chain.settle()
                    nc.vector.tensor_tensor(x4, ps[:, k + 1 if b == 0 else 6, :].rearrange("p (t d) -> p t d", t=QT), x4, ALU.add)\
                        .then_inc(s_proj_read, 1)
                    dve.wait_ge(s_proj_read, c + 1)
                    chain.add(nc.vector.tensor_tensor(x4, x4, bproj_s[:].unsqueeze(1).to_broadcast([P, QT, DIM]), ALU.add))

            def x_low_steps(g, r):
                b, col = quad_cols(g % QUADS)
                dve.wait_ge(s_xt, xt_count(g))
                dve.wait_ge(s_xh, r + 1)
                if r >= 2:
                    dve.wait_ge(s_up, 2 * len(ITEMS) * (r - 1))
                nc.vector.tensor_tensor(xl[:, r % 2, :], xn_t[:, b, col:col + QCOLS], xh[:, r % 2, :].bitcast(F32),
                                        ALU.subtract).then_inc(s_xl, 1)
                yield

            def route_steps(g, r, bank=MISC):
                bc = lambda v: v.unsqueeze(2).to_broadcast([P, QT, EXPERTS])
                row = lambda v: v.unsqueeze(1).to_broadcast([P, QT, EXPERTS])
                dve.wait_ge(s_router, r + 1)
                if r:
                    dve.wait_ge(s_ew_t, r)
                score, biased, t0, sel1, shifted, e, sel2, t1, wts = r_s[:9]
                m1, x1, m2, x2, smax, ssum, srec, vsum, vrec = r_m[:9]
                chain.settle()
                chain.add(nc.vector.tensor_tensor(score, ps[:, bank, 0:QT * EXPERTS].rearrange("p (t n) -> p t n", t=QT),
                                             row(br_s), ALU.add))
                yield
                chain.settle()
                chain.add(nc.vector.tensor_reduce(smax, score, AX.X, ALU.max))
                yield
                chain.settle()
                nc.vector.tensor_tensor(shifted, score, bc(smax), ALU.subtract).then_inc(s_rshift, 1)
                yield
                chain.settle()
                chain.add(nc.vector.tensor_tensor(biased, score, row(bias_s), ALU.add))
                yield
                chain.settle()
                chain.add(nc.vector.tensor_reduce(m1, biased, AX.X, ALU.max))
                yield
                chain.settle()
                chain.add(nc.vector.tensor_tensor(t0, biased, bc(m1), ALU.is_equal))
                yield
                chain.settle()
                chain.add(nc.vector.tensor_tensor(t0, t0, row(order_s), ALU.mult))
                yield
                chain.settle()
                chain.add(nc.vector.tensor_reduce(x1, t0, AX.X, ALU.max))
                yield
                chain.settle()
                chain.add(nc.vector.tensor_tensor(sel1, t0, bc(x1), ALU.is_equal))
                yield
                chain.settle()
                chain.add(nc.vector.scalar_tensor_tensor(out=biased, in0=sel1, scalar=NEG_HUGE, in1=biased,
                                                    op0=ALU.mult, op1=ALU.add))
                yield
                chain.settle()
                chain.add(nc.vector.tensor_reduce(m2, biased, AX.X, ALU.max))
                yield
                chain.settle()
                chain.add(nc.vector.tensor_tensor(t1, biased, bc(m2), ALU.is_equal))
                yield
                chain.settle()
                chain.add(nc.vector.tensor_tensor(t1, t1, row(order_s), ALU.mult))
                yield
                chain.settle()
                chain.add(nc.vector.tensor_reduce(x2, t1, AX.X, ALU.max))
                yield
                chain.settle()
                chain.add(nc.vector.tensor_tensor(sel2, t1, bc(x2), ALU.is_equal))
                yield
                chain.settle()
                chain.add(nc.vector.tensor_tensor(sel1, sel1, sel2, ALU.add))
                yield
                dve.wait_ge(s_rexp, r + 1)
                chain.settle()
                chain.add(nc.vector.tensor_reduce(ssum, e, AX.X, ALU.add))
                yield
                chain.settle()
                chain.add(nc.vector.reciprocal(srec, ssum))
                yield
                chain.settle()
                chain.add(nc.vector.tensor_tensor(wts, e, bc(srec), ALU.mult))
                yield
                chain.settle()
                chain.add(nc.vector.tensor_tensor(wts, wts, sel1, ALU.mult))
                yield
                chain.settle()
                chain.add(nc.vector.tensor_reduce(vsum, wts, AX.X, ALU.add))
                yield
                chain.settle()
                chain.add(nc.vector.reciprocal(vrec, vsum))
                yield
                chain.settle()
                nc.vector.tensor_tensor(wts, wts, bc(vrec), ALU.mult).then_inc(s_ew, 1)
                yield

            def route(g, r, bank=MISC):
                for _ in route_steps(g, r, bank):
                    pass

            for r in range(N_ROUNDS):
                row_max(0, r)
            for u in range(UNITS):
                for kind, n in PLAN:
                    if kind == "S1" and u + 1 < UNITS:
                        row_max(u + 1, n)
                    if kind == "CTX":
                        ctx_norm(u, 0)
                    if kind == "CTX_PREV" and u % GROUPS:
                        ctx_norm(u - 1, 1)
                    early = EARLY.get(n) if kind == "S2" and u == UNITS - 1 else None
                    if early == "NORM":
                        norm_dve(dve, chain, QUADS)
                    if early == "ROUTER":
                        dve.wait_ge(s_w, W_ALL)
                        for _ in x_low_steps(QUADS, 0):
                            pass
                        route(QUADS, 0, 1)
                if u % GROUPS == GROUPS - 1:
                    ctx_norm(u, 1)
                if u == GROUPS - 1:
                    project(0)

            def low(k):
                dve.wait_ge(s_hi, k + 1)
                if k >= 3:
                    dve.wait_ge(s_down, k - 2)
                nc.vector.tensor_tensor(hid_lo[:, k % 3, :], hidden[:, k % 2, :], hid_hi[:, k % 3, :].bitcast(F32),
                                        ALU.subtract).then_inc(s_lo, 1)

            def b_v(c):
                dve.wait_ge(s_bconst, 1)
                for k in range(2):
                    dve.wait_ge(s_bv, 2 * c + k + 1)
                    if c >= 2:
                        dve.wait_ge(s_bo, QT * (c - 1))
                    for e in range(2):
                        lanes = slice(WIN * e, WIN * (e + 1))
                        src = ps[lanes, b_banks(c)[k], :].rearrange("p (w g e d) -> p w g e d", w=4, g=B_PAIRS, e=2)[:, :, :, e, :]
                        bias = b_bv[lanes, :].rearrange("p (g e d) -> p g e d", g=B_PAIRS, e=2)[:, :, e, :]
                        nc.vector.tensor_tensor(b_vbd[lanes, c % 2, 4 * k:4 * k + 4, :, e * B_VCOLS:e * B_VCOLS + B_DIM],
                                                src, bias.unsqueeze(1).to_broadcast([WIN, 4, B_PAIRS, B_DIM]),
                                                ALU.add).then_inc(s_bv_c, 1)

            def b_k_mask(c, heads):
                dve.wait_ge(s_bk1, c + 1)
                if c >= 2:
                    dve.wait_ge(s_bs, QT * (c - 1))
                else:
                    dve.wait_ge(s_hid, len(ITEMS) * (QUADS - 1 + c))
                for h in heads:
                    nc.vector.tensor_scalar(bk_s[c % 2][:, h, :], bk1_s, mask_s[:, h:h + 1], None, ALU.mult)\
                        .then_inc(s_bkd, 1)

            def expert_items(f, between):
                def take(i):
                    for steps, first, count in between:
                        if i >= first:
                            for _ in range(count):
                                if next(steps, "end") == "end":
                                    break

                for i, (n, half) in enumerate(ITEMS):
                    k = len(ITEMS) * f + i
                    dve.wait_ge(s_silu, k + 1)
                    dve.wait_ge(s_up, 2 * k + 2)
                    if k >= 2:
                        dve.wait_ge(s_hid, k - 1)
                    nc.vector.scalar_tensor_tensor(out=gated[:, k % 2, :], in0=ps[:, 2 * (k % 2) + 1, :],
                                                   scalar=bl1_s[:, n, 2 + half:3 + half], in1=silu_s[:, k % 2, :],
                                                   op0=ALU.add, op1=ALU.mult).then_inc(s_gate, 1)
                    take(i)
                    if i or f % QUADS:
                        low(k - 1)
                        take(i)
                    if i == Y_ADD_AT and f % QUADS:
                        y_add(f - 1)
                    if f == 0 and i in FINISH_AT[2:]:
                        project(1, (FINISH_AT.index(i) - 2,))
                    if f == QUADS - 1 and i - FIRST_K_AT - 1 in range(len(K_DVE)):
                        b_k_mask(0, [K_DVE[i - FIRST_K_AT - 1]])
                    if f == QUADS - 1 and i == FIRST_V_AT + 1:
                        b_v(0)
                for steps, _, _ in between:
                    for _ in steps:
                        pass

            def y_add(f):
                dve.wait_ge(s_y_t, f + 1)
                x4 = xs[:, (f % QUADS) * QT:(f % QUADS + 1) * QT, :]
                chain.settle()
                nc.vector.tensor_tensor(x4, ps[:, 6, :].rearrange("p (t d) -> p t d", t=QT), x4, ALU.add)\
                    .then_inc(s_added, 1)
                dve.wait_ge(s_added, f + 1 + (QUADS if f >= QUADS else 0))

            def moe(g0, r0):
                for c in range(QUADS):
                    between = []
                    if c + 1 < QUADS:
                        between = [(norm_steps(dve, chain, g0 + c + 1), 0, 2),
                                   (x_low_steps(g0 + c + 1, r0 + c + 1), X_LOW_AT, 1),
                                   (route_steps(g0 + c + 1, r0 + c + 1), ROUTE_AT, 2)]
                    elif g0 == QUADS:
                        between = [(norm_steps(dve, chain, 2 * QUADS), 0, 2),
                                   (norm_steps(dve, chain, 2 * QUADS + 1), SECOND_NORM_AT, 2)]
                    expert_items(r0 + c, between)
                low(len(ITEMS) * (r0 + QUADS) - 1)
                y_add(r0 + QUADS - 1)

            dve.wait_ge(s_late, 1)
            moe(QUADS, 0)

            def b_shift(p, take):
                dve.wait_ge(s_bs, p + 1)
                s = ps[:, 2 + p % 2, :].rearrange("p (h k) -> p h k", h=B_HEADS)
                if p >= 3:
                    dve.wait_ge(s_bpt, p - 2)
                chain.add(nc.vector.tensor_reduce(b_mx[:, p % 2], s, AX.X, ALU.max))
                max_at = chain.n
                take(2)
                dve.wait_ge(s_dve, max_at)
                nc.vector.tensor_tensor(b_p[:, p % 3], s, b_mx[:, p % 2].unsqueeze(2).to_broadcast([P, B_HEADS, WIN]),
                                        ALU.subtract).then_inc(s_bshift, 1)

            def b_norm(p, take):
                dve.wait_ge(s_bo, p + 1)
                if p:
                    dve.wait_ge(s_bo_n, p)
                o = ps[:, 6, 0:B_HEADS * B_VCOLS].rearrange("p (h w) -> p h w", h=B_HEADS)
                chain.add(nc.vector.reciprocal(b_rec, o[:, :, B_DIM]))
                rec_at = chain.n
                take(3)
                dve.wait_ge(s_dve, rec_at)
                if p >= 2:
                    dve.wait_ge(s_bot, p - 1)
                nc.vector.tensor_tensor(b_o[:, p % 2, :].rearrange("p (h d) -> p h d", h=B_HEADS), o[:, :, 0:B_DIM],
                                        b_rec.unsqueeze(2).to_broadcast([P, B_HEADS, B_DIM]), ALU.mult).then_inc(s_bo_n, 1)

            def b_add(c):
                dve.wait_ge(s_by, QT * (c + 1))
                x4 = xs[:, c * QT:(c + 1) * QT, :]
                chain.settle()
                chain.add(nc.vector.scalar_tensor_tensor(out=x4, in0=ps[:, 5, :].rearrange("p (t d) -> p t d", t=QT),
                                                         scalar=2.0, in1=x4, op0=ALU.mult, op1=ALU.add))
                chain.settle()
                nc.vector.tensor_tensor(x4, x4, b_bout.unsqueeze(1).to_broadcast([P, QT, DIM]), ALU.add)\
                    .then_inc(s_added, 1)
                dve.wait_ge(s_added, QUADS + c + 1)

            steps = iter(())

            def take(count):
                for _ in range(count):
                    next(steps, None)

            for kind, n in B_PLAN:
                if kind == "STEPS":
                    steps = norm_steps(dve, chain, n)
                if kind in ("NORM", "WEIGHTS"):
                    for _ in steps:
                        pass
                if kind == "ROUTER":
                    for _ in x_low_steps(3 * QUADS, QUADS):
                        pass
                    steps = route_steps(3 * QUADS, QUADS, 0)
                if kind == "V":
                    b_v(n)
                if kind == "K_MASK" and n % 2 == 0:
                    b_k_mask(n // 2, K_DVE)
                if kind == "S":
                    b_shift(n, take)
                    take(1)
                if kind == "W":
                    b_norm(n, take)
                    take(1)
                if kind == "ADD":
                    b_add(n)
            moe(3 * QUADS, QUADS)

        @block.tensor
        def _(pe):
            pe.wait_ge(s_const, 48)
            pe.wait_ge(s_wa, 80)
            pe.wait_ge(s_ctx_clear, 1)
            for b in range(BATCH):
                for g in (2 * b, 2 * b + 1):
                    if g:
                        pe.wait_ge(s_xt, xt_count(g - 1))
                    norm_pe(pe, g)
                pe.wait_ge(s_xt, xt_count(2 * b + 1))
                for k in range(2):
                    cols = xn_t[:, b, k * QCOLS:(k + 1) * QCOLS]
                    for s in range(2):
                        n = 4 * b + 2 * k + s
                        if n >= 2:
                            pe.wait_ge(s_rest, n - 1)
                        nc.tensor.matmul(ps[:, n % 2, :], wa[:, s, :], cols, start=True, stop=True).then_inc(s_qk_psum, 1)
                    c = 2 * b + k
                    if c >= 2:
                        pe.wait_ge(s_v, c - 1)
                    for t in range(QT):
                        ins = nc.tensor.matmul(ps[:, 2 + c % 2, t * P:(t + 1) * P], cols[:, t * P:(t + 1) * P],
                                               wa[:, 2, :], start=True, stop=True)
                    ins.then_inc(s_v_psum, 1)
            pe.wait_ge(s_v, QUADS)
            pe.wait_ge(s_ones, 1)

            def score_queries(u, r):
                i, h, kc, w = ROUNDS[r]
                b, hg = divmod(u, GROUPS)
                n = N_ROUNDS * u + r
                if r == 0:
                    if hg:
                        pe.wait_ge(s_rows[b][2], 16 * 9)
                    else:
                        pe.wait_ge(s_rows[b][0], 16 * 6)
                    pe.wait_ge(s_fixed, 16 * 2 * BATCH)
                if r == HALF_ROUNDS and hg == 0:
                    pe.wait_ge(s_rows[b][1], 16 * 6)
                if n >= RING:
                    pe.wait_ge(s_s1_read, n - RING + 1)
                diagonal = kc == i // QT
                ins = nc.tensor.matmul(ps[:, n % RING, 0:w],
                                       q_rows[b][0:MAX_ROWS_FROM, i // QT, hg * GROUP + h, i % QT * P:(i % QT + 1) * P],
                                       k_rows[b][0:MAX_ROWS_FROM, hg * GROUP + h, kc * QCOLS:kc * QCOLS + w],
                                       start=True, stop=not diagonal)
                if diagonal:
                    ins = nc.tensor.matmul(ps[:, n % RING, w - P:w], ident_b[:], causal_s[:], start=False, stop=True)
                ins.then_inc(s_s1, 1)

            def turn_max(u, half):
                n = 2 * u + half
                pe.wait_ge(s_maxp, n + 1)
                if half == 0 and u:
                    pe.wait_ge(s_ctx_n, 2 * (u - 1) + 1)
                if half and u:
                    pe.wait_ge(s_ctx_n, 2 * u)
                if n:
                    pe.wait_ge(s_maxc, n)
                nc.tensor.transpose(max_bank(ps), max_parts[:].rearrange("p a h t -> p (a h t)"), ident_b[:])\
                    .then_inc(s_maxt, 1)

            def score_keys(u, sh):
                s, h = divmod(sh, GROUP)
                c, j, q, w = STEPS[s]
                b, hg = divmod(u, GROUPS)
                if sh == 0:
                    pe.wait_ge(s_maxd, 16 * (2 * u + 1))
                if j == 0 and c == 1 and h == 0:
                    pe.wait_ge(s_maxd, 16 * (2 * u + 2))
                n = GROUP * N_STEPS * u + sh
                if n >= RING:
                    pe.wait_ge(s_probs, n - RING + 1)
                nc.tensor.matmul(ps[:, RING + n % RING, 0:w], k_rows[b][:, hg * GROUP + h, j * P:(j + 1) * P],
                                 q_rows[b][:, c, hg * GROUP + h, q - c * QCOLS:q - c * QCOLS + w],
                                 start=True, stop=True).then_inc(s_s2, 1)

            def weigh_values(u, s):
                c, j, q, w = STEPS[s]
                b, hg = divmod(u, GROUPS)
                pe.wait_ge(s_probs, GROUP * (N_STEPS * u + s + 1))
                if s in DIAG:
                    pe.wait_ge(s_masked, len(DIAG) * u + DIAG.index(s) + 1)
                if j == 0 and (u or c):
                    pe.wait_ge(s_ctx_copied, 2 * u + c)
                for h in range(GROUP):
                    ins = nc.tensor.matmul(ps[32 * h:32 * h + VCOLS, 6, q - c * QCOLS:q - c * QCOLS + w],
                                           v_s[:, b * TILES + j, hg * GROUP + h, :], probs[:, s % 2, h, 0:w],
                                           start=(j == 0), stop=(j == 4 * c + 3))
                ins.then_inc(s_pv, 1)

            def turn_ctx(u, half):
                n = 2 * u + half
                pe.wait_ge(s_ctx_copied, n + 1)
                if n:
                    pe.wait_ge(s_ctx_n, n)
                if half == 0:
                    pe.wait_ge(s_maxc, 2 * u + 2)
                else:
                    pe.wait_ge(s_maxc, min(2 * u + 3, 2 * UNITS))
                for t in range(QT):
                    ins = nc.tensor.transpose(ps[:, MISC, t * P:(t + 1) * P], ctx_s[:, t * P:(t + 1) * P], ident_s[:])
                ins.then_inc(s_ctx_t, 1)

            def turn_context(b, k, bank):
                for t in range(QT):
                    ins = nc.tensor.transpose(ps[:, bank, t * P:(t + 1) * P], ctx_tok[:, k * QT + t, :], ident_s[:])
                ins.then_inc(s_ctxf_t, 1)

            def project_context(b, k, bank):
                for t in range(QT):
                    col = ROLL + (k * QT + t) * P
                    ins = nc.tensor.matmul(ps[:, bank, t * P:(t + 1) * P], ctx_t[:, col:col + P], wa[:, 3, :],
                                           start=True, stop=True)
                ins.then_inc(s_proj, 1)

            def finish_batch_0():
                pe.wait_ge(s_ctx_n, 2 * GROUPS)
                pe.wait_ge(s_s1_read, N_ROUNDS * (GROUPS + 1))
                for k in range(2):
                    turn_context(0, k, k)
                pe.wait_ge(s_ctxf, 3)
                for k in range(2):
                    project_context(0, k, k + 1)
                pe.wait_ge(s_proj_read, 2)

            def finish_batch_1(step):
                k = step % 2
                if step == 0:
                    pe.wait_ge(s_ctx_n, 4 * GROUPS)
                if step < 2:
                    if step:
                        pe.wait_ge(s_ctxf, 3 + 2)
                    turn_context(1, k, 6)
                else:
                    if k == 0:
                        pe.wait_ge(s_ctxf, 3 + 3)
                    else:
                        pe.wait_ge(s_proj_read, 2 + 1)
                    project_context(1, k, 6)

            def router(g, r, bank=MISC):
                b, col = quad_cols(g % QUADS)
                pe.wait_ge(s_xt, xt_count(g))
                for t in range(QT):
                    ins = nc.tensor.matmul(ps[:, bank, t * EXPERTS:(t + 1) * EXPERTS],
                                           xn_t[:, b, col + t * P:col + (t + 1) * P], wr_s, start=True, stop=True)
                ins.then_inc(s_router, 1)

            def turn_weights(g, r, bank=6):
                pe.wait_ge(s_ew, r + 1)
                if r == 1:
                    pe.wait_ge(s_proj_read, 4)
                if r > QUADS or 2 <= r < QUADS:
                    pe.wait_ge(s_added, max(r - 1, QUADS) + QUADS if r >= QUADS else r - 1)
                for t in range(QT):
                    ins = nc.tensor.transpose(ps[0:EXPERTS, bank, t * P:(t + 1) * P], r_s[8][:, t, :], ident_s[:])
                ins.then_inc(s_ew_t, 1)

            for r in range(N_ROUNDS):
                score_queries(0, r)
                if r == HALF_ROUNDS + RING:
                    turn_max(0, 0)
            for u in range(UNITS):
                for kind, n in PLAN:
                    if kind == "S1" and u + 1 < UNITS:
                        score_queries(u + 1, n)
                    if kind == "S2":
                        score_keys(u, n)
                    if kind == "PV":
                        weigh_values(u, n)
                    if kind == "MAX":
                        turn_max(u, 1)
                    if kind == "MAX_TURN" and u + 1 < UNITS:
                        turn_max(u + 1, 0)
                    if kind == "CTX":
                        turn_ctx(u, 0)
                    if kind == "CTX_PREV" and u % GROUPS:
                        turn_ctx(u - 1, 1)
                    early = EARLY.get(n) if kind == "S2" and u == UNITS - 1 else None
                    if early == "TURN":
                        norm_pe(pe, QUADS, 0)
                    if early == "ROUTER":
                        pe.wait_ge(s_w, W_ALL)
                        router(QUADS, 0, 1)
                    if early == "WEIGHTS":
                        turn_weights(QUADS, 0, 1)
                if u % GROUPS == GROUPS - 1:
                    turn_ctx(u, 1)
                if u == GROUPS - 1:
                    finish_batch_0()

            def products(dst, w_hi, w_lo, v_hi, v_lo, start, stop):
                nc.tensor.matmul(dst, w_lo, v_hi, start=start, stop=False)
                nc.tensor.matmul(dst, w_hi, v_lo, start=False, stop=False)
                return nc.tensor.matmul(dst, w_hi, v_hi, start=False, stop=stop)

            def expert_items(f, pieces):
                pe.wait_ge(s_ew_c, f + 1)
                pe.wait_ge(s_xl, f + 1)

                def down(k):
                    i = k % len(ITEMS)
                    n, half = ITEMS[i]
                    pe.wait_ge(s_lo, k + 1)
                    products(ps[:, y_bank(k // len(ITEMS)), :], w2_hi[:, n, half, :], w2_lo[:, n, half, :], hid_hi[:, k % 3, :],
                             hid_lo[:, k % 3, :], False, i == len(ITEMS) - 1).then_inc(s_down, 1)

                for i, (n, half) in enumerate(ITEMS):
                    k = len(ITEMS) * f + i
                    if k >= 2:
                        pe.wait_ge(s_gate, k - 1)
                    for s in range(2):
                        h = s * HID + half * P
                        products(ps[:, 2 * (k % 2) + s, :], w1_hi[:, n, h:h + P], w1_lo[:, n, h:h + P],
                                 xh[:, f % 2, :], xl[:, f % 2, :], True, True).then_inc(s_up, 1)
                    if i == DOWN_LAG:
                        if f >= 2:
                            pe.wait_ge(s_y_c, f - 1)
                        if f == QUADS:
                            pe.wait_ge(s_added, 2 * QUADS)
                        nc.tensor.matmul(ps[:, y_bank(f), :], bl2_s[0:EXPERTS, :], ew_t[0:EXPERTS, f % 2, :], start=True, stop=False)
                    if i >= DOWN_LAG or f % QUADS:
                        down(k - DOWN_LAG)
                    if i == Y_TURN_AT and f % QUADS:
                        finish_y(f - 1)
                    if f == 0 and i in FINISH_AT:
                        finish_batch_1(FINISH_AT.index(i))
                    if i in pieces:
                        pieces[i]()
                if f % QUADS == QUADS - 1:
                    for k in range(len(ITEMS) * (f + 1) - DOWN_LAG, len(ITEMS) * (f + 1)):
                        down(k)
                    finish_y(f)

            def b_qk(c):
                b, col = quad_cols(c)
                pe.wait_ge(s_xt, xt_count(2 * QUADS + c))
                if c >= 2:
                    pe.wait_ge(s_bv_c, 4 * c)
                if c == 0:
                    pe.wait_ge(s_added, QUADS - 1)
                for s in range(2):
                    nc.tensor.matmul(ps[:, b_banks(c)[s], :], b_win[:, s * DIM:(s + 1) * DIM],
                                     xn_t[:, b, col:col + QCOLS], start=True, stop=True).then_inc(s_bqk, 1)

            def b_v(c):
                b, col = quad_cols(c)
                for k in range(2):
                    if k == 0:
                        pe.wait_ge(s_bq_c, c + 1)
                    else:
                        pe.wait_ge(s_bk1, c + 1)
                        pe.wait_ge(s_bk_c, len(K_ACT) * (c + 1))
                    for w in range(4):
                        at_col = col + (4 * k + w) * WIN
                        for e in range(2):
                            ins = nc.tensor.matmul(ps[WIN * e:WIN * (e + 1), b_banks(c)[k], w * P:(w + 1) * P],
                                                   xn_t[:, b, at_col:at_col + WIN], b_win[:, 2 * DIM:3 * DIM],
                                                   start=True, stop=True)
                    ins.then_inc(s_bv, 1)

            def finish_y(f):
                pe.wait_ge(s_y_c, f + 1)
                if f == QUADS - 1:
                    pe.wait_ge(s_bv_c, 4)
                if f % QUADS < QUADS - 1:
                    pe.wait_ge(s_ew_c, f + 2)
                for t in range(QT):
                    ins = nc.tensor.transpose(ps[:, 6, t * P:(t + 1) * P], y_s[:, t * P:(t + 1) * P], ident_s[:])
                ins.then_inc(s_y_t, 1)

            def moe(g0, r0):
                for c in range(QUADS):
                    pieces = {}
                    if c + 1 < QUADS:
                        pieces = {TURN_AT: lambda c=c: norm_pe_after(pe, g0 + c + 1, r0 + c),
                                  ROUTE_AT - 1: lambda c=c: router(g0 + c + 1, r0 + c + 1),
                                  WEIGHTS_AT: lambda c=c: turn_weights(g0 + c + 1, r0 + c + 1)}
                    elif g0 == QUADS:
                        pieces = {TURN_AT: lambda c=c: norm_pe_after(pe, g0 + c + 1, r0 + c),
                                  FIRST_QK_AT: lambda: b_qk(0), FIRST_V_AT: lambda: b_v(0)}
                    expert_items(r0 + c, pieces)

            def norm_pe_after(pe, g, r):
                pe.wait_ge(s_ew_c, r + 1)
                norm_pe(pe, g)

            pe.wait_ge(s_late, 1)
            moe(QUADS, 0)

            def scores(p):
                c, t = divmod(p, QT)
                if t == 0:
                    pe.wait_ge(s_bq_c, c + 1)
                    pe.wait_ge(s_bk_c, len(K_ACT) * (c + 1))
                    pe.wait_ge(s_bkd, len(K_DVE) * (c + 1))
                if p >= 2:
                    pe.wait_ge(s_bshift, p - 1)
                for e in range(2):
                    w = 2 * t + e
                    ins = nc.tensor.matmul(ps[WIN * e:WIN * (e + 1), 2 + p % 2, :],
                                           bq_s[:, c % 2, w * WIN:(w + 1) * WIN],
                                           bk_s[c % 2][:, :, w * WIN:(w + 1) * WIN], start=True, stop=True)
                ins.then_inc(s_bs, 1)

            def turn_probs(p):
                pe.wait_ge(s_bexp, p + 1)
                if p:
                    pe.wait_ge(s_bpt_c, p)
                for g2 in range(B_PAIRS):
                    ins = nc.tensor.transpose(ps[:, 4, g2 * P:(g2 + 1) * P],
                                              b_p[:, p % 3, 2 * g2:2 * g2 + 2, :].rearrange("p h k -> p (h k)"), ident_s[:])
                ins.then_inc(s_bpt, 1)

            def weigh(p):
                c, t = divmod(p, QT)
                pe.wait_ge(s_bpt_c, p + 1)
                pe.wait_ge(s_bv_c, 4 * c + 4)
                if p:
                    pe.wait_ge(s_bo_n, p)
                for g2 in range(B_PAIRS):
                    for e in range(2):
                        ins = nc.tensor.matmul(ps[WIN * e:WIN * (e + 1), 6, g2 * 2 * B_VCOLS:(g2 + 1) * 2 * B_VCOLS],
                                               b_pt[:, p % 2, g2, WIN * e:WIN * (e + 1)], b_vbd[:, c % 2, 2 * t + e, g2, :],
                                               start=True, stop=True)
                ins.then_inc(s_bo, 1)

            def turn_out(p, free):
                pe.wait_ge(s_bo_n, p + 1)
                if p:
                    pe.wait_ge(s_bot_c, p)
                pe.wait_ge(s_xt, free)
                nc.tensor.transpose(ps[:, MISC, 0:P], b_o[:, p % 2, :], ident_s[:]).then_inc(s_bot, 1)

            def out_proj(p):
                c, t = divmod(p, QT)
                pe.wait_ge(s_bot_c, p + 1)
                if t == 0:
                    pe.wait_ge(s_added, QUADS + c)
                nc.tensor.matmul(ps[:, 5, t * DIM:(t + 1) * DIM], b_ot[:, p % 2, :], b_wout,
                                 start=True, stop=True).then_inc(s_by, 1)

            turned, free = 0, xt_count(2 * QUADS)
            for kind, n in B_PLAN:
                if kind == "NORM":
                    if n < 3 * QUADS and turned:
                        pe.wait_ge(s_bot_c, turned)
                    if n == 3 * QUADS:
                        pe.wait_ge(s_bv_c, 4 * QUADS)
                    norm_pe(pe, n, norm_bank(n))
                    free = xt_count(n)
                if kind == "QK":
                    b_qk(n)
                if kind == "V":
                    b_v(n)
                if kind == "S":
                    scores(n)
                if kind == "T":
                    turn_probs(n)
                if kind == "W":
                    weigh(n)
                if kind == "O":
                    turn_out(n, free)
                    turned = n + 1
                if kind == "Y":
                    out_proj(n)
                if kind == "ROUTER":
                    router(3 * QUADS, QUADS, 0)
                if kind == "WEIGHTS":
                    turn_weights(3 * QUADS, QUADS, 1)
            moe(3 * QUADS, QUADS)


def max_bank(ps):
    return ps[0:PARTS * GROUP * QT, 7, 0:P // 2].bitcast(BF16)


def constants():
    import numpy as np

    def bf(a):
        bits = np.ascontiguousarray(a, np.float32).view(np.uint32)
        return ((bits + 0x7FFF + ((bits >> 16) & 1)) >> 16).astype(np.uint16)

    def split(a):
        parts = []
        for _ in range(PARTS):
            parts.append(bf(a))
            a = a - (parts[-1].astype(np.uint32) << 16).view(np.float32)
        return np.stack(parts)

    slopes = (np.float32(2.0) ** (np.float32(-8.0) * np.arange(1, A_HEADS + 1, dtype=np.float32) / A_HEADS)).astype(np.float32)
    slope_pos = slopes[:, None] * np.arange(TOKENS, dtype=np.float32)[None, :]
    key_rows = np.concatenate([split(slope_pos), bf(np.ones((PARTS, A_HEADS, TOKENS)))])
    causal = bf(np.where(np.arange(P)[None, :] > np.arange(P)[:, None], NEG_BIG, 0.0))
    mask = np.zeros((P, B_HEADS), np.float32)
    for h in range(B_HEADS):
        mask[h * B_DIM:(h + 1) * B_DIM, h] = 1
    return {
        "ident": np.eye(P, dtype=np.float32), "ident_bf": bf(np.eye(P)), "causal": causal,
        "key_rows": key_rows, "head_mask": mask,
        "order": np.tile(np.arange(EXPERTS, 0, -1, dtype=np.float32), (P, 1)),
    }


def kernel(**inputs):
    import numpy as np
    import concourse.bacc as bacc
    from concourse.bass_utils import run_bass_kernel_spmd

    a = {k: np.asarray(v) for k, v in inputs.items()}
    bl1 = a["L0_ffn_bl1"]
    arrays = {
        "x": a["L0_attn_a_x"], "w_q": a["L0_attn_a_W_query"], "w_k": a["L0_attn_a_W_key"],
        "w_v": a["L0_attn_a_W_value"], "w_proj": a["L0_attn_a_W_proj"], "b_proj": a["L0_attn_a_b_proj"],
        "b_in_wt": a["L0_attn_b_in_proj_w"].T, "b_in_b": a["L0_attn_b_in_proj_b"],
        "b_in_b_t": a["L0_attn_b_in_proj_b"].reshape(3, P).T,
        "b_out_wt": a["L0_attn_b_out_w"].T, "b_out_b": a["L0_attn_b_out_b"],
        "wr_t": a["L0_ffn_Wr"].T, "br": a["L0_ffn_br"], "wl1": a["L0_ffn_Wl1"],
        "bl1_t": bl1.reshape(EXPERTS, 4, P).transpose(2, 0, 1), "wl2": a["L0_ffn_Wl2"], "bl2": a["L0_ffn_bl2"],
        "biases": a["L0_ffn_biases_N"], **constants(),
    }
    nc = bacc.Bacc("TRN2", target_bir_lowering=False, num_devices=1)
    feed, args = {}, {}
    for name, v in arrays.items():
        v = np.ascontiguousarray(v)
        feed[f"in_{name}"] = v
        ap = nc.dram_tensor(f"in_{name}", v.shape, mybir.dt.from_np(v.dtype), kind="ExternalInput").ap()
        args[name] = ap.bitcast(BF16) if v.dtype == np.uint16 else ap
    out = nc.dram_tensor("out_x", (BATCH, TOKENS, DIM), F32, kind="ExternalOutput").ap()
    build(nc, **args, out=out)
    r = run_bass_kernel_spmd(nc, [feed], core_ids=[0])
    return r.results[0]["out_x"]
```
